# Optimizing a Trainium2 kernel written in Bass

```python
import numpy as np
import jax
import jax.numpy as jnp

def _softmax(x, axis=-1):
    return jax.nn.softmax(x, axis=axis)

def _gelu(x):
    return jax.nn.gelu(x, approximate=True)

def _silu(x):
    return jax.nn.silu(x)

def _sigmoid(x):
    return jax.nn.sigmoid(x)

def _layernorm(x, axis=-1, eps=1e-05):
    m = jnp.mean(x, axis=axis, keepdims=True)
    v = jnp.var(x, axis=axis, keepdims=True)
    return (x - m) / jnp.sqrt(v + eps)

def _scatter_add(tgt, idx, src, axis=0):
    return tgt.at[idx].add(src)

def _segment_sum(src, seg, n):
    return jax.ops.segment_sum(src, seg, n)
kernel_name = 'mk_decoder_postln_d1_seqx_r8_329ef3'

def setup_inputs(seed: int=0):
    np.random.seed(seed)
    _w = jnp.asarray

    def _rec_inputs():
        import jax
        import jax.numpy as jnp
        _rk = jax.random.key(seed)
        x = 4.136e-05 + 0.9999 * jax.random.normal(jax.random.fold_in(_rk, 1), (4, 256, 256), jnp.float32)
        _lenS = 256 - jax.random.randint(jax.random.fold_in(_rk, 7), (4,), 0, max(1, 256 // 4) + 1, jnp.int32)
        _lenS2 = 256 - jax.random.randint(jax.random.fold_in(_rk, 8), (4,), 0, max(1, 256 // 4) + 1, jnp.int32)
        _ctx_1024P = jax.random.normal(jax.random.fold_in(_rk, 11), (4, 16, 128), jnp.float32)
        _ctx_1024c = jax.random.dirichlet(jax.random.fold_in(_rk, 511), 0.3 * jnp.ones((16,), jnp.float32), (4, 256))
        _ctx_1024t = jnp.einsum('bsk,bkd->bsd', _ctx_1024c, _ctx_1024P)
        _ctx_1024t = _ctx_1024t * jax.lax.rsqrt(jnp.mean(jnp.square(_ctx_1024t)) + 1e-12) * 0.953939
        ctx_1024 = -0.000292821 + 1.00034 * (_ctx_1024t + 0.3 * jax.random.normal(jax.random.fold_in(_rk, 611), (4, 256, 128), jnp.float32))
        return (x, ctx_1024)
    x, ctx_1024 = _rec_inputs()

    def _L0_attn_setup():
        import jax, jax.numpy as jnp
        import numpy as np
        import math
        NUM_HEADS = 16
        SPARSITY_THRESHOLD = 0.2
        MIN_TOKENS = 32

        def _forward(x, Wq, bq, Wk, bk, Wv, bv, Wo, bo, Wi, bi):
            B, S, H = x.shape
            nh = NUM_HEADS
            hd = H // nh
            importance = (x @ Wi + bi)[..., 0]
            sorted_desc = jnp.sort(importance, axis=-1)[:, ::-1]
            tidx = min(max(1, int(S * SPARSITY_THRESHOLD)), S - 1)
            threshold = sorted_desc[:, tidx][:, None]
            sparse_mask = (importance > threshold).astype(x.dtype)
            if MIN_TOKENS > 0 and S > MIN_TOKENS:
                _, top_idx = jax.lax.top_k(importance, min(MIN_TOKENS, S))
                rows = jnp.arange(B)[:, None]
                min_mask = jnp.zeros_like(importance).at[rows, top_idx].set(1.0)
                sparse_mask = jnp.maximum(sparse_mask, min_mask)
            mask = sparse_mask[:, :, None, None]
            q = (x @ Wq + bq).reshape(B, S, nh, hd)
            k = (x @ Wk + bk).reshape(B, S, nh, hd) * mask
            v = (x @ Wv + bv).reshape(B, S, nh, hd) * mask
            scale = 1.0 / math.sqrt(hd)
            scores = jnp.einsum('bqhd,bkhd->bhqk', q, k) * scale
            attn = jax.nn.softmax(scores, axis=-1)
            out = jnp.einsum('bhqk,bkhd->bqhd', attn, v).reshape(B, S, H)
            return out @ Wo + bo
        key = jax.random.key(seed)
        ks = jax.random.split(key, 11)
        B, S, H = (4, 256, 256)
        s = 0.02
        return {'x': jax.random.normal(ks[0], (B, S, H), jnp.float32), 'Wq': jax.random.normal(ks[1], (H, H), jnp.float32) * s, 'bq': jax.random.normal(ks[2], (H,), jnp.float32) * s, 'Wk': jax.random.normal(ks[3], (H, H), jnp.float32) * s, 'bk': jax.random.normal(ks[4], (H,), jnp.float32) * s, 'Wv': jax.random.normal(ks[5], (H, H), jnp.float32) * s, 'bv': jax.random.normal(ks[6], (H,), jnp.float32) * s, 'Wo': jax.random.normal(ks[7], (H, H), jnp.float32) * s, 'bo': jax.random.normal(ks[8], (H,), jnp.float32) * s, 'Wi': jax.random.normal(ks[9], (H, 1), jnp.float32) * s, 'bi': jax.random.normal(ks[10], (1,), jnp.float32) * s}
    _L0_attn_all = _L0_attn_setup()
    _L0_attn_in = {k: v for k, v in _L0_attn_all.items() if k in ('Wq', 'bq', 'Wk', 'bk', 'Wv', 'bv', 'Wo', 'bo', 'Wi', 'bi')}
    del _L0_attn_all

    def _L0_xattn_setup():
        import jax, jax.numpy as jnp
        import numpy as np
        import math
        B, L, DM = (2, 256, 128)
        DS, DC, EXP = (16, 4, 2)
        DI = EXP * DM
        DR = math.ceil(DM / 16)
        DT_MIN, DT_MAX, DT_FLOOR = (0.001, 0.1, 0.0001)

        def _ssm_forward(hidden_states, z, in_proj_w, conv_w, conv_b, x_proj_w, dt_proj_w, dt_proj_b, A_log, D):
            b = hidden_states.shape[0]
            x = jnp.einsum('ed,bld->bel', in_proj_w, hidden_states)
            xp = jnp.pad(x, ((0, 0), (0, 0), (DC - 1, 0)))
            xc = jax.lax.conv_general_dilated(xp, conv_w[:, None, :], window_strides=(1,), padding='VALID', dimension_numbers=('NCH', 'OIH', 'NCH'), feature_group_count=DI)
            u = jax.nn.silu(xc + conv_b[None, :, None])
            x_dbl = jnp.einsum('ke,bel->bkl', x_proj_w, u)
            dt_lo = x_dbl[:, :DR]
            Bm = x_dbl[:, DR:DR + DS]
            Cm = x_dbl[:, DR + DS:]
            delta = jax.nn.softplus(jnp.einsum('er,brl->bel', dt_proj_w, dt_lo) + dt_proj_b[None, :, None])
            A = -jnp.exp(A_log)

            def step(state, xs):
                d_t, B_t, C_t, u_t = xs
                dA = jnp.exp(d_t[..., None] * A)
                state = state * dA + (d_t * u_t)[..., None] * B_t[:, None, :]
                y_t = jnp.einsum('ben,bn->be', state, C_t)
                return (state, y_t)
            xs = (jnp.moveaxis(delta, -1, 0), jnp.moveaxis(Bm, -1, 0), jnp.moveaxis(Cm, -1, 0), jnp.moveaxis(u, -1, 0))
            state0 = jnp.zeros((b, DI, DS), delta.dtype)
            _, ys = jax.lax.scan(step, state0, xs)
            y = jnp.moveaxis(ys, 0, -1)
            y = y + D[None, :, None] * u
            y = y * jax.nn.silu(z)
            return jnp.swapaxes(y, 1, 2)
        key = jax.random.key(seed)
        ks = jax.random.split(key, 8)
        hidden_states = jax.random.normal(ks[0], (B, L, DM), jnp.float32)
        z = jax.random.normal(ks[1], (B, DI, L), jnp.float32)
        in_proj_w = jax.random.normal(ks[2], (DI, DM), jnp.float32) * DM ** (-0.5)
        conv_w = jax.random.normal(ks[3], (DI, DC), jnp.float32) * DC ** (-0.5)
        conv_b = jnp.zeros((DI,), jnp.float32)
        x_proj_w = jax.random.normal(ks[4], (DR + 2 * DS, DI), jnp.float32) * DI ** (-0.5)
        dt_std = DR ** (-0.5)
        dt_proj_w = jax.random.uniform(ks[5], (DI, DR), jnp.float32, -dt_std, dt_std)
        dt = jnp.exp(jax.random.uniform(ks[6], (DI,), jnp.float32) * (math.log(DT_MAX) - math.log(DT_MIN)) + math.log(DT_MIN))
        dt = jnp.clip(dt, DT_FLOOR)
        dt_proj_b = dt + jnp.log(-jnp.expm1(-dt))
        A_log = jnp.log(jnp.broadcast_to(jnp.arange(1, DS + 1, dtype=jnp.float32), (DI, DS)))
        D = jnp.ones((DI,), jnp.float32)
        return dict(hidden_states=hidden_states, z=z, in_proj_w=in_proj_w, conv_w=conv_w, conv_b=conv_b, x_proj_w=x_proj_w, dt_proj_w=dt_proj_w, dt_proj_b=dt_proj_b, A_log=A_log, D=D)
    _L0_xattn_all = _L0_xattn_setup()
    _L0_xattn_in = {k: v for k, v in _L0_xattn_all.items() if k in ('in_proj_w', 'conv_w', 'conv_b', 'x_proj_w', 'dt_proj_w', 'dt_proj_b', 'A_log', 'D')}
    del _L0_xattn_all

    def _L0_ffn_setup():
        import jax, jax.numpy as jnp
        import numpy as np
        B, S, H, E, D, K = (2, 256, 256, 8, 256, 2)
        key = jax.random.key(seed)
        ks = jax.random.split(key, 4)
        return {'x': jax.random.normal(ks[0], (B, S, H), jnp.float32), 'router_w': jax.random.normal(ks[1], (H, E), jnp.float32) / np.sqrt(H).astype(np.float32), 'router_b': jnp.zeros((E,), jnp.float32), 'expert_w': jax.random.normal(ks[2], (E, H, D), jnp.float32) / np.sqrt(H).astype(np.float32), 'expert_b': jnp.zeros((E, D), jnp.float32), 'out_w': jax.random.normal(ks[3], (D, D), jnp.float32) / np.sqrt(D).astype(np.float32), 'out_b': jnp.zeros((D,), jnp.float32)}
    _L0_ffn_all = _L0_ffn_setup()
    _L0_ffn_in = {k: v for k, v in _L0_ffn_all.items() if k in ('router_w', 'router_b', 'expert_w', 'expert_b', 'out_w', 'out_b')}
    del _L0_ffn_all
    return {'x': x, 'ctx_1024': ctx_1024, 'L0_attn_Wq': _L0_attn_in['Wq'], 'L0_attn_bq': _L0_attn_in['bq'], 'L0_attn_Wk': _L0_attn_in['Wk'], 'L0_attn_bk': _L0_attn_in['bk'], 'L0_attn_Wv': _L0_attn_in['Wv'], 'L0_attn_bv': _L0_attn_in['bv'], 'L0_attn_Wo': _L0_attn_in['Wo'], 'L0_attn_bo': _L0_attn_in['bo'], 'L0_attn_Wi': _L0_attn_in['Wi'], 'L0_attn_bi': _L0_attn_in['bi'], 'L0_xattn_in_proj_w': _L0_xattn_in['in_proj_w'], 'L0_xattn_conv_w': _L0_xattn_in['conv_w'], 'L0_xattn_conv_b': _L0_xattn_in['conv_b'], 'L0_xattn_x_proj_w': _L0_xattn_in['x_proj_w'], 'L0_xattn_dt_proj_w': _L0_xattn_in['dt_proj_w'], 'L0_xattn_dt_proj_b': _L0_xattn_in['dt_proj_b'], 'L0_xattn_A_log': _L0_xattn_in['A_log'], 'L0_xattn_D': _L0_xattn_in['D'], 'L0_ffn_router_w': _L0_ffn_in['router_w'], 'L0_ffn_router_b': _L0_ffn_in['router_b'], 'L0_ffn_expert_w': _L0_ffn_in['expert_w'], 'L0_ffn_expert_b': _L0_ffn_in['expert_b'], 'L0_ffn_out_w': _L0_ffn_in['out_w'], 'L0_ffn_out_b': _L0_ffn_in['out_b']}

def reference(x, ctx_1024, L0_attn_Wq, L0_attn_bq, L0_attn_Wk, L0_attn_bk, L0_attn_Wv, L0_attn_bv, L0_attn_Wo, L0_attn_bo, L0_attn_Wi, L0_attn_bi, L0_xattn_in_proj_w, L0_xattn_conv_w, L0_xattn_conv_b, L0_xattn_x_proj_w, L0_xattn_dt_proj_w, L0_xattn_dt_proj_b, L0_xattn_A_log, L0_xattn_D, L0_ffn_router_w, L0_ffn_router_b, L0_ffn_expert_w, L0_ffn_expert_b, L0_ffn_out_w, L0_ffn_out_b):
    import jax
    import jax.numpy as jnp

    def _L0_attn_ref(x, Wq, bq, Wk, bk, Wv, bv, Wo, bo, Wi, bi):
        import jax, jax.numpy as jnp
        import numpy as np
        import math
        NUM_HEADS = 16
        SPARSITY_THRESHOLD = 0.2
        MIN_TOKENS = 32

        def _forward(x, Wq, bq, Wk, bk, Wv, bv, Wo, bo, Wi, bi):
            B, S, H = x.shape
            nh = NUM_HEADS
            hd = H // nh
            importance = (x @ Wi + bi)[..., 0]
            sorted_desc = jnp.sort(importance, axis=-1)[:, ::-1]
            tidx = min(max(1, int(S * SPARSITY_THRESHOLD)), S - 1)
            threshold = sorted_desc[:, tidx][:, None]
            sparse_mask = (importance > threshold).astype(x.dtype)
            if MIN_TOKENS > 0 and S > MIN_TOKENS:
                _, top_idx = jax.lax.top_k(importance, min(MIN_TOKENS, S))
                rows = jnp.arange(B)[:, None]
                min_mask = jnp.zeros_like(importance).at[rows, top_idx].set(1.0)
                sparse_mask = jnp.maximum(sparse_mask, min_mask)
            mask = sparse_mask[:, :, None, None]
            q = (x @ Wq + bq).reshape(B, S, nh, hd)
            k = (x @ Wk + bk).reshape(B, S, nh, hd) * mask
            v = (x @ Wv + bv).reshape(B, S, nh, hd) * mask
            scale = 1.0 / math.sqrt(hd)
            scores = jnp.einsum('bqhd,bkhd->bhqk', q, k) * scale
            attn = jax.nn.softmax(scores, axis=-1)
            out = jnp.einsum('bhqk,bkhd->bqhd', attn, v).reshape(B, S, H)
            return out @ Wo + bo
        return _forward(x, Wq, bq, Wk, bk, Wv, bv, Wo, bo, Wi, bi)

    def _L0_xattn_ref(hidden_states, z, in_proj_w, conv_w, conv_b, x_proj_w, dt_proj_w, dt_proj_b, A_log, D):
        import jax, jax.numpy as jnp
        import numpy as np
        import math
        B, L, DM = (2, 256, 128)
        DS, DC, EXP = (16, 4, 2)
        DI = EXP * DM
        DR = math.ceil(DM / 16)
        DT_MIN, DT_MAX, DT_FLOOR = (0.001, 0.1, 0.0001)

        def _ssm_forward(hidden_states, z, in_proj_w, conv_w, conv_b, x_proj_w, dt_proj_w, dt_proj_b, A_log, D):
            b = hidden_states.shape[0]
            x = jnp.einsum('ed,bld->bel', in_proj_w, hidden_states)
            xp = jnp.pad(x, ((0, 0), (0, 0), (DC - 1, 0)))
            xc = jax.lax.conv_general_dilated(xp, conv_w[:, None, :], window_strides=(1,), padding='VALID', dimension_numbers=('NCH', 'OIH', 'NCH'), feature_group_count=DI)
            u = jax.nn.silu(xc + conv_b[None, :, None])
            x_dbl = jnp.einsum('ke,bel->bkl', x_proj_w, u)
            dt_lo = x_dbl[:, :DR]
            Bm = x_dbl[:, DR:DR + DS]
            Cm = x_dbl[:, DR + DS:]
            delta = jax.nn.softplus(jnp.einsum('er,brl->bel', dt_proj_w, dt_lo) + dt_proj_b[None, :, None])
            A = -jnp.exp(A_log)

            def step(state, xs):
                d_t, B_t, C_t, u_t = xs
                dA = jnp.exp(d_t[..., None] * A)
                state = state * dA + (d_t * u_t)[..., None] * B_t[:, None, :]
                y_t = jnp.einsum('ben,bn->be', state, C_t)
                return (state, y_t)
            xs = (jnp.moveaxis(delta, -1, 0), jnp.moveaxis(Bm, -1, 0), jnp.moveaxis(Cm, -1, 0), jnp.moveaxis(u, -1, 0))
            state0 = jnp.zeros((b, DI, DS), delta.dtype)
            _, ys = jax.lax.scan(step, state0, xs)
            y = jnp.moveaxis(ys, 0, -1)
            y = y + D[None, :, None] * u
            y = y * jax.nn.silu(z)
            return jnp.swapaxes(y, 1, 2)
        return _ssm_forward(hidden_states, z, in_proj_w, conv_w, conv_b, x_proj_w, dt_proj_w, dt_proj_b, A_log, D)

    def _L0_ffn_ref(x, router_w, router_b, expert_w, expert_b, out_w, out_b):
        import jax, jax.numpy as jnp
        import numpy as np
        B, S, H, E, D, K = (2, 256, 256, 8, 256, 2)
        num_experts = expert_w.shape[0]
        router_logits = jnp.einsum('bsh,he->bse', x, router_w) + router_b
        router_probs = jax.nn.softmax(router_logits, axis=-1)
        top_k_probs, top_k_indices = jax.lax.top_k(router_probs, K)
        top_k_probs = top_k_probs / jnp.sum(top_k_probs, axis=-1, keepdims=True)
        onehot = jax.nn.one_hot(top_k_indices, num_experts, dtype=x.dtype)
        gates = jnp.einsum('bsk,bske->bse', top_k_probs, onehot)
        expert_out = jax.nn.gelu(jnp.einsum('bsh,ehd->ebsd', x, expert_w) + expert_b[:, None, None, :])
        combined = jnp.einsum('bse,ebsd->bsd', gates, expert_out)
        return jnp.einsum('bsd,df->bsf', combined, out_w) + out_b
    x = _layernorm(x + _L0_attn_ref(x, L0_attn_Wq, L0_attn_bq, L0_attn_Wk, L0_attn_bk, L0_attn_Wv, L0_attn_bv, L0_attn_Wo, L0_attn_bo, L0_attn_Wi, L0_attn_bi), axis=-1)
    x = _layernorm(x + _L0_xattn_ref(ctx_1024, x, L0_xattn_in_proj_w, L0_xattn_conv_w, L0_xattn_conv_b, L0_xattn_x_proj_w, L0_xattn_dt_proj_w, L0_xattn_dt_proj_b, L0_xattn_A_log, L0_xattn_D), axis=-1)
    x = _layernorm(x + _L0_ffn_ref(x, L0_ffn_router_w, L0_ffn_router_b, L0_ffn_expert_w, L0_ffn_expert_b, L0_ffn_out_w, L0_ffn_out_b), axis=-1)
    return x

_drawn_inputs = setup_inputs


def setup_inputs(seed=0):
    import zlib

    import numpy as np

    out = dict(_drawn_inputs(seed))
    spreads = {'L0_xattn_conv_b': (0.0, 0.1),
     'L0_xattn_D': (1.0, 0.2),
     'L0_ffn_router_b': (0.0, 0.1),
     'L0_ffn_expert_b': (0.0, 0.1),
     'L0_ffn_out_b': (0.0, 0.1)}
    factors = {'L0_attn_Wq': 8.0,
     'L0_attn_bq': 8.0,
     'L0_attn_Wk': 8.0,
     'L0_attn_bk': 38.893,
     'L0_attn_Wv': 3.101,
     'L0_attn_bv': 6.097,
     'L0_attn_Wo': 2.918,
     'L0_attn_Wi': 3.481,
     'L0_xattn_dt_proj_w': 2.916}
    for name, (base, spread) in spreads.items():
        noise = np.random.default_rng([zlib.crc32(name.encode()), seed]).standard_normal(out[name].shape)
        drawn = base * np.exp(spread * noise) if base else spread * noise
        out[name] = jnp.asarray(drawn.astype(out[name].dtype))
    for name, factor in factors.items():
        out[name] = (out[name] * factor).astype(out[name].dtype)
    return out
```

```python
from contextlib import ExitStack

import numpy as np

import concourse.bass as bass
from concourse import mybir

F32 = mybir.dt.float32
F32R = mybir.dt.float32r
BF16 = mybir.dt.bfloat16
ALU = mybir.AluOpType
ACT = mybir.ActivationFunctionType
AX = mybir.AxisListType

P = 128
B, S, H = 4, 256, 256
DC = 128
TOK = B * S
NT = TOK // P
HC = H // P
NH, HD = 16, 16
HPC = P // HD
TIDX = max(1, int(S * 0.2))
MINTOK = 32
SLOTS = 52
PAIRS = NH // 2
SC = 2 * SLOTS
NS, TAPS, DR = 16, 4, 8
E = 8
HALF = TOK // 2
HT = NT // 2
NPAIR = NS // 2
ITER = 2 * NPAIR
EPS = 1e-5
BIAS = 64

A_INP, A_CW, A_CB, A_XP, A_DTB, A_AL, A_D, A_END = np.cumsum([0, H, 2 * TAPS, 2, 2 * P, 2, 2 * NS, 2]).tolist()
C_ID, C_WI, C_BQ, C_BI, C_M8, C_IOTA, C_TRI, C_VM, C_VD, C_TR8, C_ON2, C_END = np.cumsum(
    [0, P, 2 * P, 2, 1, HPC, SLOTS, 2 * S, 2, 2, E * E, P]).tolist()


def decoder_layer(nc, ctxT, pkA, dtpT, pkC, xT, x, wq, wk, wv, wo, rows, headones, sel, bo, ob, ew, rw, ow, eb, rb, out):
    with ExitStack() as ctx:
        def sb(name, shape, dt=F32):
            return ctx.enter_context(nc.sbuf_tensor(name, shape, dt))

        def psum(name, shape):
            return ctx.enter_context(nc.psum_tensor(name, shape, F32))

        def sem(name):
            return ctx.enter_context(nc.semaphore(name))

        psS = psum("psS", [P, 4, 512])
        psB = psum("psB", [P, 512])
        psA = psum("psA", [P, 3, 512])

        s_ctxT = sb("s_ctxT", [P, TOK])
        imp = s_ctxT
        a = sb("s_pkA", [P, A_END])
        c = sb("s_pkC", [P, C_END])
        s_xT = sb("s_xT", [P, HC, TOK])
        ew_in = [s_xT[:, q, :] for q in range(2)]
        s_eb = s_xT[BIAS:P, :, :].rearrange("p m t -> p (m t)")
        ge = s_xT[:, :, :].rearrange("p m (h t) -> p (m h) t", h=2)
        s_x = sb("s_x", [P, NT, H])
        xb, zt, x2b = s_x, s_x, s_x
        s_wq = sb("s_wq", [P, HC, H])
        s_ow = s_wq
        s_wk = sb("s_wk", [P, HC, H])
        s_wv = sb("s_wv", [P, HC, H])
        s_wo = sb("s_wo", [P, HC, H])
        cmb, y3 = s_wk, s_wv
        ho_eb = sb("ho_eb", [P, E * H], F32R)
        ho_r = ho_eb[0:NH, 0:NH * SLOTS].rearrange("p (m s) -> p m s", m=HC)
        eb_st = ho_eb[BIAS:P, :]
        s_sel = sb("s_sel", [P, 2 * NS, P], BF16)
        s_bo = sb("s_bo", [P, H])
        s_ob = sb("s_ob", [P, H])
        ew_hi = sb("ew_hi", [P, HC, E * H], F32R)
        ew_lo = sb("ew_lo", [P, HC, E * H], F32R)
        s_rw = sb("s_rw", [P, HC, E])
        rw_hi = sb("rw_hi", [P, HC, E], F32R)
        rw_lo = sb("rw_lo", [P, HC, E], F32R)
        s_rb = sb("s_rb", [P, E])[BIAS:P, :]
        rb_st = sb("rb_st", [P, E], F32R)[BIAS:P, :]
        ones2 = c[BIAS:P, C_ON2:C_ON2 + P]
        ones2r = sb("ones2r", [P, P], F32R)[BIAS:P, :]

        ident = c[:, C_ID:C_ID + P]

        cwh = sb("cwh", [P, 2 * TAPS + 2])
        aneg = sb("aneg", [P, 2 * NS])
        aexp = sb("aexp", [P, 2 * NS])
        diagD = sb("diagD", [P, 2, P])
        xc = sb("xc", [P, 2, TOK])
        th = sb("th", [P, 2, TOK])
        spm, spe = xc, th
        ysum, yg = xc[:, 0, :].rearrange("p (e l) -> p e l", e=2), xc[:, 1, :].rearrange("p (e l) -> p e l", e=2)
        xs = th[:, :, 0:B * SC].rearrange("p k (b d s) -> p k b d s", b=B, d=2)
        occ = th[0:1, 0, B * SC:2 * B * SC].rearrange("p (b d s) -> p b d s", b=B, d=2)
        u = sb("u", [P, 2, TOK])
        stack = sb("stack", [P, TOK], BF16)
        delta = sb("delta", [P, 2, TOK])
        du = sb("du", [P, 2, TOK])
        dA = sb("dA", [P, 2, 2, 2, S])
        dBu = sb("dBu", [P, 2, TOK])
        Bb = sb("Bb", [P, 2, TOK])
        hs = sb("hs", [P, 2, TOK])
        psm = sb("psm", [P, 2, 512])
        r1 = dtl = psm[:, :, :].rearrange("p e l -> p (e l)")

        impc = sb("impc", [P, NT])
        junk = sb("junk", [P, S])
        cge = sb("cge", [P, NT])
        gtc = sb("gtc", [P, NT])
        eqc = sb("eqc", [P, NT])
        rank = sb("rank", [P, NT])
        kept = sb("kept", [P, NT])
        kep2 = sb("kep2", [P, NT])
        rk = sb("rk", [P, NT])
        onehot = sb("onehot", [P, NT, SLOTS])
        onescol = sb("onescol", [P, 1])
        QT = sb("QT", [P, HC, TOK])
        bdK = sb("bdK", [P, HC * B, HPC, SLOTS])
        Vbd = sb("Vbd", [SC, B * PAIRS, 2, HD + 1])
        mx = sb("mx", [P, NH])
        mTn = sb("mTn", [NH, P], F32R)
        Pm = sb("Pm", [P, PAIRS, SC])
        s_dtpT = Pm[:, 0:3, :].rearrange("p j s -> p (j s)")[:, 0:H]
        s_ho = Pm[0:NH, :, :].rearrange("p (m j) s -> p m (j s)", m=HC)
        PT = sb("PT", [SC, PAIRS, P])
        s_rows = PT[0:1, 0:4, :].rearrange("p (i j) t -> p i (j t)", i=2)
        rden = sb("rden", [P, NH])
        On = junk
        OT = sb("OT", [P, HC, P])
        x1 = sb("x1", [P, NT, H])
        x2, fin = x1, x1
        st = sb("st", [P, 6])
        mv1, mv2, mv3 = (sb(f"mv{i}", [P, NT, 2]) for i in (1, 2, 3))
        ve1, ve2, ve3 = (sb(f"ve{i}", [P, NT]) for i in (1, 2, 3))
        rs1, rs2, rs3 = (sb(f"rs{i}", [P, NT]) for i in (1, 2, 3))
        mhalf = sb("mhalf", [P, NT])

        x2h = sb("x2h", [P, HT, HC, P], F32R)
        x2l = sb("x2l", [P, HT, HC, P], F32R)
        lg = sb("lg", [P, HT, E])
        cmp1 = imp[:, 0:HT * E * E].rearrange("p (t i j) -> p t i j", t=HT, i=E)
        cmp2 = imp[:, 512:512 + HT * E * E].rearrange("p (t i j) -> p t i j", t=HT, i=E)
        rk8 = sb("rk8", [P, HT, E])
        lm = sb("lm", [P, HT])
        ls = sb("ls", [P, HT, E])
        le = sb("le", [P, HT, E])
        gs = sb("gs", [P, HT])
        gr = sb("gr", [P, HT])
        gates = sb("gates", [P, NT, E])
        cT = OT

        names = ["ctxT", "pkA", "dtpT", "pkC", "xT", "x", "wq", "wk", "wv", "wo", "rows", "ho", "sel", "bo", "ob",
                 "rw", "rb", "ow", "eb"]
        L = {n: sem("ld_" + n) for n in names}
        inproj_mm, xc_ok, th_ok, u_ok, xdbl_mm = sem("inproj_mm"), sem("xc_ok"), sem("th_ok"), sem("u_ok"), sem("xdbl_mm")
        part1_ok, dtl_ok, rest_ok, part2_ok, bc_ok = (sem(n) for n in ("part1_ok", "dtl_ok", "rest_ok", "part2_ok", "bc_ok"))
        dt_mm, spm_ok, spe_ok, spl_ok, delta_ok, du_ok = (sem(n) for n in ("dt_mm", "spm_ok", "spe_ok", "spl_ok", "delta_ok", "du_ok"))
        aexp_ok, aneg_ok, diag_ok, prep_ok = (sem(n) for n in ("aexp_ok", "aneg_ok", "diag_ok", "prep_ok"))
        imp_mm, imp_ok, impc_mm, onehot_ok, qt_mm, qt_ok = (sem(n) for n in ("imp_mm", "imp_ok", "impc_mm", "onehot_ok", "qt_mm", "qt_ok"))
        xsel_mm, xs_ok, kt_mm, v_mm, bdk_ok, vbd_ok, ho_ok = (sem(n) for n in ("xsel_mm", "xs_ok", "kt_mm", "v_mm", "bdk_ok", "vbd_ok", "ho_ok"))
        score_mm, max_ok, mT_mm, mTn_ok, shift_mm, probs_ok, pT_mm, pT_ok, av_mm, on_ok, oT_mm, oT_ok, wo_mm = (
            sem(n) for n in ("score_mm", "max_ok", "mT_mm", "mTn_ok", "shift_mm", "probs_ok", "pT_mm", "pT_ok", "av_mm",
                             "on_ok", "oT_mm", "oT_ok", "wo_mm"))
        xb_ok, y1_ok, mv1_ok, rs1_ok, x1_ok, zt_ok, z_ok = (sem(n) for n in ("xb_ok", "y1_ok", "mv1_ok", "rs1_ok", "x1_ok", "zt_ok", "z_ok"))
        b_mm, bb_ok, c_mm, dA_ok, dBu_ok, scan_ok, prod_ok, psm_ok, sum_mm = (
            sem(n) for n in ("b_mm", "bb_ok", "c_mm", "dA_ok", "dBu_ok", "scan_ok", "prod_ok", "psm_ok", "sum_mm"))
        ysum_ok, yg_ok, yT_mm, y2_ok, rs2_ok, x2_ok, x2T_mm, x2h_ok, x2l_ok, x2b_ok = (
            sem(n) for n in ("ysum_ok", "yg_ok", "yT_mm", "y2_ok", "rs2_ok", "x2_ok", "x2T_mm", "x2h_ok", "x2l_ok", "x2b_ok"))
        hi_ok, lo_ok, rt_mm, lg_ok, ls_ok, le_ok, gate_ok = (sem(n) for n in ("hi_ok", "lo_ok", "rt_mm", "lg_ok", "ls_ok", "le_ok", "gate_ok"))
        ex_mm, ge_ok, mix_ok, cT_mm, cT_ok, ow_mm, y3_ok, rs3_ok, fin_ok = (
            sem(n) for n in ("ex_mm", "ge_ok", "mix_ok", "cT_mm", "cT_ok", "ow_mm", "y3_ok", "rs3_ok", "fin_ok"))
        mv2_ok, mv3_ok, ewh_ok, ewl_ok = (sem(n) for n in ("mv2_ok", "mv3_ok", "ewh_ok", "ewl_ok"))
        ew_ld = [sem(f"ld_ew{q}") for q in range(4)]
        dve_step, pool_step, stored = sem("dve_step"), sem("pool_step"), sem("stored")

        X4 = [psS[:, 2 * e:2 * e + 2, :].rearrange("p n (b l) -> p (n b) l", b=2) for e in range(2)]
        yps = [psS[:, e, :] for e in range(2)]
        cps = psS[:, 2:4, :]
        out_t = out.rearrange("b (t p) h -> (b t) p h", p=P)

        block = ctx.enter_context(nc.Block())

        @block.sync
        def _(sp):
            for dst, src, n in ((a[:], pkA, "pkA"), (s_ctxT[:], ctxT, "ctxT"), (s_xT[:], xT, "xT"),
                                (s_dtpT[32:32 + DR, :], dtpT, "dtpT"), (s_x[:], x, "x"), (s_sel[:], sel, "sel"),
                                (s_wk[:], wk, "wk"), (s_wv[:], wv, "wv"), (s_wo[:], wo, "wo")):
                sp.dma_start(dst, src).then_inc(L[n], 16)
            sp.wait_ge(qt_mm, 4)
            sp.dma_start(s_ow[:], ow).then_inc(L["ow"], 16)
            for q in range(4):
                if q >= 2:
                    sp.wait_ge(ewl_ok, q - 1)
                sp.dma_start(ew_in[q % 2], ew[:, q // 2, (q % 2) * TOK:(q % 2 + 1) * TOK]).then_inc(ew_ld[q], 16)
            sp.wait_ge(ewl_ok, 4)
            sp.dma_start(s_eb, eb).then_inc(L["eb"], 16)
            for t in range(NT):
                sp.wait_ge(fin_ok, t + 1)
                sp.dma_start(out_t[t], fin[:, t, :]).then_inc(stored, 16)
            sp.wait_ge(stored, 16 * NT)

        @block.tensor
        def _(pe):
            def in_proj(e):
                for n in range(2):
                    mm = pe.matmul(psS[:, 2 * e + n, :], a[:, A_INP + e * P:A_INP + (e + 1) * P],
                                   s_ctxT[:, n * 512:(n + 1) * 512], start=True, stop=True)
                mm.then_inc(inproj_mm, 1)

            def importance(n):
                dst = psB[:, :] if n == 0 else psA[:, 0, :]
                for k in range(HC):
                    mm = pe.matmul(dst, c[:, C_WI + k * P:C_WI + (k + 1) * P], s_xT[:, k, n * 512:(n + 1) * 512],
                                   start=k == 0, stop=k == HC - 1)
                mm.then_inc(imp_mm, 1)

            def queries(i):
                m, n = i // 2, i % 2
                if i >= 2:
                    pe.wait_ge(qt_ok, i - 1)
                if i == 1:
                    pe.wait_ge(imp_ok, 2)
                for k in range(HC):
                    mm = pe.matmul(psA[:, 2 if n == 0 else 0, :], s_wq[:, k, m * P:(m + 1) * P],
                                   s_xT[:, k, n * 512:(n + 1) * 512], start=k == 0, stop=k == HC - 1)
                mm.then_inc(qt_mm, 1)

            def x_proj(n):
                for e in range(2):
                    mm = pe.matmul(psS[:, n, :], a[:, A_XP + e * P:A_XP + (e + 1) * P], u[:, e, n * 512:(n + 1) * 512],
                                   start=e == 0, stop=e == 1)
                mm.then_inc(xdbl_mm, 1)

            def delta_proj(e):
                for n in range(2):
                    bank = 2 + n if e == 0 else n
                    mm = pe.matmul(psS[:, bank, :], s_dtpT[32:32 + DR, e * P:(e + 1) * P],
                                   dtl[32:32 + DR, n * 512:(n + 1) * 512], start=True, stop=True)
                mm.then_inc(dt_mm, 1)

            def bcast_b(k, j):
                hb, n = k // NPAIR, 2 * (k % NPAIR) + j
                if 2 * k + j >= 1:
                    pe.wait_ge(bb_ok, 2 * k + j)
                pe.matmul(psB[:, :], s_sel[:, n, :], stack[:, hb * 512:(hb + 1) * 512],
                          start=True, stop=True).then_inc(b_mm, 1)

            def bcast_c(k):
                hb, p = k // NPAIR, k % NPAIR
                if k >= 1:
                    pe.wait_ge(prod_ok, 2 * k)
                for j in range(2):
                    mm = pe.matmul(psS[:, 2 + j, :], s_sel[:, NS + 2 * p + j, :], stack[:, hb * 512:(hb + 1) * 512],
                                   start=True, stop=True)
                mm.then_inc(c_mm, 1)

            def skip_sum(hb):
                for e in range(2):
                    if hb == 1:
                        pe.wait_ge(ysum_ok, e + 1)
                    pe.matmul(yps[e], diagD[:, e, :], u[:, e, hb * 512:(hb + 1) * 512], start=True, stop=False)

            def state_sum(k, e):
                pe.wait_ge(psm_ok, 2 * k + e + 1)
                pe.matmul(yps[e], ident, psm[:, e, :], start=False, stop=k % NPAIR == NPAIR - 1).then_inc(sum_mm, 1)

            def scores(un):
                b, t = un // 2, un
                if un >= 1:
                    pe.wait_ge(pT_ok, un)
                for m in range(HC):
                    mm = pe.matmul(psA[:, m, 0:HPC * SLOTS], QT[:, m, t * P:(t + 1) * P],
                                   bdK[:, m * B + b, :, :], start=True, stop=True)
                mm.then_inc(score_mm, 1)

            def max_turn(un):
                pe.wait_ge(max_ok, un + 1)
                if un >= 1:
                    pe.wait_ge(y1_ok, un)
                pe.transpose(psA[0:NH, 2, 0:P], mx[:, :], ident).then_inc(mT_mm, 1)

            def shift(un):
                pe.wait_ge(mTn_ok, un + 1)
                for m in range(HC):
                    mm = pe.matmul(psA[:, m, 0:HPC * SLOTS], mTn[:, :], ho_r[:, m, :], start=False, stop=True,
                                   skip_group_check=True)
                mm.then_inc(shift_mm, 1)

            def probs_turn(un):
                pe.wait_ge(probs_ok, un + 1)
                for j in range(PAIRS):
                    mm = pe.transpose(psA[0:SC, j // 4, (j % 4) * P:(j % 4 + 1) * P], Pm[:, j, :], ident)
                mm.then_inc(pT_mm, 1)

            def mix_values(un):
                pe.wait_ge(pT_ok, un + 1)
                for j in range(PAIRS):
                    mm = pe.matmul(psA[:, 2, P + 34 * j:P + 34 * (j + 1)], PT[:, j, :],
                                   Vbd[:, (un // 2) * PAIRS + j, :, :], start=True, stop=True)
                mm.then_inc(av_mm, 1)

            def out_turn(un):
                pe.wait_ge(on_ok, un + 1)
                for m in range(HC):
                    mm = pe.transpose(psA[:, 2, m * P:(m + 1) * P], On[:, m * P:(m + 1) * P], ident)
                mm.then_inc(oT_mm, 1)

            def out_proj(un):
                pe.wait_ge(oT_ok, un + 1)
                for m in range(HC):
                    mm = pe.matmul(psA[:, 2, 256:512], OT[:, m, :], s_wo[:, m, :], start=m == 0, stop=m == HC - 1)
                mm.then_inc(wo_mm, 1)

            pe.wait_ge(L["pkA"], 16)
            pe.wait_ge(L["ctxT"], 16)
            in_proj(0)
            in_proj(1)
            pe.wait_ge(L["pkC"], 16)
            pe.wait_ge(L["xT"], 16)
            importance(0)
            importance(1)
            pe.wait_ge(L["wq"], 16)
            queries(0)
            pe.wait_ge(imp_ok, 2)
            for t in range(NT):
                mm = pe.transpose(psA[:, 1, t:t + 1], imp[0:1, t * P:(t + 1) * P], ident[0:1, 0:1])
            mm.then_inc(impc_mm, 1)
            queries(1)
            queries(2)
            pe.wait_ge(u_ok, 2)
            x_proj(0)
            x_proj(1)
            queries(3)
            pe.wait_ge(L["dtpT"], 16)
            pe.wait_ge(dtl_ok, 2)
            delta_proj(0)
            pe.wait_ge(rest_ok, 2)
            delta_proj(1)
            pe.wait_ge(onehot_ok, 1)
            pe.wait_ge(prep_ok, 1)
            pe.wait_ge(L["x"], 16)
            pe.wait_ge(qt_ok, 4)
            for k in range(HC):
                for b in range(B):
                    for q in range(2):
                        t = 2 * b + q
                        pe.matmul(psA[:, 1, (k * B + b) * SLOTS:(k * B + b + 1) * SLOTS], s_x[:, t, k * P:(k + 1) * P],
                                  onehot[:, t, :], start=q == 0, stop=q == 1)
            for b in range(B):
                for q in range(2):
                    mm = pe.matmul(psA[0:1, 0, b * SLOTS:(b + 1) * SLOTS], onescol[:, :], onehot[:, 2 * b + q, :],
                                   start=q == 0, stop=q == 1)
            mm.then_inc(xsel_mm, 1)
            pe.wait_ge(xs_ok, 2)
            pe.wait_ge(L["wk"], 16)
            pe.wait_ge(L["rows"], 16)
            for m in range(HC):
                dst = psA[:, 2, m * B * SLOTS:(m + 1) * B * SLOTS]
                for k in range(HC):
                    pe.matmul(dst, s_wk[:, k, m * P:(m + 1) * P], xs[:, k, :, 0, :], start=k == 0, stop=False)
                mm = pe.matmul(dst, s_rows[0:1, 0, m * P:(m + 1) * P], occ[:, :, 0, :], start=False, stop=True)
            mm.then_inc(kt_mm, 1)
            pe.wait_ge(L["wv"], 16)
            for b in range(B):
                dst = psA[0:SC, b // 2, (b % 2) * H:(b % 2 + 1) * H]
                for k in range(HC):
                    pe.matmul(dst, xs[:, k, b, :, :], s_wv[:, k, :], start=k == 0, stop=False)
                mm = pe.matmul(dst, occ[:, b, :, :], s_rows[0:1, 1, :], start=False, stop=True)
            mm.then_inc(v_mm, 1)
            pe.wait_ge(bc_ok, 2)
            pe.wait_ge(L["sel"], 16)
            pe.wait_ge(imp_ok, 2)
            bcast_b(0, 0)
            bcast_b(0, 1)
            pe.wait_ge(delta_ok, 2)
            bcast_c(0)
            pe.wait_ge(diag_ok, 1)
            skip_sum(0)
            pe.wait_ge(bdk_ok, 1)
            pe.wait_ge(vbd_ok, 1)
            pe.wait_ge(ho_ok, 1)
            pe.wait_ge(L["wo"], 16)
            for k in range(ITER):
                un, last = k // 2, k == ITER - 1
                if k % 2 == 0:
                    scores(un)
                    if not last:
                        bcast_b(k + 1, 0)
                    max_turn(un)
                    shift(un)
                    state_sum(k, 0)
                    bcast_b(k + 1, 1)
                    probs_turn(un)
                    bcast_c(k + 1)
                    state_sum(k, 1)
                    mix_values(un)
                else:
                    if not last:
                        bcast_b(k + 1, 0)
                    out_turn(un)
                    state_sum(k, 0)
                    out_proj(un)
                    if not last:
                        bcast_b(k + 1, 1)
                        bcast_c(k + 1)
                    state_sum(k, 1)
                    if k == NPAIR - 1:
                        skip_sum(1)
            def y_turn(t):
                b, q = t // 2, t % 2
                pe.wait_ge(yg_ok, 4 if b >= 2 else 2)
                if t >= 2:
                    pe.wait_ge(y2_ok, t - 1)
                for e in range(2):
                    mm = pe.transpose(psA[:, t % 2, e * P:(e + 1) * P], yg[:, e, (b % 2) * S + q * P:(b % 2) * S + (q + 1) * P], ident)
                mm.then_inc(yT_mm, 1)

            def x2_turn(t):
                pe.wait_ge(x2_ok, t + 1)
                if t >= 1:
                    pe.wait_ge(x2l_ok, t)
                if t % HT == 0:
                    pe.wait_ge(y2_ok, t + HT)
                for m in range(HC):
                    mm = pe.transpose(psA[:, 0, m * P:(m + 1) * P], x2[:, t, m * P:(m + 1) * P], ident)
                mm.then_inc(x2T_mm, 1)

            def router(t):
                pe.wait_ge(x2h_ok, t + 1)
                pe.wait_ge(x2l_ok, t + 1)
                dst = psA[:, 1, (t % HT) * E:(t % HT + 1) * E]
                pe.matmul(dst, ones2r[:, :], rb_st[:, :], start=True, stop=False)
                i = 0
                for m in range(HC):
                    for xx in (x2h, x2l):
                        for ww in (rw_hi, rw_lo):
                            i += 1
                            mm = pe.matmul(dst, xx[:, t % HT, m, :], ww[:, m, :], start=False, stop=i == 4 * HC)
                mm.then_inc(rt_mm, 1)

            def experts(t):
                for q in range(E // 2):
                    i = t * (E // 2) + q
                    if i >= 4:
                        pe.wait_ge(ge_ok, i - 3)
                    cols = slice(q * 512, (q + 1) * 512)
                    dst = psS[:, i % 4, :]
                    pe.matmul(dst, ones2r[:, :], eb_st[:, cols], start=True, stop=False)
                    for m in range(HC):
                        pe.matmul(dst, x2h[:, t % HT, m, :], ew_hi[:, m, cols], start=False, stop=False)
                        pe.matmul(dst, x2h[:, t % HT, m, :], ew_lo[:, m, cols], start=False, stop=False)
                        mm = pe.matmul(dst, x2l[:, t % HT, m, :], ew_hi[:, m, cols], start=False, stop=m == HC - 1)
                    mm.then_inc(ex_mm, 1)

            def mixed_out(t):
                pe.wait_ge(mix_ok, (E // 2) * (t + 1))
                if t >= 1:
                    pe.wait_ge(cT_ok, t)
                for m in range(HC):
                    mm = pe.transpose(psB[:, m * P:(m + 1) * P], cmb[:, t % 2, m * P:(m + 1) * P], ident)
                mm.then_inc(cT_mm, 1)
                pe.wait_ge(cT_ok, t + 1)
                if t >= 1:
                    pe.wait_ge(y3_ok, t)
                for m in range(HC):
                    mm = pe.matmul(psA[:, 2, 0:H], cT[:, m, :], s_ow[:, m, :], start=m == 0, stop=m == HC - 1)
                mm.then_inc(ow_mm, 1)

            for hb in range(2):
                tiles = range(hb * HT, (hb + 1) * HT)
                if hb == 0:
                    pe.wait_ge(y1_ok, NT)
                else:
                    pe.wait_ge(lg_ok, 1)
                for t in tiles:
                    y_turn(t)
                if hb == 0:
                    pe.wait_ge(hi_ok, 1)
                    pe.wait_ge(lo_ok, 1)
                    pe.wait_ge(ysum_ok, 4)
                    pe.wait_ge(prod_ok, 2 * ITER)
                    pe.wait_ge(L["ow"], 16)
                for t in tiles:
                    x2_turn(t)
                    router(t)
                for t in tiles:
                    experts(t)
                    if t % HT >= 1:
                        mixed_out(t - 1)
                mixed_out(tiles[-1])

        @block.scalar
        def _(act):
            for dst, src, n in ((c[:], pkC, "pkC"), (s_wq[:], wq, "wq"), (s_rows, rows, "rows"), (s_ho, headones, "ho"),
                                (s_bo[:], bo, "bo"), (s_rw[:], rw, "rw"), (s_rb, rb, "rb"), (s_ob[:], ob, "ob")):
                act.dma_start(dst, src).then_inc(L[n], 16)

            def exps(k, e):
                hb, p = k // NPAIR, k % NPAIR
                act.wait_ge(aneg_ok, 1)
                if k >= 1:
                    act.wait_ge(scan_ok, 2 * (k - 1) + e + 1)
                for j in range(2):
                    o = dA[:, e, j, :, 1:]
                    i = delta[:, e, hb * 512:(hb + 1) * 512].rearrange("p (b l) -> p b l", b=2)[:, :, 1:]
                    x_ = act.activation(o, i, ACT.Exp, scale=aneg[:, e * NS + 2 * p + j:e * NS + 2 * p + j + 1])
                x_.then_inc(dA_ok, 1)

            def copy_b(k, j):
                act.wait_ge(b_mm, 2 * k + j + 1)
                if k >= 2:
                    act.wait_ge(dBu_ok, 2 * (k - 1))
                act.copy(Bb[:, k % 2, j * 512:(j + 1) * 512], psB[:, :]).then_inc(bb_ok, 1)

            act.wait_ge(prep_ok, 1)
            act.wait_ge(L["pkA"], 16)
            act.activation(aexp[:, :], a[:, A_AL:A_AL + 2 * NS], ACT.Exp).then_inc(aexp_ok, 1)
            act.wait_ge(L["pkC"], 16)
            for n in range(2):
                act.wait_ge(imp_mm, n + 1)
                act.activation(imp[:, n * 512:(n + 1) * 512], psB[:, :] if n == 0 else psA[:, 0, :], ACT.Identity,
                               bias=c[:, C_BI:C_BI + 1]).then_inc(imp_ok, 1)

            def copy_q(i):
                m, n = i // 2, i % 2
                act.wait_ge(qt_mm, i + 1)
                act.activation(QT[:, m, n * 512:(n + 1) * 512], psA[:, 2 if n == 0 else 0, :], ACT.Identity,
                               bias=c[:, C_BQ + m:C_BQ + m + 1]).then_inc(qt_ok, 1)

            copy_q(0)
            for e in range(2):
                act.wait_ge(xc_ok, e + 1)
                act.activation(th[:, e, :], xc[:, e, :], ACT.Tanh).then_inc(th_ok, 1)
                copy_q(1 + e)
            for n in range(2):
                act.wait_ge(xdbl_mm, n + 1)
                cols = slice(n * 512, (n + 1) * 512)
                act.copy(stack[:, cols], psS[:, n, :]).then_inc(part1_ok, 1)
                act.copy(dtl[32:32 + DR, cols], psS[32:32 + DR, n, :]).then_inc(dtl_ok, 1)
            for n in range(2):
                act.wait_ge(rest_ok, n + 1)
                cols = slice(n * 512, (n + 1) * 512)
                act.copy(stack[64:128, cols], r1[64:128, cols]).then_inc(part2_ok, 1)
            copy_q(3)
            for e in range(2):
                act.wait_ge(spm_ok, e + 1)
                act.activation(spe[:, e, :], spm[:, e, :], ACT.Exp).then_inc(spe_ok, 1)
            for e in range(2):
                act.wait_ge(spe_ok, e + 1)
                act.activation(spm[:, e, :], spe[:, e, :], ACT.Ln, bias=onescol[:, 0:1]).then_inc(spl_ok, 1)
            act.wait_ge(delta_ok, 1)
            exps(0, 0)
            act.wait_ge(xsel_mm, 1)
            act.wait_ge(spl_ok, 2)
            sel_in = psA[:, 1, 0:HC * B * SLOTS].rearrange("p (k b s) -> p k b s", k=HC, s=SLOTS)
            for d in range(2):
                act.copy(xs[:, :, :, d, :], sel_in)
                act.copy(occ[:, :, d, :], psA[0:1, 0, 0:B * SLOTS].rearrange("p (b s) -> p b s", s=SLOTS)).then_inc(xs_ok, 1)
            copy_b(0, 0)
            copy_b(0, 1)
            act.wait_ge(delta_ok, 2)
            exps(0, 1)
            act.wait_ge(L["ho"], 16)
            act.copy(ho_r[:, :, :], s_ho[:, :, :]).then_inc(ho_ok, 1)
            for k in range(ITER):
                un, more = k // 2, k < ITER - 1
                if more:
                    exps(k + 1, 0)
                if 4 <= k < 8:
                    q = k - 4
                    act.wait_ge(ew_ld[q], 16)
                    act.copy(ew_hi[:, q // 2, (q % 2) * TOK:(q % 2 + 1) * TOK], ew_in[q % 2]).then_inc(ewh_ok, 1)
                if k % 2 == 0:
                    if more:
                        copy_b(k + 1, 0)
                    act.wait_ge(mT_mm, un + 1)
                    act.mul(mTn[:, :], psA[0:NH, 2, 0:P], -1.0).then_inc(mTn_ok, 1)
                    if more:
                        copy_b(k + 1, 1)
                    act.wait_ge(shift_mm, un + 1)
                    if un >= 1:
                        act.wait_ge(pT_mm, un)
                    act.activation(Pm[:, :, :].rearrange("p (m j) s -> p m (j s)", m=HC), psA[:, 0:2, 0:HPC * SLOTS],
                                   ACT.Exp, scale=float(HD) ** -0.5).then_inc(probs_ok, 1)
                    if more:
                        exps(k + 1, 1)
                    act.wait_ge(pT_mm, un + 1)
                    if un >= 1:
                        act.wait_ge(av_mm, un)
                    act.copy(PT[:, :, :].rearrange("p (m j) s -> p m (j s)", m=2), psA[0:SC, 0:2, :]).then_inc(pT_ok, 1)
                else:
                    if more:
                        copy_b(k + 1, 0)
                    act.wait_ge(oT_mm, un + 1)
                    if un >= 1:
                        act.wait_ge(wo_mm, un)
                    act.copy(OT[:, :, :].rearrange("p m t -> p (m t)"), psA[:, 2, 0:256]).then_inc(oT_ok, 1)
                    if more:
                        copy_b(k + 1, 1)
                        exps(k + 1, 1)
                    if k % NPAIR == NPAIR - 1:
                        for e in range(2):
                            act.wait_ge(sum_mm, 2 * k + e + 1)
                            if k > NPAIR:
                                act.wait_ge(yg_ok, e + 1)
                            act.copy(ysum[:, e, :], yps[e]).then_inc(ysum_ok, 1)
                    if un >= 1:
                        act.wait_ge(x1_ok, un)
                        act.activation(zt[:, un - 1, :], x1[:, un - 1, :], ACT.Tanh, scale=0.5).then_inc(zt_ok, 1)
            act.wait_ge(x1_ok, NT)
            act.activation(zt[:, NT - 1, :], x1[:, NT - 1, :], ACT.Tanh, scale=0.5).then_inc(zt_ok, 1)
            act.wait_ge(L["rw"], 16)
            act.wait_ge(L["rb"], 16)
            act.wait_ge(prep_ok, 1)
            act.wait_ge(L["eb"], 16)
            act.copy(rw_hi[:, :, :], s_rw[:, :, :])
            act.copy(ones2r[:, :], ones2[:, :])
            act.copy(rb_st[:, :], s_rb[:, :])
            act.copy(eb_st[:, :], s_eb).then_inc(hi_ok, 1)
            for hb in range(2):
                tiles = range(hb * HT, (hb + 1) * HT)
                for t in tiles:
                    act.wait_ge(x2T_mm, t + 1)
                    if hb == 1:
                        act.wait_ge(ex_mm, (E // 2) * HT)
                    act.copy(x2h[:, t % HT, :, :].rearrange("p m t -> p (m t)"), psA[:, 0, 0:256]).then_inc(x2h_ok, 1)
                act.wait_ge(ls_ok, hb + 1)
                act.activation(le[:, :, :], ls[:, :, :], ACT.Exp).then_inc(le_ok, 1)

                def copy_mixed(t):
                    act.wait_ge(cT_mm, t + 1)
                    if t >= 1:
                        act.wait_ge(ow_mm, t)
                    act.copy(cT[:, :, :].rearrange("p m t -> p (m t)"), psB[:, 0:256]).then_inc(cT_ok, 1)

                for t in tiles:
                    for q in range(E // 2):
                        i = t * (E // 2) + q
                        act.wait_ge(ex_mm, i + 1)
                        if i >= 4:
                            act.wait_ge(mix_ok, i - 3)
                        act.activation(ge[:, i % 4, :], psS[:, i % 4, :], ACT.Gelu_apprx_tanh).then_inc(ge_ok, 1)
                        if t % HT >= 1 and q == 1:
                            copy_mixed(t - 1)
                copy_mixed(tiles[-1])

        @block.vector
        def _(dve):
            steps = [0]

            def link(ins):
                steps[0] += 1
                ins.then_inc(dve_step, 1)
                dve.wait_ge(dve_step, steps[0])

            def conv(e):
                dve.wait_ge(inproj_mm, e + 1)
                o = xc[:, e, :].rearrange("p (b l) -> p b l", b=B)
                link(dve.tensor_scalar(o, X4[e], cwh[:, e * TAPS + 3:e * TAPS + 4], cwh[:, 2 * TAPS + e:2 * TAPS + e + 1],
                                       ALU.mult, ALU.add))
                for d in range(1, TAPS):
                    i = dve.scalar_tensor_tensor(o[:, :, d:], X4[e][:, :, :S - d],
                                                 cwh[:, e * TAPS + 3 - d:e * TAPS + 4 - d], o[:, :, d:], ALU.mult, ALU.add)
                    if d < TAPS - 1:
                        link(i)
                i.then_inc(xc_ok, 1)

            def silu(e):
                dve.wait_ge(th_ok, e + 1)
                dve.scalar_tensor_tensor(u[:, e, :], th[:, e, :], 1.0, xc[:, e, :], ALU.add, ALU.mult).then_inc(u_ok, 1)

            def count(t):
                row, col = imp[:, (t // 2) * S:(t // 2 + 1) * S], impc[:, t:t + 1]
                link(dve.tensor_scalar(junk[:, :], row, col, None, ALU.is_ge, ALU.add, accum_out=cge[:, t:t + 1]))
                link(dve.tensor_scalar(junk[:, :], row, col, None, ALU.is_gt, ALU.add, accum_out=gtc[:, t:t + 1]))
                link(dve.scalar_tensor_tensor(junk[:, :], row, col, c[:, C_TRI + (t % 2) * S:C_TRI + (t % 2 + 1) * S],
                                              ALU.is_equal, ALU.mult, accum_out=eqc[:, t:t + 1]))

            def delta_in(e):
                return psS[:, 2 if e == 0 else 0:4 if e == 0 else 2, :].rearrange("p n l -> p (n l)")

            dve.wait_ge(L["pkA"], 16)
            link(dve.tensor_scalar(cwh[:, :], a[:, A_CW:A_CB + 2], 0.5, None, ALU.mult))
            conv(0)
            conv(1)
            silu(0)
            silu(1)
            dve.wait_ge(aexp_ok, 1)
            dve.tensor_scalar(aneg[:, :], aexp[:, :], -1.0, None, ALU.mult).then_inc(aneg_ok, 1)
            dve.wait_ge(L["pkC"], 16)
            for e in range(2):
                i = dve.tensor_scalar(diagD[:, e, :], ident, a[:, A_D + e:A_D + e + 1], None, ALU.mult)
            i.then_inc(diag_ok, 1)
            dve.wait_ge(impc_mm, 1)
            dve.wait_ge(imp_ok, 2)
            link(dve.tensor_copy(impc[:, :], psA[:, 1, 0:NT]))
            for t in range(4):
                count(t)
            for n in range(2):
                dve.wait_ge(part1_ok, n + 1)
                cols = slice(n * 512, (n + 1) * 512)
                dve.tensor_tensor(r1[64:128, cols], psS[64:128, n, :], stack[64:128, cols], ALU.subtract).then_inc(rest_ok, 1)
            for t in range(4, 5):
                count(t)
            for n in range(2):
                dve.wait_ge(part2_ok, n + 1)
                cols = slice(n * 512, (n + 1) * 512)
                dve.tensor_tensor(stack[96:128, cols], r1[96:128, cols], stack[96:128, cols], ALU.subtract).then_inc(bc_ok, 1)
            for e in range(2):
                dve.wait_ge(dt_mm, e + 1)
                dve.tensor_scalar(spm[:, e, :], delta_in(e), a[:, A_DTB + e:A_DTB + e + 1], 40.0, ALU.add,
                                  ALU.min).then_inc(spm_ok, 1)
            for t in range(5, NT):
                count(t)
            link(dve.tensor_tensor(rank[:, :], gtc[:, :], eqc[:, :], ALU.add))
            link(dve.tensor_scalar(kept[:, :], cge[:, :], float(TIDX), None, ALU.is_le))
            link(dve.tensor_scalar(kep2[:, :], rank[:, :], float(MINTOK), None, ALU.is_lt))
            link(dve.tensor_tensor(kept[:, :], kept[:, :], kep2[:, :], ALU.max))
            link(dve.tensor_scalar(kept[:, :], kept[:, :], -1000.0, 1000.0, ALU.mult, ALU.add))
            link(dve.tensor_tensor(rk[:, :], rank[:, :], kept[:, :], ALU.add))
            dve.tensor_tensor(onehot[:, :, :], c[:, C_IOTA:C_IOTA + SLOTS].unsqueeze(1).to_broadcast([P, NT, SLOTS]),
                              rk[:, :].unsqueeze(2).to_broadcast([P, NT, SLOTS]), ALU.is_equal).then_inc(onehot_ok, 1)
            for e in range(2):
                dve.wait_ge(spl_ok, e + 1)
                dve.scalar_tensor_tensor(delta[:, e, :], delta_in(e), a[:, A_DTB + e:A_DTB + e + 1], spm[:, e, :],
                                         ALU.add, ALU.max).then_inc(delta_ok, 1)
                dve.wait_ge(delta_ok, e + 1)
                dve.tensor_tensor(du[:, e, :], delta[:, e, :], u[:, e, :], ALU.mult).then_inc(du_ok, 1)

            def keys_values():
                dve.wait_ge(kt_mm, 1)
                dve.tensor_tensor(bdK[:, :, :, :],
                                  psA[:, 2, 0:HC * B * SLOTS].rearrange("p (g s) -> p g s", s=SLOTS).unsqueeze(2)
                                  .to_broadcast([P, HC * B, HPC, SLOTS]),
                                  c[:, C_M8:C_M8 + HPC].unsqueeze(1).unsqueeze(3).to_broadcast([P, HC * B, HPC, SLOTS]),
                                  ALU.mult).then_inc(bdk_ok, 1)
                dve.wait_ge(v_mm, 1)
                for g in range(2):
                    dve.tensor_tensor(Vbd[:, g * 2 * PAIRS:(g + 1) * 2 * PAIRS, :, 0:HD],
                                      psA[0:SC, g, :].rearrange("p (g h d) -> p g h d", h=2, d=HD),
                                      c[0:SC, C_VM:C_VM + 2].unsqueeze(1).unsqueeze(3).to_broadcast([SC, 2 * PAIRS, 2, HD]),
                                      ALU.mult)
                dve.tensor_copy(Vbd[:, :, :, HD:HD + 1],
                                c[0:SC, C_VD:C_VD + 2].unsqueeze(1).unsqueeze(3).to_broadcast([SC, B * PAIRS, 2, 1])
                                ).then_inc(vbd_ok, 1)

            def scan(k, e):
                dve.wait_ge(dA_ok, 2 * k + e + 1)
                dve.wait_ge(dBu_ok, 2 * k + e + 1)
                dve.tensor_tensor_scan(hs[:, e, :], dA[:, e, :, :, :].rearrange("p j b l -> p (j b l)"), dBu[:, e, :],
                                       0.0, ALU.mult, ALU.add).then_inc(scan_ok, 1)

            def times_c(k, e):
                dve.wait_ge(c_mm, k + 1)
                dve.wait_ge(scan_ok, 2 * k + e + 1)
                dve.tensor_tensor(hs[:, e, :], hs[:, e, :], cps.rearrange("p n l -> p (n l)"), ALU.mult).then_inc(prod_ok, 1)

            def add_pair(k, e):
                dve.wait_ge(prod_ok, 2 * k + e + 1)
                if k >= 1:
                    dve.wait_ge(sum_mm, 2 * (k - 1) + e + 1)
                dve.tensor_tensor(psm[:, e, :], hs[:, e, 0:512], hs[:, e, 512:1024], ALU.add).then_inc(psm_ok, 1)

            def score_max(un):
                dve.wait_ge(score_mm, un + 1)
                if un >= 1:
                    dve.wait_ge(mT_mm, un)
                dve.tensor_reduce(mx[:, :].rearrange("p (m h) -> p m h", m=HC),
                                  psA[:, 0:2, 0:HPC * SLOTS].rearrange("p m (h s) -> p m h s", s=SLOTS), AX.X, ALU.max
                                  ).then_inc(max_ok, 1)

            def normalise(un):
                dve.wait_ge(av_mm, un + 1)
                if un >= 1:
                    dve.wait_ge(oT_mm, un)
                o = psA[:, 2, P:P + NH * (HD + 1)].rearrange("p (h d) -> p h d", d=HD + 1)
                link(dve.reciprocal(rden[:, :].unsqueeze(2), o[:, :, HD:HD + 1]))
                dve.tensor_tensor(On[:, :].rearrange("p (h d) -> p h d", d=HD), o[:, :, 0:HD],
                                  rden[:, :].unsqueeze(2).to_broadcast([P, NH, HD]), ALU.mult).then_inc(on_ok, 1)

            def moments(y, mv, done):
                link(dve.bn_stats(st[:, :], y))
                dve.bn_aggr(mv, st[:, :]).then_inc(done, 1)

            def residual1(t):
                dve.wait_ge(wo_mm, t + 1)
                dve.wait_ge(xb_ok, t + 1)
                dve.tensor_tensor(x1[:, t, :], psA[:, 2, 256:512], xb[:, t, :], ALU.add).then_inc(y1_ok, 1)
                dve.wait_ge(y1_ok, t + 1)
                moments(x1[:, t, :], mv1[:, t, :], mv1_ok)

            def norm1(t):
                dve.wait_ge(rs1_ok, t + 1)
                dve.tensor_scalar(x1[:, t, :], x1[:, t, :], mv1[:, t, 0:1], rs1[:, t:t + 1], ALU.subtract,
                                  ALU.mult).then_inc(x1_ok, 1)

            def gate_z(t):
                dve.wait_ge(zt_ok, t + 1)
                dve.scalar_tensor_tensor(zt[:, t, :], zt[:, t, :], 1.0, x1[:, t, :], ALU.add, ALU.mult).then_inc(z_ok, 1)

            def gated(hb, e):
                dve.wait_ge(ysum_ok, 2 * hb + e + 1)
                dve.wait_ge(z_ok, 4 * (hb + 1))
                if hb == 1:
                    dve.wait_ge(yT_mm, HT)
                dve.scalar_tensor_tensor(yg[:, e, :].rearrange("p (b l) -> p b l", b=2),
                                         ysum[:, e, :].rearrange("p (b l) -> p b l", b=2), 0.5,
                                         zt[:, :, :].rearrange("p (b e) l -> p b e l", e=2)[:, 2 * hb:2 * hb + 2, e, :],
                                         ALU.mult, ALU.mult).then_inc(yg_ok, 1)

            keys_values()
            for k in range(ITER):
                un = k // 2
                scan(k, 0)
                times_c(k, 0)
                if k % 2 == 0:
                    score_max(un)
                else:
                    normalise(un)
                add_pair(k, 0)
                scan(k, 1)
                times_c(k, 1)
                add_pair(k, 1)
                if k % 2 == 0 and un >= 1:
                    norm1(un - 1)
                if k % 2 == 1:
                    residual1(un)
                    if un >= 1:
                        gate_z(un - 1)
                if k == NPAIR + 2:
                    gated(0, 0)
                    gated(0, 1)
            norm1(NT - 1)
            gate_z(NT - 1)

            def residual2(t):
                dve.wait_ge(yT_mm, t + 1)
                dve.tensor_tensor(x2[:, t, :], psA[:, t % 2, 0:H], x1[:, t, :], ALU.add).then_inc(y2_ok, 1)
                dve.wait_ge(y2_ok, t + 1)
                moments(x2[:, t, :], mv2[:, t, :], mv2_ok)

            def norm2(t):
                dve.wait_ge(rs2_ok, t + 1)
                dve.tensor_scalar(x2[:, t, :], x2[:, t, :], mv2[:, t, 0:1], rs2[:, t:t + 1], ALU.subtract,
                                  ALU.mult).then_inc(x2_ok, 1)

            def x2_low(t):
                dve.wait_ge(x2h_ok, t + 1)
                dve.tensor_tensor(x2l[:, t % HT, :, :].rearrange("p m t -> p (m t)"), psA[:, 0, 0:256],
                                  x2h[:, t % HT, :, :].rearrange("p m t -> p (m t)").bitcast(F32), ALU.subtract
                                  ).then_inc(x2l_ok, 1)

            def gating(hb):
                dve.wait_ge(rt_mm, HT * (hb + 1))
                dve.tensor_copy(lg[:, :, :].rearrange("p t e -> p (t e)"), psA[:, 1, 0:HT * E]).then_inc(lg_ok, 1)
                dve.wait_ge(lg_ok, hb + 1)
                over = lg[:, :, :].unsqueeze(2).to_broadcast([P, HT, E, E])
                own = lg[:, :, :].unsqueeze(3).to_broadcast([P, HT, E, E])
                tri8 = c[:, C_TR8:C_TR8 + E * E].rearrange("p (i j) -> p i j", i=E).unsqueeze(1).to_broadcast([P, HT, E, E])
                link(dve.tensor_reduce(lm[:, :], lg[:, :, :], AX.X, ALU.max))
                dve.tensor_tensor(ls[:, :, :], lg[:, :, :], lm[:, :].unsqueeze(2).to_broadcast([P, HT, E]),
                                  ALU.subtract).then_inc(ls_ok, 1)
                dve.tensor_tensor(cmp1, over, own, ALU.is_gt)
                link(dve.tensor_tensor(cmp2, over, own, ALU.is_equal))
                link(dve.tensor_tensor(cmp2, cmp2, tri8, ALU.mult))
                link(dve.tensor_tensor(cmp1, cmp1, cmp2, ALU.add))
                link(dve.tensor_reduce(rk8[:, :, :], cmp1, AX.X, ALU.add))
                link(dve.tensor_scalar(rk8[:, :, :], rk8[:, :, :], 2.0, None, ALU.is_lt))
                dve.wait_ge(le_ok, hb + 1)
                link(dve.tensor_tensor(le[:, :, :], le[:, :, :], rk8[:, :, :], ALU.mult))
                link(dve.tensor_reduce(gs[:, :], le[:, :, :], AX.X, ALU.add))
                link(dve.reciprocal(gr[:, :], gs[:, :]))
                link(dve.tensor_tensor(gates[:, hb * HT:(hb + 1) * HT, :], le[:, :, :],
                                       gr[:, :].unsqueeze(2).to_broadcast([P, HT, E]), ALU.mult))

            def mix(t, q):
                i, o = t * (E // 2) + q, cmb[:, t % 2, :]
                if q == 0 and t >= 2:
                    dve.wait_ge(cT_mm, t - 1)
                dve.wait_ge(ge_ok, i + 1)
                for h in range(2):
                    x_ = 2 * q + h
                    g, src = gates[:, t, x_:x_ + 1], ge[:, i % 4, h * H:(h + 1) * H]
                    if x_ == 0:
                        link(dve.tensor_scalar(o, src, g, None, ALU.mult))
                    else:
                        ins = dve.scalar_tensor_tensor(o, src, g, o, ALU.mult, ALU.add)
                        if h == 0:
                            link(ins)
                ins.then_inc(mix_ok, 1)
                dve.wait_ge(mix_ok, i + 1)

            def residual3(t):
                dve.wait_ge(ow_mm, t + 1)
                dve.wait_ge(x2b_ok, t // HT + 1)
                dve.tensor_tensor(y3[:, t % 2, :], psA[:, 2, 0:H], x2b[:, t, :], ALU.add).then_inc(y3_ok, 1)
                dve.wait_ge(y3_ok, t + 1)
                moments(y3[:, t % 2, :], mv3[:, t, :], mv3_ok)

            def norm3(t):
                dve.wait_ge(rs3_ok, t + 1)
                dve.tensor_scalar(fin[:, t, :], y3[:, t % 2, :], mv3[:, t, 0:1], rs3[:, t:t + 1], ALU.subtract,
                                  ALU.mult).then_inc(fin_ok, 1)

            for hb in range(2):
                tiles = range(hb * HT, (hb + 1) * HT)
                if hb == 1:
                    gated(1, 0)
                    gated(1, 1)
                for t in tiles:
                    residual2(t)
                    if t % HT >= 1:
                        norm2(t - 1)
                norm2(tiles[-1])
                for t in tiles:
                    x2_low(t)
                gating(hb)
                for t in tiles:
                    for q in range(E // 2):
                        mix(t, q)
                        if q == 2 and t % HT >= 1:
                            residual3(t - 1)
                    if t % HT >= 1:
                        norm3(t - 1)
                residual3(tiles[-1])
                norm3(tiles[-1])

        @block.gpsimd
        def _(pool):
            steps = [0]

            def link(ins):
                steps[0] += 1
                ins.then_inc(pool_step, 1)
                pool.wait_ge(pool_step, steps[0])

            def rstd(mv, ve, rs, t, done, ready):
                pool.wait_ge(ready, t + 1)
                link(pool.tensor_scalar(ve[:, t:t + 1], mv[:, t, 1:2], EPS, 1.0, ALU.add, ALU.mult))
                pool.tensor_tensor(rs[:, t:t + 1], ve[:, t:t + 1], mhalf[:, t:t + 1], ALU.pow).then_inc(done, 1)

            for e in range(2):
                pool.memset(dA[:, e, :, :, 0:1], 0.0)
            pool.memset(mhalf[:, :], -0.5)
            pool.memset(onescol[:, :], 1.0).then_inc(prep_ok, 1)
            pool.wait_ge(prep_ok, 1)
            pool.wait_ge(L["bo"], 16)
            for k in range(ITER):
                hb = k // NPAIR
                for e in range(2):
                    pool.wait_ge(du_ok, e + 1)
                    pool.wait_ge(bb_ok, 2 * k + 2)
                    if k >= 1:
                        pool.wait_ge(scan_ok, 2 * (k - 1) + e + 1)
                    pool.tensor_tensor(dBu[:, e, :].rearrange("p (j l) -> p j l", j=2),
                                       Bb[:, k % 2, :].rearrange("p (j l) -> p j l", j=2),
                                       du[:, e, hb * 512:(hb + 1) * 512].unsqueeze(1).to_broadcast([P, 2, 512]),
                                       ALU.mult).then_inc(dBu_ok, 1)
                if k % 2 == 0 and k >= 2:
                    rstd(mv1, ve1, rs1, k // 2 - 1, rs1_ok, mv1_ok)
                if 4 <= k < 8:
                    q = k - 4
                    pool.wait_ge(ewh_ok, q + 1)
                    part = slice((q % 2) * TOK, (q % 2 + 1) * TOK)
                    pool.tensor_tensor(ew_lo[:, q // 2, part], ew_in[q % 2], ew_hi[:, q // 2, part].bitcast(F32),
                                       ALU.subtract).then_inc(ewl_ok, 1)
                if k % 2 == 0:
                    pool.wait_ge(xsel_mm, 1)
                    pool.tensor_tensor(xb[:, k // 2, :], s_x[:, k // 2, :], s_bo[:, :], ALU.add).then_inc(xb_ok, 1)
            rstd(mv1, ve1, rs1, NT - 1, rs1_ok, mv1_ok)
            pool.wait_ge(hi_ok, 1)
            link(pool.tensor_tensor(rw_lo[:, :, :], s_rw[:, :, :], rw_hi[:, :, :].bitcast(F32), ALU.subtract))
            link(pool.tensor_tensor(rb_st[32:33, :], s_rb[32:33, :], rb_st[32:33, :].bitcast(F32), ALU.subtract))
            pool.tensor_tensor(eb_st[32:33, :], s_eb[32:33, :], eb_st[32:33, :].bitcast(F32), ALU.subtract).then_inc(lo_ok, 1)
            pool.wait_ge(lo_ok, 1)
            for hb in range(2):
                tiles = range(hb * HT, (hb + 1) * HT)
                for t in tiles:
                    rstd(mv2, ve2, rs2, t, rs2_ok, mv2_ok)
                pool.wait_ge(x2_ok, HT * (hb + 1))
                pool.wait_ge(L["ob"], 16)
                pool.tensor_tensor(x2b[:, tiles[0]:tiles[-1] + 1, :], x2[:, tiles[0]:tiles[-1] + 1, :],
                                   s_ob[:, :].unsqueeze(1).to_broadcast([P, HT, H]), ALU.add).then_inc(x2b_ok, 1)
                for t in tiles:
                    rstd(mv3, ve3, rs3, t, rs3_ok, mv3_ok)


def constants():
    p = np.arange(P)
    j = np.arange(S)
    tri = np.concatenate([(j[None, :] < (q * P + p)[:, None]) for q in range(2)], 1).astype(np.float32)
    mask8 = (p[:, None] // HD == np.arange(HPC)[None, :]).astype(np.float32)
    iota = np.broadcast_to(np.arange(SLOTS, dtype=np.float32), (P, SLOTS))
    own = (p[:, None] // SLOTS == np.arange(2)[None, :]).astype(np.float32)
    weight = np.where(p % SLOTS == SLOTS - 1, S - SLOTS + 1, 1).astype(np.float32)
    i8 = np.arange(E)
    tri8 = np.broadcast_to((i8[None, :] < i8[:, None]).astype(np.float32).reshape(1, -1), (P, E * E))
    ones2 = np.zeros((P, P), np.float32)
    ones2[[BIAS, BIAS + 32]] = 1
    headones = np.zeros((NH, HC, HPC, SLOTS), np.float32)
    for h in range(NH):
        headones[h, h // HPC, h % HPC] = 1
    sel = np.zeros((P, 2 * NS, P), np.float32)
    for r in range(2 * NS):
        for first in (0, 64, 96):
            sel[first + r, r] = 1
    return np.eye(P, dtype=np.float32), mask8, iota, tri, own, own * weight[:, None], tri8, ones2, headones.reshape(NH, HC, -1), sel


def chunked(w):
    return np.ascontiguousarray(w.reshape(2, P, -1).transpose(1, 0, 2))


def kernel(**inputs):
    import concourse.bacc as bacc
    from concourse.bass_utils import run_bass_kernel_spmd
    import ml_dtypes

    g = {k: np.asarray(v) for k, v in inputs.items()}
    at, xa, ff = ({k[len(p):]: v for k, v in g.items() if k.startswith(p)} for p in ("L0_attn_", "L0_xattn_", "L0_ffn_"))
    ident, mask8, iota, tri, own, weight, tri8, ones2, headones, sel = constants()
    x = g["x"].reshape(TOK, H)

    def flat(v):
        return chunked(v).reshape(P, -1)

    rows_of = list(range(DR, DR + 2 * NS))
    xp = np.zeros((P, H), np.float32)
    xp[0:32] = xa["x_proj_w"][rows_of]
    xp[32:32 + DR] = xa["x_proj_w"][0:DR]
    xp[64:96] = xa["x_proj_w"][rows_of]
    xp[96:128] = xa["x_proj_w"][rows_of]
    pkA = np.concatenate([xa["in_proj_w"].T, flat(xa["conv_w"]), flat(xa["conv_b"]), flat(xp.T), flat(xa["dt_proj_b"]),
                          flat(xa["A_log"]), flat(xa["D"])], 1)
    pkC = np.concatenate([ident, np.repeat(chunked(at["Wi"]), P, 2).reshape(P, -1), flat(at["bq"]),
                          np.broadcast_to(at["bi"].reshape(1, 1), (P, 1)), mask8, iota, tri, own, weight, tri8, ones2], 1)
    eb, rb = np.zeros((64, E * H), np.float32), np.zeros((64, E), np.float32)
    eb[0] = eb[32] = ff["expert_b"].reshape(-1)
    rb[0] = rb[32] = ff["router_b"]
    arrays = dict(
        ctxT=g["ctx_1024"].reshape(TOK, DC).T, pkA=pkA, dtpT=xa["dt_proj_w"].T, pkC=pkC,
        xT=chunked(x.T), x=x.reshape(NT, P, H).transpose(1, 0, 2), wq=chunked(at["Wq"]), wk=chunked(at["Wk"]),
        wv=chunked(at["Wv"]), wo=chunked(at["Wo"]), rows=np.stack([at["bk"], at["bv"]])[None], headones=headones,
        sel=sel.astype(ml_dtypes.bfloat16), bo=np.broadcast_to(at["bo"], (P, H)), ob=np.broadcast_to(ff["out_b"], (P, H)),
        ew=ff["expert_w"].reshape(E, HC, P, H).transpose(2, 1, 0, 3).reshape(P, HC, E * H), rw=chunked(ff["router_w"]),
        ow=chunked(ff["out_w"]), eb=eb, rb=rb)
    nc = bacc.Bacc("TRN2", target_bir_lowering=False, num_devices=1, dynamic_dma_scratch_size=1024)
    feed, args = {}, []
    for name, v in arrays.items():
        v = np.ascontiguousarray(v)
        feed["in_" + name] = v
        args.append(nc.dram_tensor("in_" + name, v.shape, mybir.dt.from_np(v.dtype), kind="ExternalInput").ap())
    out = nc.dram_tensor("out", (B, S, H), F32, kind="ExternalOutput").ap()
    decoder_layer(nc, *args, out)
    r = run_bass_kernel_spmd(nc, [feed], core_ids=[0])
    return r.results[0]["out"]
```

```python
from contextlib import ExitStack

import numpy as np

import concourse.bass as bass
from concourse import mybir

F32 = mybir.dt.float32
F32R = mybir.dt.float32r
BF16 = mybir.dt.bfloat16
ALU = mybir.AluOpType
ACT = mybir.ActivationFunctionType
AX = mybir.AxisListType

P = 128
B, S, H = 4, 256, 256
DC = 128
TOK = B * S
NT = TOK // P
HC = H // P
NH, HD = 16, 16
HPC = P // HD
TIDX = max(1, int(S * 0.2))
MINTOK = 32
SLOTS = 52
PAIRS = NH // 2
SC = 2 * SLOTS
NS, TAPS, DR = 16, 4, 8
E = 8
HALF = TOK // 2
HT = NT // 2
NPAIR = NS // 2
ITER = 2 * NPAIR
EPS = 1e-5
MOE0 = NPAIR + 3
PER_ITER = 2
UNITS = HT * E // 2
INLOOP = (ITER - MOE0) * PER_ITER
BIAS = 64

A_INP, A_CW, A_CB, A_XP, A_DTB, A_AL, A_D, A_END = np.cumsum([0, H, 2 * TAPS, 2, 2 * P, 2, 2 * NS, 2]).tolist()
C_ID, C_WI, C_BQ, C_BI, C_M8, C_IOTA, C_TRI, C_VM, C_VD, C_TR8, C_ON2, C_END = np.cumsum(
    [0, P, 2 * P, 2, 1, HPC, SLOTS, 2 * S, 2, 2, E * E, P]).tolist()


def decoder_layer(nc, ctxT, pkA, dtpT, pkC, xT, x, wq, wk, wv, wo, rows, headones, sel, bo, ob, ew, rw, ow, eb, rb, out):
    with ExitStack() as ctx:
        def sb(name, shape, dt=F32):
            return ctx.enter_context(nc.sbuf_tensor(name, shape, dt))

        def psum(name, shape):
            return ctx.enter_context(nc.psum_tensor(name, shape, F32))

        def sem(name):
            return ctx.enter_context(nc.semaphore(name))

        psS = psum("psS", [P, 4, 512])
        psB = psum("psB", [P, 512])
        psA = psum("psA", [P, 3, 512])

        s_ctxT = sb("s_ctxT", [P, TOK])
        imp = s_ctxT
        a = sb("s_pkA", [P, A_END])
        c = sb("s_pkC", [P, C_END])
        s_xT = sb("s_xT", [P, HC, TOK])
        ew_in = [s_xT[:, q, :] for q in range(2)]
        s_eb = s_xT[BIAS:P, :, :].rearrange("p m t -> p (m t)")
        ge = s_xT[:, :, :].rearrange("p m (h t) -> p (m h) t", h=2)
        s_x = sb("s_x", [P, NT, H])
        xb, zt, x2b = s_x, s_x, s_x
        s_wq = sb("s_wq", [P, HC, H])
        s_ow = s_wq
        s_wk = sb("s_wk", [P, HC, H])
        s_wv = sb("s_wv", [P, HC, H])
        s_wo = sb("s_wo", [P, HC, H])
        cmb, y3 = s_wk, s_wv
        ho_eb = sb("ho_eb", [P, E * H], F32R)
        ho_r = ho_eb[0:NH, 0:NH * SLOTS].rearrange("p (m s) -> p m s", m=HC)
        eb_st = ho_eb[BIAS:P, :]
        s_sel = sb("s_sel", [P, 2 * NS, P], BF16)
        s_bo = sb("s_bo", [P, H])
        s_ob = sb("s_ob", [P, H])
        ew_hi = sb("ew_hi", [P, HC, E * H], F32R)
        ew_lo = sb("ew_lo", [P, HC, E * H], F32R)
        s_rw = sb("s_rw", [P, HC, E])
        rw_hi = sb("rw_hi", [P, HC, E], F32R)
        rw_lo = sb("rw_lo", [P, HC, E], F32R)
        s_rb = sb("s_rb", [P, E])[BIAS:P, :]
        rb_st = sb("rb_st", [P, E], F32R)[BIAS:P, :]
        ones2 = c[BIAS:P, C_ON2:C_ON2 + P]
        ones2r = sb("ones2r", [P, P], F32R)[BIAS:P, :]

        ident = c[:, C_ID:C_ID + P]

        cwh = sb("cwh", [P, 2 * TAPS + 2])
        aneg = sb("aneg", [P, 2 * NS])
        aexp = sb("aexp", [P, 2 * NS])
        diagD = sb("diagD", [P, 2, P])
        xc = sb("xc", [P, 2, TOK])
        th = sb("th", [P, 2, TOK])
        spm, spe = xc, th
        ysum, yg = xc[:, 0, :].rearrange("p (e l) -> p e l", e=2), xc[:, 1, :].rearrange("p (e l) -> p e l", e=2)
        xs = th[:, :, 0:B * SC].rearrange("p k (b d s) -> p k b d s", b=B, d=2)
        occ = th[0:1, 0, B * SC:2 * B * SC].rearrange("p (b d s) -> p b d s", b=B, d=2)
        u = sb("u", [P, 2, TOK])
        stack = sb("stack", [P, TOK], BF16)
        delta = sb("delta", [P, 2, TOK])
        du = sb("du", [P, 2, TOK])
        dA = sb("dA", [P, 2, 2, 2, S])
        dBu = sb("dBu", [P, 2, TOK])
        Bb = sb("Bb", [P, 2, TOK])
        hs = sb("hs", [P, 2, TOK])
        psm = sb("psm", [P, 2, 512])
        r1 = dtl = psm[:, :, :].rearrange("p e l -> p (e l)")

        impc = sb("impc", [P, NT])
        junk = sb("junk", [P, S])
        cge = sb("cge", [P, NT])
        gtc = sb("gtc", [P, NT])
        eqc = sb("eqc", [P, NT])
        rank = sb("rank", [P, NT])
        kept = sb("kept", [P, NT])
        kep2 = sb("kep2", [P, NT])
        rk = sb("rk", [P, NT])
        onehot = sb("onehot", [P, NT, SLOTS])
        onescol = sb("onescol", [P, 1])
        QT = sb("QT", [P, HC, TOK])
        bdK = sb("bdK", [P, HC * B, HPC, SLOTS])
        Vbd = sb("Vbd", [SC, B * PAIRS, 2, HD + 1])
        mx = sb("mx", [P, NH])
        mTn = sb("mTn", [NH, P], F32R)
        Pm = sb("Pm", [P, PAIRS, SC])
        s_dtpT = Pm[:, 0:3, :].rearrange("p j s -> p (j s)")[:, 0:H]
        s_ho = Pm[0:NH, :, :].rearrange("p (m j) s -> p m (j s)", m=HC)
        PT = sb("PT", [SC, PAIRS, P])
        s_rows = PT[0:1, 0:4, :].rearrange("p (i j) t -> p i (j t)", i=2)
        rden = sb("rden", [P, NH])
        On = junk
        OT = sb("OT", [P, HC, P])
        x1 = sb("x1", [P, NT, H])
        x2, fin = x1, x1
        st = sb("st", [P, 6])
        mv1, mv2, mv3 = (sb(f"mv{i}", [P, NT, 2]) for i in (1, 2, 3))
        ve1, ve2, ve3 = (sb(f"ve{i}", [P, NT]) for i in (1, 2, 3))
        rs1, rs2, rs3 = (sb(f"rs{i}", [P, NT]) for i in (1, 2, 3))
        mhalf = sb("mhalf", [P, NT])

        x2h = sb("x2h", [P, HT, HC, P], F32R)
        x2l = sb("x2l", [P, HT, HC, P], F32R)
        lg = sb("lg", [P, HT, E])
        cmp1 = imp[:, 0:HT * E * E].rearrange("p (t i j) -> p t i j", t=HT, i=E)
        cmp2 = imp[:, 512:512 + HT * E * E].rearrange("p (t i j) -> p t i j", t=HT, i=E)
        rk8 = sb("rk8", [P, HT, E])
        lm = sb("lm", [P, HT])
        ls = sb("ls", [P, HT, E])
        le = sb("le", [P, HT, E])
        gs = sb("gs", [P, HT])
        gr = sb("gr", [P, HT])
        gates = sb("gates", [P, NT, E])
        cT = OT

        names = ["ctxT", "pkA", "dtpT", "pkC", "xT", "x", "wq", "wk", "wv", "wo", "rows", "ho", "sel", "bo", "ob",
                 "rw", "rb", "ow", "eb"]
        L = {n: sem("ld_" + n) for n in names}
        inproj_mm, xc_ok, th_ok, u_ok, xdbl_mm = sem("inproj_mm"), sem("xc_ok"), sem("th_ok"), sem("u_ok"), sem("xdbl_mm")
        part1_ok, dtl_ok, rest_ok, part2_ok, bc_ok = (sem(n) for n in ("part1_ok", "dtl_ok", "rest_ok", "part2_ok", "bc_ok"))
        dt_mm, spm_ok, spe_ok, spl_ok, delta_ok, du_ok = (sem(n) for n in ("dt_mm", "spm_ok", "spe_ok", "spl_ok", "delta_ok", "du_ok"))
        aexp_ok, aneg_ok, diag_ok, prep_ok = (sem(n) for n in ("aexp_ok", "aneg_ok", "diag_ok", "prep_ok"))
        imp_mm, imp_ok, impc_mm, onehot_ok, qt_mm, qt_ok = (sem(n) for n in ("imp_mm", "imp_ok", "impc_mm", "onehot_ok", "qt_mm", "qt_ok"))
        xsel_mm, xs_ok, kt_mm, v_mm, bdk_ok, vbd_ok, ho_ok = (sem(n) for n in ("xsel_mm", "xs_ok", "kt_mm", "v_mm", "bdk_ok", "vbd_ok", "ho_ok"))
        score_mm, max_ok, mT_mm, mTn_ok, shift_mm, probs_ok, pT_mm, pT_ok, av_mm, on_ok, oT_mm, oT_ok, wo_mm = (
            sem(n) for n in ("score_mm", "max_ok", "mT_mm", "mTn_ok", "shift_mm", "probs_ok", "pT_mm", "pT_ok", "av_mm",
                             "on_ok", "oT_mm", "oT_ok", "wo_mm"))
        xb_ok, y1_ok, mv1_ok, rs1_ok, x1_ok, zt_ok, z_ok = (sem(n) for n in ("xb_ok", "y1_ok", "mv1_ok", "rs1_ok", "x1_ok", "zt_ok", "z_ok"))
        b_mm, bb_ok, c_mm, dA_ok, dBu_ok, scan_ok, prod_ok, psm_ok, sum_mm = (
            sem(n) for n in ("b_mm", "bb_ok", "c_mm", "dA_ok", "dBu_ok", "scan_ok", "prod_ok", "psm_ok", "sum_mm"))
        ysum_ok, yg_ok, yT_mm, y2_ok, rs2_ok, x2_ok, x2T_mm, x2h_ok, x2l_ok, x2b_ok = (
            sem(n) for n in ("ysum_ok", "yg_ok", "yT_mm", "y2_ok", "rs2_ok", "x2_ok", "x2T_mm", "x2h_ok", "x2l_ok", "x2b_ok"))
        hi_ok, lo_ok, rt_mm, lg_ok, ls_ok, le_ok, gate_ok = (sem(n) for n in ("hi_ok", "lo_ok", "rt_mm", "lg_ok", "ls_ok", "le_ok", "gate_ok"))
        ex_mm, ge_ok, mix_ok, cT_mm, cT_ok, ow_mm, y3_ok, rs3_ok, fin_ok = (
            sem(n) for n in ("ex_mm", "ge_ok", "mix_ok", "cT_mm", "cT_ok", "ow_mm", "y3_ok", "rs3_ok", "fin_ok"))
        mv2_ok, mv3_ok, ewh_ok, ewl_ok, ebh_ok, ebl_ok, top_ok = (
            sem(n) for n in ("mv2_ok", "mv3_ok", "ewh_ok", "ewl_ok", "ebh_ok", "ebl_ok", "top_ok"))
        ew_ld = [sem(f"ld_ew{q}") for q in range(4)]
        dve_step, pool_step, stored = sem("dve_step"), sem("pool_step"), sem("stored")

        X4 = [psS[:, 2 * e:2 * e + 2, :].rearrange("p n (b l) -> p (n b) l", b=2) for e in range(2)]
        yps = [psS[:, e, :] for e in range(2)]

        def turned(t):
            return (psA if t < HT else psS)[:, (t % HT) // 2, (t % 2) * H:(t % 2 + 1) * H]

        def pair_end(t):
            return t - t % 2 + 2

        def logits(hb):
            return psA[:, 2, 0:HT * E] if hb == 0 else psS[:, 2, 0:HT * E]

        def expert_bank(i):
            return psA[:, i % 2, :] if i < UNITS else (psS[:, 3, :], psA[:, 0, :], psA[:, 1, :], psS[:, 2, :])[i % 4]

        cps = psS[:, 2:4, :]
        out_t = out.rearrange("b (t p) h -> (b t) p h", p=P)

        block = ctx.enter_context(nc.Block())

        @block.sync
        def _(sp):
            for dst, src, n in ((a[:], pkA, "pkA"), (s_ctxT[:], ctxT, "ctxT"), (s_xT[:], xT, "xT"),
                                (s_dtpT[32:32 + DR, :], dtpT, "dtpT"), (s_x[:], x, "x"), (s_sel[:], sel, "sel"),
                                (s_wk[:], wk, "wk"), (s_wv[:], wv, "wv"), (s_wo[:], wo, "wo")):
                sp.dma_start(dst, src).then_inc(L[n], 16)
            sp.wait_ge(qt_mm, 4)
            sp.dma_start(s_ow[:], ow).then_inc(L["ow"], 16)
            for q in range(4):
                if q >= 2:
                    sp.wait_ge(ewl_ok, q - 1)
                sp.dma_start(ew_in[q % 2], ew[:, q // 2, (q % 2) * TOK:(q % 2 + 1) * TOK]).then_inc(ew_ld[q], 16)
            sp.wait_ge(ewl_ok, 4)
            sp.dma_start(s_eb, eb).then_inc(L["eb"], 16)
            for t in range(NT):
                sp.wait_ge(fin_ok, t + 1)
                sp.dma_start(out_t[t], fin[:, t, :]).then_inc(stored, 16)
            sp.wait_ge(stored, 16 * NT)

        @block.tensor
        def _(pe):
            def in_proj(e):
                for n in range(2):
                    mm = pe.matmul(psS[:, 2 * e + n, :], a[:, A_INP + e * P:A_INP + (e + 1) * P],
                                   s_ctxT[:, n * 512:(n + 1) * 512], start=True, stop=True)
                mm.then_inc(inproj_mm, 1)

            def importance(n):
                dst = psB[:, :] if n == 0 else psA[:, 0, :]
                for k in range(HC):
                    mm = pe.matmul(dst, c[:, C_WI + k * P:C_WI + (k + 1) * P], s_xT[:, k, n * 512:(n + 1) * 512],
                                   start=k == 0, stop=k == HC - 1)
                mm.then_inc(imp_mm, 1)

            def queries(i):
                m, n = i // 2, i % 2
                if i >= 2:
                    pe.wait_ge(qt_ok, i - 1)
                if i == 1:
                    pe.wait_ge(imp_ok, 2)
                for k in range(HC):
                    mm = pe.matmul(psA[:, 2 if n == 0 else 0, :], s_wq[:, k, m * P:(m + 1) * P],
                                   s_xT[:, k, n * 512:(n + 1) * 512], start=k == 0, stop=k == HC - 1)
                mm.then_inc(qt_mm, 1)

            def x_proj(n):
                for e in range(2):
                    mm = pe.matmul(psS[:, n, :], a[:, A_XP + e * P:A_XP + (e + 1) * P], u[:, e, n * 512:(n + 1) * 512],
                                   start=e == 0, stop=e == 1)
                mm.then_inc(xdbl_mm, 1)

            def delta_proj(e):
                for n in range(2):
                    bank = 2 + n if e == 0 else n
                    mm = pe.matmul(psS[:, bank, :], s_dtpT[32:32 + DR, e * P:(e + 1) * P],
                                   dtl[32:32 + DR, n * 512:(n + 1) * 512], start=True, stop=True)
                mm.then_inc(dt_mm, 1)

            def bcast_b(k, j):
                hb, n = k // NPAIR, 2 * (k % NPAIR) + j
                if 2 * k + j >= 1:
                    pe.wait_ge(bb_ok, 2 * k + j)
                pe.matmul(psB[:, :], s_sel[:, n, :], stack[:, hb * 512:(hb + 1) * 512],
                          start=True, stop=True).then_inc(b_mm, 1)

            def bcast_c(k):
                hb, p = k // NPAIR, k % NPAIR
                if k >= 1:
                    pe.wait_ge(prod_ok, 2 * k)
                for j in range(2):
                    mm = pe.matmul(psS[:, 2 + j, :], s_sel[:, NS + 2 * p + j, :], stack[:, hb * 512:(hb + 1) * 512],
                                   start=True, stop=True)
                mm.then_inc(c_mm, 1)

            def skip_sum(hb):
                for e in range(2):
                    if hb == 1:
                        pe.wait_ge(ysum_ok, e + 1)
                    pe.matmul(yps[e], diagD[:, e, :], u[:, e, hb * 512:(hb + 1) * 512], start=True, stop=False)

            def state_sum(k, e):
                pe.wait_ge(psm_ok, 2 * k + e + 1)
                pe.matmul(yps[e], ident, psm[:, e, :], start=False, stop=k % NPAIR == NPAIR - 1).then_inc(sum_mm, 1)

            def scores(un):
                b, t = un // 2, un
                if un >= 1:
                    pe.wait_ge(pT_ok, un)
                for m in range(HC):
                    mm = pe.matmul(psA[:, m, 0:HPC * SLOTS], QT[:, m, t * P:(t + 1) * P],
                                   bdK[:, m * B + b, :, :], start=True, stop=True)
                mm.then_inc(score_mm, 1)

            def max_turn(un):
                pe.wait_ge(max_ok, un + 1)
                if un >= 2:
                    pe.wait_ge(oT_ok, un - 1)
                pe.transpose(psA[0:NH, 2, 0:P], mx[:, :], ident).then_inc(mT_mm, 1)

            def shift(un):
                pe.wait_ge(mTn_ok, un + 1)
                for m in range(HC):
                    mm = pe.matmul(psA[:, m, 0:HPC * SLOTS], mTn[:, :], ho_r[:, m, :], start=False, stop=True,
                                   skip_group_check=True)
                mm.then_inc(shift_mm, 1)

            def probs_turn(un):
                pe.wait_ge(probs_ok, un + 1)
                for j in range(PAIRS):
                    mm = pe.transpose(psA[0:SC, j // 4, (j % 4) * P:(j % 4 + 1) * P], Pm[:, j, :], ident)
                mm.then_inc(pT_mm, 1)

            def mix_values(un):
                pe.wait_ge(pT_ok, un + 1)
                if un >= 1:
                    pe.wait_ge(oT_ok, un)
                    pe.wait_ge(y1_ok, un)
                for j in range(PAIRS):
                    mm = pe.matmul(psA[:, 2, P + 34 * j:P + 34 * (j + 1)], PT[:, j, :],
                                   Vbd[:, (un // 2) * PAIRS + j, :, :], start=True, stop=True)
                mm.then_inc(av_mm, 1)

            def out_turn(un):
                pe.wait_ge(on_ok, un + 1)
                for m in range(HC):
                    mm = pe.transpose(psA[:, 2, m * P:(m + 1) * P], On[:, m * P:(m + 1) * P], ident)
                mm.then_inc(oT_mm, 1)

            def out_proj(un):
                pe.wait_ge(oT_ok, un + 1)
                for m in range(HC):
                    mm = pe.matmul(psA[:, 2, 256:512], OT[:, m, :], s_wo[:, m, :], start=m == 0, stop=m == HC - 1)
                mm.then_inc(wo_mm, 1)

            pe.wait_ge(L["pkA"], 16)
            pe.wait_ge(L["ctxT"], 16)
            in_proj(0)
            in_proj(1)
            pe.wait_ge(L["pkC"], 16)
            pe.wait_ge(L["xT"], 16)
            importance(0)
            importance(1)
            pe.wait_ge(L["wq"], 16)
            queries(0)
            pe.wait_ge(imp_ok, 2)
            for t in range(NT):
                mm = pe.transpose(psA[:, 1, t:t + 1], imp[0:1, t * P:(t + 1) * P], ident[0:1, 0:1])
            mm.then_inc(impc_mm, 1)
            queries(1)
            queries(2)
            pe.wait_ge(u_ok, 2)
            x_proj(0)
            x_proj(1)
            queries(3)
            pe.wait_ge(L["dtpT"], 16)
            pe.wait_ge(dtl_ok, 2)
            delta_proj(0)
            pe.wait_ge(rest_ok, 2)
            delta_proj(1)
            pe.wait_ge(onehot_ok, 1)
            pe.wait_ge(prep_ok, 1)
            pe.wait_ge(L["x"], 16)
            pe.wait_ge(qt_ok, 4)
            for k in range(HC):
                for b in range(B):
                    for q in range(2):
                        t = 2 * b + q
                        pe.matmul(psA[:, 1, (k * B + b) * SLOTS:(k * B + b + 1) * SLOTS], s_x[:, t, k * P:(k + 1) * P],
                                  onehot[:, t, :], start=q == 0, stop=q == 1)
            for b in range(B):
                for q in range(2):
                    mm = pe.matmul(psA[0:1, 0, b * SLOTS:(b + 1) * SLOTS], onescol[:, :], onehot[:, 2 * b + q, :],
                                   start=q == 0, stop=q == 1)
            mm.then_inc(xsel_mm, 1)
            pe.wait_ge(xs_ok, 2)
            pe.wait_ge(L["wk"], 16)
            pe.wait_ge(L["rows"], 16)
            for m in range(HC):
                dst = psA[:, 2, m * B * SLOTS:(m + 1) * B * SLOTS]
                for k in range(HC):
                    pe.matmul(dst, s_wk[:, k, m * P:(m + 1) * P], xs[:, k, :, 0, :], start=k == 0, stop=False)
                mm = pe.matmul(dst, s_rows[0:1, 0, m * P:(m + 1) * P], occ[:, :, 0, :], start=False, stop=True)
            mm.then_inc(kt_mm, 1)
            pe.wait_ge(L["wv"], 16)
            for b in range(B):
                dst = psA[0:SC, b // 2, (b % 2) * H:(b % 2 + 1) * H]
                for k in range(HC):
                    pe.matmul(dst, xs[:, k, b, :, :], s_wv[:, k, :], start=k == 0, stop=False)
                mm = pe.matmul(dst, occ[:, b, :, :], s_rows[0:1, 1, :], start=False, stop=True)
            mm.then_inc(v_mm, 1)
            pe.wait_ge(bc_ok, 2)
            pe.wait_ge(L["sel"], 16)
            pe.wait_ge(imp_ok, 2)
            bcast_b(0, 0)
            bcast_b(0, 1)
            pe.wait_ge(delta_ok, 2)
            bcast_c(0)
            pe.wait_ge(diag_ok, 1)
            skip_sum(0)
            bcast_b(1, 0)
            bcast_b(1, 1)

            def y_turns(hb):
                pe.wait_ge(yg_ok, 2 * (hb + 1))
                if hb == 0:
                    pe.wait_ge(pT_ok, NT)
                else:
                    pe.wait_ge(ysum_ok, 4)
                for t in range(hb * HT, (hb + 1) * HT):
                    b, q = t // 2, t % 2
                    for e in range(2):
                        mm = pe.transpose(turned(t)[:, e * P:(e + 1) * P],
                                          yg[:, e, (b % 2) * S + q * P:(b % 2) * S + (q + 1) * P], ident)
                    mm.then_inc(yT_mm, 1)

            def x2_turn(t):
                pe.wait_ge(x2_ok, t + 1)
                pe.wait_ge(y2_ok, pair_end(t))
                for m in range(HC):
                    mm = pe.transpose(turned(t)[:, m * P:(m + 1) * P], x2[:, t, m * P:(m + 1) * P], ident)
                mm.then_inc(x2T_mm, 1)

            def router(t):
                hb = t // HT
                if t == 0:
                    pe.wait_ge(hi_ok, 1)
                    pe.wait_ge(lo_ok, 1)
                    pe.wait_ge(y1_ok, NT)
                if t == HT:
                    pe.wait_ge(prod_ok, 2 * ITER)
                pe.wait_ge(x2h_ok, t + 1)
                pe.wait_ge(x2l_ok, t + 1)
                dst = logits(hb)[:, (t % HT) * E:(t % HT + 1) * E]
                pe.matmul(dst, ones2r[:, :], rb_st[:, :], start=True, stop=False)
                i = 0
                for m in range(HC):
                    for xx in (x2h, x2l):
                        for ww in (rw_hi, rw_lo):
                            i += 1
                            mm = pe.matmul(dst, xx[:, t % HT, m, :], ww[:, m, :], start=False, stop=i == 4 * HC)
                mm.then_inc(rt_mm, 1)

            def expert_pair(i):
                t, q = i // (E // 2), i % (E // 2)
                if i == 0:
                    pe.wait_ge(ebl_ok, 2)
                    pe.wait_ge(x2l_ok, HT)
                elif 2 <= i < UNITS:
                    pe.wait_ge(ge_ok, i - 1)
                elif UNITS <= i < UNITS + 4:
                    pe.wait_ge(ge_ok, UNITS)
                    pe.wait_ge(lg_ok, 2)
                elif i >= UNITS + 4:
                    pe.wait_ge(ge_ok, i - 3)
                cols = slice(q * 512, (q + 1) * 512)
                dst = expert_bank(i)
                pe.matmul(dst, ones2r[:, :], eb_st[:, cols], start=True, stop=False)
                for m in range(HC):
                    pe.matmul(dst, x2h[:, t % HT, m, :], ew_hi[:, m, cols], start=False, stop=False)
                    pe.matmul(dst, x2h[:, t % HT, m, :], ew_lo[:, m, cols], start=False, stop=False)
                    mm = pe.matmul(dst, x2l[:, t % HT, m, :], ew_hi[:, m, cols], start=False, stop=m == HC - 1)
                mm.then_inc(ex_mm, 1)

            def mixed_turn(t):
                pe.wait_ge(mix_ok, (E // 2) * (t + 1))
                if t == 0:
                    pe.wait_ge(lg_ok, 1)
                if t >= 1:
                    pe.wait_ge(y3_ok, t)
                for m in range(HC):
                    mm = pe.transpose(psA[:, 2, m * P:(m + 1) * P], cmb[:, t % 2, m * P:(m + 1) * P], ident)
                mm.then_inc(cT_mm, 1)

            def mixed_proj(t):
                if t == 0:
                    pe.wait_ge(L["ow"], 16)
                pe.wait_ge(cT_ok, t + 1)
                if t >= 1:
                    pe.wait_ge(y3_ok, t)
                for m in range(HC):
                    mm = pe.matmul(psA[:, 2, H:2 * H], cT[:, m, :], s_ow[:, m, :], start=m == 0, stop=m == HC - 1)
                mm.then_inc(ow_mm, 1)

            pe.wait_ge(bdk_ok, 1)
            pe.wait_ge(vbd_ok, 1)
            pe.wait_ge(ho_ok, 1)
            for k in range(ITER):
                if k < NT:
                    scores(k)
                if 1 <= k <= NT:
                    mix_values(k - 1)
                if k >= 1:
                    state_sum(k - 1, 0)
                if k < NT:
                    max_turn(k)
                if k >= 1:
                    state_sum(k - 1, 1)
                if k + 2 < ITER:
                    bcast_b(k + 2, 0)
                if k < NT:
                    shift(k)
                if k >= MOE0:
                    expert_pair(PER_ITER * (k - MOE0))
                if k == NPAIR + 2:
                    for t in range(HT):
                        x2_turn(t)
                if k + 2 < ITER:
                    bcast_b(k + 2, 1)
                if 1 <= k <= NT:
                    out_turn(k - 1)
                if k == NPAIR:
                    skip_sum(1)
                if k == NPAIR + 1:
                    y_turns(0)
                if k < NT:
                    probs_turn(k)
                if k == 1:
                    pe.wait_ge(L["wo"], 16)
                if k == MOE0 + 3:
                    mixed_turn(0)
                if k >= MOE0:
                    expert_pair(PER_ITER * (k - MOE0) + 1)
                if k + 1 < ITER:
                    bcast_c(k + 1)
                if 1 <= k <= NT:
                    out_proj(k - 1)
                if k == MOE0 + 3:
                    mixed_proj(0)
                if k == NPAIR + 2:
                    for t in range(HT):
                        router(t)
            state_sum(ITER - 1, 0)
            state_sum(ITER - 1, 1)
            expert_pair(10)
            expert_pair(11)
            mixed_turn(1)
            y_turns(1)
            expert_pair(12)
            mixed_proj(1)
            expert_pair(13)
            x2_turn(4)
            x2_turn(5)
            expert_pair(14)
            expert_pair(15)
            mixed_turn(2)
            x2_turn(6)
            x2_turn(7)
            mixed_proj(2)
            for t in range(HT, NT):
                router(t)
            for t in range(HT, NT):
                for q in range(E // 2):
                    expert_pair(t * (E // 2) + q)
                    if q == 1:
                        mixed_turn(t - 1)
                    if q == 2:
                        mixed_proj(t - 1)
            mixed_turn(NT - 1)
            mixed_proj(NT - 1)

        @block.scalar
        def _(act):
            for dst, src, n in ((c[:], pkC, "pkC"), (s_wq[:], wq, "wq"), (s_rows, rows, "rows"), (s_ho, headones, "ho"),
                                (s_bo[:], bo, "bo"), (s_rw[:], rw, "rw"), (s_rb, rb, "rb"), (s_ob[:], ob, "ob")):
                act.dma_start(dst, src).then_inc(L[n], 16)

            def exps(k, e):
                hb, p = k // NPAIR, k % NPAIR
                act.wait_ge(aneg_ok, 1)
                if k >= 1:
                    act.wait_ge(scan_ok, 2 * (k - 1) + e + 1)
                for j in range(2):
                    o = dA[:, e, j, :, 1:]
                    i = delta[:, e, hb * 512:(hb + 1) * 512].rearrange("p (b l) -> p b l", b=2)[:, :, 1:]
                    x_ = act.activation(o, i, ACT.Exp, scale=aneg[:, e * NS + 2 * p + j:e * NS + 2 * p + j + 1])
                x_.then_inc(dA_ok, 1)

            def copy_b(k, j):
                act.wait_ge(b_mm, 2 * k + j + 1)
                if k >= 2:
                    act.wait_ge(dBu_ok, 2 * (k - 1))
                act.copy(Bb[:, k % 2, j * 512:(j + 1) * 512], psB[:, :]).then_inc(bb_ok, 1)

            act.wait_ge(prep_ok, 1)
            act.wait_ge(L["pkA"], 16)
            act.activation(aexp[:, :], a[:, A_AL:A_AL + 2 * NS], ACT.Exp).then_inc(aexp_ok, 1)
            act.wait_ge(L["pkC"], 16)
            for n in range(2):
                act.wait_ge(imp_mm, n + 1)
                act.activation(imp[:, n * 512:(n + 1) * 512], psB[:, :] if n == 0 else psA[:, 0, :], ACT.Identity,
                               bias=c[:, C_BI:C_BI + 1]).then_inc(imp_ok, 1)

            def copy_q(i):
                m, n = i // 2, i % 2
                act.wait_ge(qt_mm, i + 1)
                act.activation(QT[:, m, n * 512:(n + 1) * 512], psA[:, 2 if n == 0 else 0, :], ACT.Identity,
                               bias=c[:, C_BQ + m:C_BQ + m + 1]).then_inc(qt_ok, 1)

            copy_q(0)
            for e in range(2):
                act.wait_ge(xc_ok, e + 1)
                act.activation(th[:, e, :], xc[:, e, :], ACT.Tanh).then_inc(th_ok, 1)
                copy_q(1 + e)
            for n in range(2):
                act.wait_ge(xdbl_mm, n + 1)
                cols = slice(n * 512, (n + 1) * 512)
                act.copy(stack[:, cols], psS[:, n, :]).then_inc(part1_ok, 1)
                act.copy(dtl[32:32 + DR, cols], psS[32:32 + DR, n, :]).then_inc(dtl_ok, 1)
            for n in range(2):
                act.wait_ge(rest_ok, n + 1)
                cols = slice(n * 512, (n + 1) * 512)
                act.copy(stack[64:128, cols], r1[64:128, cols]).then_inc(part2_ok, 1)
            copy_q(3)
            for e in range(2):
                act.wait_ge(spm_ok, e + 1)
                act.activation(spe[:, e, :], spm[:, e, :], ACT.Exp).then_inc(spe_ok, 1)
            for e in range(2):
                act.wait_ge(spe_ok, e + 1)
                act.activation(spm[:, e, :], spe[:, e, :], ACT.Ln, bias=onescol[:, 0:1]).then_inc(spl_ok, 1)
            act.wait_ge(delta_ok, 1)
            exps(0, 0)
            act.wait_ge(xsel_mm, 1)
            act.wait_ge(spl_ok, 2)
            sel_in = psA[:, 1, 0:HC * B * SLOTS].rearrange("p (k b s) -> p k b s", k=HC, s=SLOTS)
            for d in range(2):
                act.copy(xs[:, :, :, d, :], sel_in)
                act.copy(occ[:, :, d, :], psA[0:1, 0, 0:B * SLOTS].rearrange("p (b s) -> p b s", s=SLOTS)).then_inc(xs_ok, 1)
            copy_b(0, 0)
            copy_b(0, 1)
            act.wait_ge(delta_ok, 2)
            exps(0, 1)
            act.wait_ge(L["ho"], 16)
            act.copy(ho_r[:, :, :], s_ho[:, :, :]).then_inc(ho_ok, 1)
            copy_b(1, 0)
            copy_b(1, 1)

            def weight_high(q):
                act.wait_ge(ew_ld[q], 16)
                act.copy(ew_hi[:, q // 2, (q % 2) * TOK:(q % 2 + 1) * TOK], ew_in[q % 2]).then_inc(ewh_ok, 1)

            def bias_high(q):
                if q == 0:
                    act.wait_ge(L["eb"], 16)
                act.copy(eb_st[:, q * TOK:(q + 1) * TOK], s_eb[:, q * TOK:(q + 1) * TOK]).then_inc(ebh_ok, 1)

            def router_high():
                act.wait_ge(L["rw"], 16)
                act.wait_ge(L["rb"], 16)
                act.copy(rw_hi[:, :, :], s_rw[:, :, :])
                act.copy(ones2r[:, :], ones2[:, :])
                act.copy(rb_st[:, :], s_rb[:, :]).then_inc(hi_ok, 1)

            def copy_sums(hb):
                for e in range(2):
                    act.wait_ge(sum_mm, 2 * (NPAIR * (hb + 1) - 1) + e + 1)
                    if hb == 1:
                        act.wait_ge(yg_ok, e + 1)
                    act.copy(ysum[:, e, :], yps[e]).then_inc(ysum_ok, 1)

            def gate_tanh(t):
                act.wait_ge(x1_ok, t + 1)
                act.activation(zt[:, t, :], x1[:, t, :], ACT.Tanh, scale=0.5).then_inc(zt_ok, 1)

            def x2_high(t):
                act.wait_ge(x2T_mm, pair_end(t))
                if t >= HT:
                    act.wait_ge(ex_mm, (E // 2) * (t - HT + 1))
                act.copy(x2h[:, t % HT, :, :].rearrange("p m t -> p (m t)"), turned(t)).then_inc(x2h_ok, 1)

            def gate_exp(hb):
                act.wait_ge(ls_ok, hb + 1)
                act.activation(le[:, :, :], ls[:, :, :], ACT.Exp).then_inc(le_ok, 1)

            def gelu(i):
                act.wait_ge(ex_mm, i + 1)
                if i >= 4:
                    act.wait_ge(mix_ok, i - 3)
                act.activation(ge[:, i % 4, :], expert_bank(i), ACT.Gelu_apprx_tanh).then_inc(ge_ok, 1)

            def copy_mixed(t):
                act.wait_ge(cT_mm, t + 1)
                if t >= 1:
                    act.wait_ge(ow_mm, t)
                act.copy(cT[:, :, :].rearrange("p m t -> p (m t)"), psA[:, 2, 0:H]).then_inc(cT_ok, 1)

            for k in range(ITER):
                if k + 1 < ITER:
                    exps(k + 1, 0)
                    exps(k + 1, 1)
                if k < NT:
                    act.wait_ge(mT_mm, k + 1)
                    if k >= 1:
                        act.wait_ge(shift_mm, k)
                    act.mul(mTn[:, :], psA[0:NH, 2, 0:P], -1.0).then_inc(mTn_ok, 1)
                if k == NPAIR:
                    copy_sums(0)
                if k + 2 < ITER:
                    copy_b(k + 2, 0)
                if k == MOE0:
                    gate_exp(0)
                if k == NPAIR + 2:
                    for t in range(HT):
                        x2_high(t)
                if k < NT:
                    act.wait_ge(shift_mm, k + 1)
                    if k >= 1:
                        act.wait_ge(pT_mm, k)
                    act.activation(Pm[:, :, :].rearrange("p (m j) s -> p m (j s)", m=HC), psA[:, 0:2, 0:HPC * SLOTS],
                                   ACT.Exp, scale=float(HD) ** -0.5).then_inc(probs_ok, 1)
                if k + 2 < ITER:
                    copy_b(k + 2, 1)
                if 1 <= k <= NT:
                    act.wait_ge(oT_mm, k)
                    if k >= 2:
                        act.wait_ge(wo_mm, k - 1)
                    act.copy(OT[:, :, :].rearrange("p m t -> p (m t)"), psA[:, 2, 0:256]).then_inc(oT_ok, 1)
                if k < NT:
                    act.wait_ge(pT_mm, k + 1)
                    if k >= 1:
                        act.wait_ge(av_mm, k)
                    act.copy(PT[:, :, :].rearrange("p (m j) s -> p m (j s)", m=2), psA[0:SC, 0:2, :]).then_inc(pT_ok, 1)
                if 2 <= k < NT + 2:
                    gate_tanh(k - 2)
                if 1 <= k < 5:
                    weight_high(k - 1)
                if k == 6:
                    router_high()
                if 7 <= k < 9:
                    bias_high(k - 7)
                if k == MOE0 + 3:
                    copy_mixed(0)
                if k == MOE0:
                    act.wait_ge(ebl_ok, 2)
                if k >= MOE0:
                    for j in range(PER_ITER):
                        gelu(PER_ITER * (k - MOE0) + j)
            copy_sums(1)
            gelu(10)
            gelu(11)
            copy_mixed(1)
            gelu(12)
            gelu(13)
            x2_high(4)
            x2_high(5)
            gelu(14)
            gelu(15)
            copy_mixed(2)
            x2_high(6)
            x2_high(7)
            gate_exp(1)
            for t in range(HT, NT):
                for q in range(E // 2):
                    gelu(t * (E // 2) + q)
                    if q == 2:
                        copy_mixed(t - 1)
            copy_mixed(NT - 1)

        @block.vector
        def _(dve):
            steps = [0]

            def link(ins):
                steps[0] += 1
                ins.then_inc(dve_step, 1)
                dve.wait_ge(dve_step, steps[0])

            def conv(e):
                dve.wait_ge(inproj_mm, e + 1)
                o = xc[:, e, :].rearrange("p (b l) -> p b l", b=B)
                link(dve.tensor_scalar(o, X4[e], cwh[:, e * TAPS + 3:e * TAPS + 4], cwh[:, 2 * TAPS + e:2 * TAPS + e + 1],
                                       ALU.mult, ALU.add))
                for d in range(1, TAPS):
                    i = dve.scalar_tensor_tensor(o[:, :, d:], X4[e][:, :, :S - d],
                                                 cwh[:, e * TAPS + 3 - d:e * TAPS + 4 - d], o[:, :, d:], ALU.mult, ALU.add)
                    if d < TAPS - 1:
                        link(i)
                i.then_inc(xc_ok, 1)

            def silu(e):
                dve.wait_ge(th_ok, e + 1)
                dve.scalar_tensor_tensor(u[:, e, :], th[:, e, :], 1.0, xc[:, e, :], ALU.add, ALU.mult).then_inc(u_ok, 1)

            def count(t):
                row, col = imp[:, (t // 2) * S:(t // 2 + 1) * S], impc[:, t:t + 1]
                link(dve.tensor_scalar(junk[:, :], row, col, None, ALU.is_ge, ALU.add, accum_out=cge[:, t:t + 1]))
                link(dve.tensor_scalar(junk[:, :], row, col, None, ALU.is_gt, ALU.add, accum_out=gtc[:, t:t + 1]))
                link(dve.scalar_tensor_tensor(junk[:, :], row, col, c[:, C_TRI + (t % 2) * S:C_TRI + (t % 2 + 1) * S],
                                              ALU.is_equal, ALU.mult, accum_out=eqc[:, t:t + 1]))

            def delta_in(e):
                return psS[:, 2 if e == 0 else 0:4 if e == 0 else 2, :].rearrange("p n l -> p (n l)")

            dve.wait_ge(L["pkA"], 16)
            link(dve.tensor_scalar(cwh[:, :], a[:, A_CW:A_CB + 2], 0.5, None, ALU.mult))
            conv(0)
            conv(1)
            silu(0)
            silu(1)
            dve.wait_ge(aexp_ok, 1)
            dve.tensor_scalar(aneg[:, :], aexp[:, :], -1.0, None, ALU.mult).then_inc(aneg_ok, 1)
            dve.wait_ge(L["pkC"], 16)
            for e in range(2):
                i = dve.tensor_scalar(diagD[:, e, :], ident, a[:, A_D + e:A_D + e + 1], None, ALU.mult)
            i.then_inc(diag_ok, 1)
            dve.wait_ge(impc_mm, 1)
            dve.wait_ge(imp_ok, 2)
            link(dve.tensor_copy(impc[:, :], psA[:, 1, 0:NT]))
            for t in range(4):
                count(t)
            for n in range(2):
                dve.wait_ge(part1_ok, n + 1)
                cols = slice(n * 512, (n + 1) * 512)
                dve.tensor_tensor(r1[64:128, cols], psS[64:128, n, :], stack[64:128, cols], ALU.subtract).then_inc(rest_ok, 1)
            for t in range(4, 5):
                count(t)
            for n in range(2):
                dve.wait_ge(part2_ok, n + 1)
                cols = slice(n * 512, (n + 1) * 512)
                dve.tensor_tensor(stack[96:128, cols], r1[96:128, cols], stack[96:128, cols], ALU.subtract).then_inc(bc_ok, 1)
            for e in range(2):
                dve.wait_ge(dt_mm, e + 1)
                dve.tensor_scalar(spm[:, e, :], delta_in(e), a[:, A_DTB + e:A_DTB + e + 1], 40.0, ALU.add,
                                  ALU.min).then_inc(spm_ok, 1)
            for t in range(5, NT):
                count(t)
            link(dve.tensor_tensor(rank[:, :], gtc[:, :], eqc[:, :], ALU.add))
            link(dve.tensor_scalar(kept[:, :], cge[:, :], float(TIDX), None, ALU.is_le))
            link(dve.tensor_scalar(kep2[:, :], rank[:, :], float(MINTOK), None, ALU.is_lt))
            link(dve.tensor_tensor(kept[:, :], kept[:, :], kep2[:, :], ALU.max))
            link(dve.tensor_scalar(kept[:, :], kept[:, :], -1000.0, 1000.0, ALU.mult, ALU.add))
            link(dve.tensor_tensor(rk[:, :], rank[:, :], kept[:, :], ALU.add))
            dve.tensor_tensor(onehot[:, :, :], c[:, C_IOTA:C_IOTA + SLOTS].unsqueeze(1).to_broadcast([P, NT, SLOTS]),
                              rk[:, :].unsqueeze(2).to_broadcast([P, NT, SLOTS]), ALU.is_equal).then_inc(onehot_ok, 1)
            for e in range(2):
                dve.wait_ge(spl_ok, e + 1)
                dve.scalar_tensor_tensor(delta[:, e, :], delta_in(e), a[:, A_DTB + e:A_DTB + e + 1], spm[:, e, :],
                                         ALU.add, ALU.max).then_inc(delta_ok, 1)
                dve.wait_ge(delta_ok, e + 1)
                dve.tensor_tensor(du[:, e, :], delta[:, e, :], u[:, e, :], ALU.mult).then_inc(du_ok, 1)

            def keys_values():
                dve.wait_ge(kt_mm, 1)
                dve.tensor_tensor(bdK[:, :, :, :],
                                  psA[:, 2, 0:HC * B * SLOTS].rearrange("p (g s) -> p g s", s=SLOTS).unsqueeze(2)
                                  .to_broadcast([P, HC * B, HPC, SLOTS]),
                                  c[:, C_M8:C_M8 + HPC].unsqueeze(1).unsqueeze(3).to_broadcast([P, HC * B, HPC, SLOTS]),
                                  ALU.mult).then_inc(bdk_ok, 1)
                dve.wait_ge(v_mm, 1)
                for g in range(2):
                    dve.tensor_tensor(Vbd[:, g * 2 * PAIRS:(g + 1) * 2 * PAIRS, :, 0:HD],
                                      psA[0:SC, g, :].rearrange("p (g h d) -> p g h d", h=2, d=HD),
                                      c[0:SC, C_VM:C_VM + 2].unsqueeze(1).unsqueeze(3).to_broadcast([SC, 2 * PAIRS, 2, HD]),
                                      ALU.mult)
                dve.tensor_copy(Vbd[:, :, :, HD:HD + 1],
                                c[0:SC, C_VD:C_VD + 2].unsqueeze(1).unsqueeze(3).to_broadcast([SC, B * PAIRS, 2, 1])
                                ).then_inc(vbd_ok, 1)

            def scan(k, e):
                dve.wait_ge(dA_ok, 2 * k + e + 1)
                dve.wait_ge(dBu_ok, 2 * k + e + 1)
                if k >= 1:
                    dve.wait_ge(psm_ok, 2 * (k - 1) + e + 1)
                dve.tensor_tensor_scan(hs[:, e, :], dA[:, e, :, :, :].rearrange("p j b l -> p (j b l)"), dBu[:, e, :],
                                       0.0, ALU.mult, ALU.add).then_inc(scan_ok, 1)

            def times_c(k, e):
                dve.wait_ge(c_mm, k + 1)
                dve.wait_ge(scan_ok, 2 * k + e + 1)
                dve.tensor_tensor(hs[:, e, :], hs[:, e, :], cps.rearrange("p n l -> p (n l)"), ALU.mult).then_inc(prod_ok, 1)

            def add_pair(k, e):
                dve.wait_ge(prod_ok, 2 * k + e + 1)
                if k >= 1:
                    dve.wait_ge(sum_mm, 2 * (k - 1) + e + 1)
                dve.tensor_tensor(psm[:, e, :], hs[:, e, 0:512], hs[:, e, 512:1024], ALU.add).then_inc(psm_ok, 1)

            def score_max(un):
                dve.wait_ge(score_mm, un + 1)
                if un >= 1:
                    dve.wait_ge(mT_mm, un)
                dve.tensor_reduce(mx[:, :].rearrange("p (m h) -> p m h", m=HC),
                                  psA[:, 0:2, 0:HPC * SLOTS].rearrange("p m (h s) -> p m h s", s=SLOTS), AX.X, ALU.max
                                  ).then_inc(max_ok, 1)

            def normalise(un):
                dve.wait_ge(av_mm, un + 1)
                if un >= 1:
                    dve.wait_ge(oT_mm, un)
                if un + 1 < NT:
                    dve.wait_ge(mTn_ok, un + 2)
                o = psA[:, 2, P:P + NH * (HD + 1)].rearrange("p (h d) -> p h d", d=HD + 1)
                link(dve.reciprocal(rden[:, :].unsqueeze(2), o[:, :, HD:HD + 1]))
                dve.tensor_tensor(On[:, :].rearrange("p (h d) -> p h d", d=HD), o[:, :, 0:HD],
                                  rden[:, :].unsqueeze(2).to_broadcast([P, NH, HD]), ALU.mult).then_inc(on_ok, 1)

            def moments(y, mv, done):
                link(dve.bn_stats(st[:, :], y))
                dve.bn_aggr(mv, st[:, :]).then_inc(done, 1)

            def residual1(t):
                dve.wait_ge(wo_mm, t + 1)
                dve.wait_ge(xb_ok, t + 1)
                dve.tensor_tensor(x1[:, t, :], psA[:, 2, 256:512], xb[:, t, :], ALU.add).then_inc(y1_ok, 1)
                dve.wait_ge(y1_ok, t + 1)
                moments(x1[:, t, :], mv1[:, t, :], mv1_ok)

            def norm1(t):
                dve.wait_ge(rs1_ok, t + 1)
                dve.tensor_scalar(x1[:, t, :], x1[:, t, :], mv1[:, t, 0:1], rs1[:, t:t + 1], ALU.subtract,
                                  ALU.mult).then_inc(x1_ok, 1)

            def gate_z(t):
                dve.wait_ge(zt_ok, t + 1)
                dve.scalar_tensor_tensor(zt[:, t, :], zt[:, t, :], 1.0, x1[:, t, :], ALU.add, ALU.mult).then_inc(z_ok, 1)

            def gated(hb, e):
                dve.wait_ge(ysum_ok, 2 * hb + e + 1)
                dve.wait_ge(z_ok, 4 * (hb + 1))
                if hb == 1:
                    dve.wait_ge(yT_mm, HT)
                dve.scalar_tensor_tensor(yg[:, e, :].rearrange("p (b l) -> p b l", b=2),
                                         ysum[:, e, :].rearrange("p (b l) -> p b l", b=2), 0.5,
                                         zt[:, :, :].rearrange("p (b e) l -> p b e l", e=2)[:, 2 * hb:2 * hb + 2, e, :],
                                         ALU.mult, ALU.mult).then_inc(yg_ok, 1)

            def residual2(t):
                dve.wait_ge(yT_mm, pair_end(t))
                dve.tensor_tensor(x2[:, t, :], turned(t), x1[:, t, :], ALU.add).then_inc(y2_ok, 1)
                dve.wait_ge(y2_ok, t + 1)
                moments(x2[:, t, :], mv2[:, t, :], mv2_ok)

            def norm2(t):
                dve.wait_ge(rs2_ok, t + 1)
                dve.tensor_scalar(x2[:, t, :], x2[:, t, :], mv2[:, t, 0:1], rs2[:, t:t + 1], ALU.subtract,
                                  ALU.mult).then_inc(x2_ok, 1)

            def x2_low(t):
                dve.wait_ge(x2h_ok, pair_end(t))
                dve.tensor_tensor(x2l[:, t % HT, :, :].rearrange("p m t -> p (m t)"), turned(t),
                                  x2h[:, t % HT, :, :].rearrange("p m t -> p (m t)").bitcast(F32), ALU.subtract
                                  ).then_inc(x2l_ok, 1)

            def gate_ranks(hb):
                dve.wait_ge(rt_mm, HT * (hb + 1))
                dve.tensor_copy(lg[:, :, :].rearrange("p t e -> p (t e)"), logits(hb)).then_inc(lg_ok, 1)
                dve.wait_ge(lg_ok, hb + 1)
                over = lg[:, :, :].unsqueeze(2).to_broadcast([P, HT, E, E])
                own = lg[:, :, :].unsqueeze(3).to_broadcast([P, HT, E, E])
                tri8 = c[:, C_TR8:C_TR8 + E * E].rearrange("p (i j) -> p i j", i=E).unsqueeze(1).to_broadcast([P, HT, E, E])
                link(dve.tensor_reduce(lm[:, :], lg[:, :, :], AX.X, ALU.max))
                dve.tensor_tensor(ls[:, :, :], lg[:, :, :], lm[:, :].unsqueeze(2).to_broadcast([P, HT, E]),
                                  ALU.subtract).then_inc(ls_ok, 1)
                dve.tensor_tensor(cmp1, over, own, ALU.is_gt)
                link(dve.tensor_tensor(cmp2, over, own, ALU.is_equal))
                link(dve.tensor_tensor(cmp2, cmp2, tri8, ALU.mult))
                link(dve.tensor_tensor(cmp1, cmp1, cmp2, ALU.add))
                link(dve.tensor_reduce(rk8[:, :, :], cmp1, AX.X, ALU.add))
                dve.tensor_scalar(rk8[:, :, :], rk8[:, :, :], 2.0, None, ALU.is_lt).then_inc(top_ok, 1)

            def gate_weights(hb):
                dve.wait_ge(le_ok, hb + 1)
                dve.wait_ge(top_ok, hb + 1)
                link(dve.tensor_tensor(le[:, :, :], le[:, :, :], rk8[:, :, :], ALU.mult))
                link(dve.tensor_reduce(gs[:, :], le[:, :, :], AX.X, ALU.add))
                link(dve.reciprocal(gr[:, :], gs[:, :]))
                link(dve.tensor_tensor(gates[:, hb * HT:(hb + 1) * HT, :], le[:, :, :],
                                       gr[:, :].unsqueeze(2).to_broadcast([P, HT, E]), ALU.mult))

            def mix(i):
                t, q = i // (E // 2), i % (E // 2)
                o = cmb[:, t % 2, :]
                if q == 0 and t >= 2:
                    dve.wait_ge(cT_mm, t - 1)
                dve.wait_ge(ge_ok, i + 1)
                for h in range(2):
                    x_ = 2 * q + h
                    g, src = gates[:, t, x_:x_ + 1], ge[:, i % 4, h * H:(h + 1) * H]
                    if x_ == 0:
                        link(dve.tensor_scalar(o, src, g, None, ALU.mult))
                    else:
                        ins = dve.scalar_tensor_tensor(o, src, g, o, ALU.mult, ALU.add)
                        if h == 0:
                            link(ins)
                ins.then_inc(mix_ok, 1)
                dve.wait_ge(mix_ok, i + 1)

            def residual3(t):
                dve.wait_ge(ow_mm, t + 1)
                dve.wait_ge(x2b_ok, t // HT + 1)
                dve.tensor_tensor(y3[:, t % 2, :], psA[:, 2, H:2 * H], x2b[:, t, :], ALU.add).then_inc(y3_ok, 1)
                dve.wait_ge(y3_ok, t + 1)
                moments(y3[:, t % 2, :], mv3[:, t, :], mv3_ok)

            def norm3(t):
                dve.wait_ge(rs3_ok, t + 1)
                dve.tensor_scalar(fin[:, t, :], y3[:, t % 2, :], mv3[:, t, 0:1], rs3[:, t:t + 1], ALU.subtract,
                                  ALU.mult).then_inc(fin_ok, 1)

            keys_values()
            for k in range(ITER):
                scan(k, 0)
                scan(k, 1)
                if k < NT:
                    score_max(k)
                if k == NPAIR + 2:
                    for t in range(HT):
                        norm2(t)
                if k == MOE0:
                    gate_ranks(0)
                if k > MOE0:
                    mix(PER_ITER * (k - MOE0 - 1))
                times_c(k, 0)
                if 1 <= k <= NT:
                    normalise(k - 1)
                times_c(k, 1)
                if 2 <= k < NT + 2:
                    norm1(k - 2)
                if 3 <= k < NT + 3:
                    gate_z(k - 3)
                if k > MOE0:
                    mix(PER_ITER * (k - MOE0 - 1) + 1)
                add_pair(k, 0)
                add_pair(k, 1)
                if 1 <= k <= NT:
                    residual1(k - 1)
                if k == NPAIR:
                    gated(0, 0)
                    gated(0, 1)
                if k == NPAIR + 1:
                    for t in range(HT):
                        residual2(t)
                if k == NPAIR + 2:
                    for t in range(HT):
                        x2_low(t)
                if k == MOE0:
                    gate_weights(0)
                if k == MOE0 + 4:
                    residual3(0)
            mix(8)
            mix(9)
            norm3(0)
            gated(1, 0)
            gated(1, 1)
            mix(10)
            mix(11)
            for t in range(HT, NT):
                residual2(t)
            residual3(1)
            mix(12)
            for t in range(HT, NT):
                norm2(t)
            mix(13)
            norm3(1)
            x2_low(4)
            x2_low(5)
            mix(14)
            mix(15)
            x2_low(6)
            x2_low(7)
            residual3(2)
            gate_ranks(1)
            norm3(2)
            gate_weights(1)
            for t in range(HT, NT):
                for q in range(E // 2):
                    mix(t * (E // 2) + q)
                    if q == 2:
                        residual3(t - 1)
                norm3(t - 1)
            residual3(NT - 1)
            norm3(NT - 1)

        @block.gpsimd
        def _(pool):
            steps = [0]

            def link(ins):
                steps[0] += 1
                ins.then_inc(pool_step, 1)
                pool.wait_ge(pool_step, steps[0])

            def rstd(mv, ve, rs, t, done, ready, n=1):
                pool.wait_ge(ready, t + n)
                link(pool.tensor_scalar(ve[:, t:t + n], mv[:, t:t + n, 1], EPS, 1.0, ALU.add, ALU.mult))
                pool.tensor_tensor(rs[:, t:t + n], ve[:, t:t + n], mhalf[:, t:t + n], ALU.pow).then_inc(done, n)

            def add_bias(hb):
                pool.wait_ge(x2_ok, HT * (hb + 1))
                pool.wait_ge(L["ob"], 16)
                pool.tensor_tensor(x2b[:, hb * HT:(hb + 1) * HT, :], x2[:, hb * HT:(hb + 1) * HT, :],
                                   s_ob[:, :].unsqueeze(1).to_broadcast([P, HT, H]), ALU.add).then_inc(x2b_ok, 1)

            for e in range(2):
                pool.memset(dA[:, e, :, :, 0:1], 0.0)
            pool.memset(mhalf[:, :], -0.5)
            pool.memset(onescol[:, :], 1.0).then_inc(prep_ok, 1)
            pool.wait_ge(prep_ok, 1)
            pool.wait_ge(L["bo"], 16)
            for k in range(ITER):
                hb = k // NPAIR
                for e in range(2):
                    pool.wait_ge(du_ok, e + 1)
                    pool.wait_ge(bb_ok, 2 * k + 2)
                    if k >= 1:
                        pool.wait_ge(scan_ok, 2 * (k - 1) + e + 1)
                    pool.tensor_tensor(dBu[:, e, :].rearrange("p (j l) -> p j l", j=2),
                                       Bb[:, k % 2, :].rearrange("p (j l) -> p j l", j=2),
                                       du[:, e, hb * 512:(hb + 1) * 512].unsqueeze(1).to_broadcast([P, 2, 512]),
                                       ALU.mult).then_inc(dBu_ok, 1)
                if k < NT:
                    pool.wait_ge(xsel_mm, 1)
                    pool.tensor_tensor(xb[:, k, :], s_x[:, k, :], s_bo[:, :], ALU.add).then_inc(xb_ok, 1)
                if 2 <= k < NT + 2:
                    rstd(mv1, ve1, rs1, k - 2, rs1_ok, mv1_ok)
                if 3 <= k < 7:
                    q = k - 3
                    pool.wait_ge(ewh_ok, q + 1)
                    part = slice((q % 2) * TOK, (q % 2 + 1) * TOK)
                    pool.tensor_tensor(ew_lo[:, q // 2, part], ew_in[q % 2], ew_hi[:, q // 2, part].bitcast(F32),
                                       ALU.subtract).then_inc(ewl_ok, 1)
                if k == NPAIR:
                    pool.wait_ge(hi_ok, 1)
                    link(pool.tensor_tensor(rw_lo[:, :, :], s_rw[:, :, :], rw_hi[:, :, :].bitcast(F32), ALU.subtract))
                    pool.tensor_tensor(rb_st[32:33, :], s_rb[32:33, :], rb_st[32:33, :].bitcast(F32), ALU.subtract).then_inc(lo_ok, 1)
                    pool.wait_ge(lo_ok, 1)
                if k in (NPAIR + 1, NPAIR + 3):
                    q = (k - NPAIR) // 2
                    pool.wait_ge(ebh_ok, q + 1)
                    pool.wait_ge(dBu_ok, 2 * k + 2)
                    pool.wait_ge(rs1_ok, NT)
                    part = slice(q * TOK, (q + 1) * TOK)
                    pool.tensor_tensor(eb_st[32:33, part], s_eb[32:33, part], eb_st[32:33, part].bitcast(F32),
                                       ALU.subtract).then_inc(ebl_ok, 1)
                    pool.wait_ge(ebl_ok, q + 1)
                if k == NPAIR + 2:
                    rstd(mv2, ve2, rs2, 0, rs2_ok, mv2_ok, HT)
                if k == MOE0 + 1:
                    add_bias(0)
            rstd(mv3, ve3, rs3, 0, rs3_ok, mv3_ok)
            rstd(mv2, ve2, rs2, HT, rs2_ok, mv2_ok, HT)
            rstd(mv3, ve3, rs3, 1, rs3_ok, mv3_ok)
            rstd(mv3, ve3, rs3, 2, rs3_ok, mv3_ok)
            add_bias(1)
            for t in range(3, NT):
                rstd(mv3, ve3, rs3, t, rs3_ok, mv3_ok)


def constants():
    p = np.arange(P)
    j = np.arange(S)
    tri = np.concatenate([(j[None, :] < (q * P + p)[:, None]) for q in range(2)], 1).astype(np.float32)
    mask8 = (p[:, None] // HD == np.arange(HPC)[None, :]).astype(np.float32)
    iota = np.broadcast_to(np.arange(SLOTS, dtype=np.float32), (P, SLOTS))
    own = (p[:, None] // SLOTS == np.arange(2)[None, :]).astype(np.float32)
    weight = np.where(p % SLOTS == SLOTS - 1, S - SLOTS + 1, 1).astype(np.float32)
    i8 = np.arange(E)
    tri8 = np.broadcast_to((i8[None, :] < i8[:, None]).astype(np.float32).reshape(1, -1), (P, E * E))
    ones2 = np.zeros((P, P), np.float32)
    ones2[[BIAS, BIAS + 32]] = 1
    headones = np.zeros((NH, HC, HPC, SLOTS), np.float32)
    for h in range(NH):
        headones[h, h // HPC, h % HPC] = 1
    sel = np.zeros((P, 2 * NS, P), np.float32)
    for r in range(2 * NS):
        for first in (0, 64, 96):
            sel[first + r, r] = 1
    return np.eye(P, dtype=np.float32), mask8, iota, tri, own, own * weight[:, None], tri8, ones2, headones.reshape(NH, HC, -1), sel


def chunked(w):
    return np.ascontiguousarray(w.reshape(2, P, -1).transpose(1, 0, 2))


def kernel(**inputs):
    import concourse.bacc as bacc
    from concourse.bass_utils import run_bass_kernel_spmd
    import ml_dtypes

    g = {k: np.asarray(v) for k, v in inputs.items()}
    at, xa, ff = ({k[len(p):]: v for k, v in g.items() if k.startswith(p)} for p in ("L0_attn_", "L0_xattn_", "L0_ffn_"))
    ident, mask8, iota, tri, own, weight, tri8, ones2, headones, sel = constants()
    x = g["x"].reshape(TOK, H)

    def flat(v):
        return chunked(v).reshape(P, -1)

    rows_of = list(range(DR, DR + 2 * NS))
    xp = np.zeros((P, H), np.float32)
    xp[0:32] = xa["x_proj_w"][rows_of]
    xp[32:32 + DR] = xa["x_proj_w"][0:DR]
    xp[64:96] = xa["x_proj_w"][rows_of]
    xp[96:128] = xa["x_proj_w"][rows_of]
    pkA = np.concatenate([xa["in_proj_w"].T, flat(xa["conv_w"]), flat(xa["conv_b"]), flat(xp.T), flat(xa["dt_proj_b"]),
                          flat(xa["A_log"]), flat(xa["D"])], 1)
    pkC = np.concatenate([ident, np.repeat(chunked(at["Wi"]), P, 2).reshape(P, -1), flat(at["bq"]),
                          np.broadcast_to(at["bi"].reshape(1, 1), (P, 1)), mask8, iota, tri, own, weight, tri8, ones2], 1)
    eb, rb = np.zeros((64, E * H), np.float32), np.zeros((64, E), np.float32)
    eb[0] = eb[32] = ff["expert_b"].reshape(-1)
    rb[0] = rb[32] = ff["router_b"]
    arrays = dict(
        ctxT=g["ctx_1024"].reshape(TOK, DC).T, pkA=pkA, dtpT=xa["dt_proj_w"].T, pkC=pkC,
        xT=chunked(x.T), x=x.reshape(NT, P, H).transpose(1, 0, 2), wq=chunked(at["Wq"]), wk=chunked(at["Wk"]),
        wv=chunked(at["Wv"]), wo=chunked(at["Wo"]), rows=np.stack([at["bk"], at["bv"]])[None], headones=headones,
        sel=sel.astype(ml_dtypes.bfloat16), bo=np.broadcast_to(at["bo"], (P, H)), ob=np.broadcast_to(ff["out_b"], (P, H)),
        ew=ff["expert_w"].reshape(E, HC, P, H).transpose(2, 1, 0, 3).reshape(P, HC, E * H), rw=chunked(ff["router_w"]),
        ow=chunked(ff["out_w"]), eb=eb, rb=rb)
    nc = bacc.Bacc("TRN2", target_bir_lowering=False, num_devices=1, dynamic_dma_scratch_size=1024)
    feed, args = {}, []
    for name, v in arrays.items():
        v = np.ascontiguousarray(v)
        feed["in_" + name] = v
        args.append(nc.dram_tensor("in_" + name, v.shape, mybir.dt.from_np(v.dtype), kind="ExternalInput").ap())
    out = nc.dram_tensor("out", (B, S, H), F32, kind="ExternalOutput").ap()
    decoder_layer(nc, *args, out)
    r = run_bass_kernel_spmd(nc, [feed], core_ids=[0])
    return r.results[0]["out"]
```

```python
from contextlib import ExitStack

import numpy as np

import concourse.bass as bass
from concourse import mybir

F32 = mybir.dt.float32
F32R = mybir.dt.float32r
BF16 = mybir.dt.bfloat16
ALU = mybir.AluOpType
ACT = mybir.ActivationFunctionType
AX = mybir.AxisListType

P = 128
B, S, H = 4, 256, 256
DC = 128
TOK = B * S
NT = TOK // P
HC = H // P
NH, HD = 16, 16
HPC = P // HD
TIDX = max(1, int(S * 0.2))
MINTOK = 32
SLOTS = 52
PAIRS = NH // 2
UNUSED = 12
SC = 2 * SLOTS
NS, TAPS, DR = 16, 4, 8
E = 8
HALF = TOK // 2
HT = NT // 2
NPAIR = NS // 2
ITER = 2 * NPAIR
EPS = 1e-5
LAG = 2
MOE0 = NPAIR + LAG + 2
PER_ITER = 2
DIRECT = MOE0
UNITS = HT * E // 2
LOOPED = PER_ITER * (ITER - MOE0)
TURN_AFTER = {17: 2, 20: 3, 22: 4, 25: 5, 29: 6}
PROJ_AFTER = {18: 2, 21: 3, 23: 4, 26: 5, 30: 6}
RESIDUAL_AFTER = {17: 2, 20: 3, 23: 4, 26: 5, 30: 6}
NORM_AFTER = {18: 2, 22: 3, 24: 4, 27: 5, 31: 6}
BIAS = 64

A_INP, A_CW, A_CB, A_XP, A_DTB, A_AL, A_D, A_END = np.cumsum([0, H, 2 * TAPS, 2, 2 * P, 2, 2 * NS, 2]).tolist()
C_ID, C_WI, C_BQ, C_BI, C_M8, C_IOTA, C_TRI, C_VM, C_VD, C_TR8, C_ON2, C_END = np.cumsum(
    [0, P, 2 * P, 2, 1, HPC, SLOTS, 2 * S, 2, 2, E * E, P]).tolist()


def decoder_layer(nc, ctxT, pkA, dtpT, pkC, xT, x, wq, wk, wv, wo, rows, headones, sel, bo, ob, ew, rw, ow, eb, rb, out):
    with ExitStack() as ctx:
        def sb(name, shape, dt=F32):
            return ctx.enter_context(nc.sbuf_tensor(name, shape, dt))

        def psum(name, shape):
            return ctx.enter_context(nc.psum_tensor(name, shape, F32))

        def sem(name):
            return ctx.enter_context(nc.semaphore(name))

        psS = psum("psS", [P, 4, 512])
        psB = psum("psB", [P, 512])
        psA = psum("psA", [P, 3, 512])

        s_ctxT = sb("s_ctxT", [P, TOK])
        imp = s_ctxT
        a = sb("s_pkA", [P, A_END])
        c = sb("s_pkC", [P, C_END])
        s_xT = sb("s_xT", [P, HC, TOK])
        ge = s_xT[:, :, :].rearrange("p m (h t) -> p (m h) t", h=2)
        s_x = sb("s_x", [P, NT, H])
        xb, zt, x2b = s_x, s_x, s_x
        s_wq = sb("s_wq", [P, HC, H])
        s_ow = s_wq
        s_wk = sb("s_wk", [P, HC, H])
        s_wv = sb("s_wv", [P, HC, H])
        s_wo = sb("s_wo", [P, HC, H])
        cmb, y3 = s_wk, s_wv
        ho_eb = sb("ho_eb", [P, E * H], F32R)
        ho_r = ho_eb[0:NH, 0:NH * SLOTS].rearrange("p (m s) -> p m s", m=HC)
        eb_st = ho_eb[BIAS:P, :]
        s_sel = sb("s_sel", [P, 2 * NS, P], BF16)
        s_bo = sb("s_bo", [P, H])
        s_ob = sb("s_ob", [P, H])
        ew_hi = sb("ew_hi", [P, HC, E * H], F32R)
        ew_lo = sb("ew_lo", [P, HC, E * H], F32R)
        s_rw = sb("s_rw", [P, HC, E])
        rw_hi = sb("rw_hi", [P, HC, E], F32R)
        rw_lo = sb("rw_lo", [P, HC, E], F32R)
        s_rb = sb("s_rb", [E, 1])
        ones2 = c[BIAS:P, C_ON2:C_ON2 + P]
        ones2r = sb("ones2r", [P, P], F32R)[BIAS:P, :]

        ident = c[:, C_ID:C_ID + P]

        cwh = sb("cwh", [P, 2 * TAPS + 2])
        aneg = sb("aneg", [P, 2 * NS])
        aexp = sb("aexp", [P, 2 * NS])
        diagD = sb("diagD", [P, 2, P])
        xc = sb("xc", [P, 2, TOK])
        th = sb("th", [P, 2, TOK])
        spm, spe = xc, th
        ysum, yg = xc[:, 0, :].rearrange("p (e l) -> p e l", e=2), xc[:, 1, :].rearrange("p (e l) -> p e l", e=2)
        xs = th[:, :, 0:B * SC].rearrange("p k (b d s) -> p k b d s", b=B, d=2)
        occ = th[0:1, 0, B * SC:2 * B * SC].rearrange("p (b d s) -> p b d s", b=B, d=2)
        u = sb("u", [P, 2, TOK])
        stack = sb("stack", [P, TOK], BF16)
        delta = sb("delta", [P, 2, TOK])
        du = sb("du", [P, 2, TOK])
        dA = sb("dA", [P, 2, 2, 2, S])
        dBu = sb("dBu", [P, 2, TOK])
        Bb = sb("Bb", [P, 2, TOK])
        hs = sb("hs", [P, 2, TOK])
        ew_in = [buf[:, q, :] for buf in (hs, dBu) for q in range(2)]
        s_eb = du[BIAS:P, :, :].rearrange("p e t -> p (e t)")
        psm = sb("psm", [P, 2, 512])
        r1 = dtl = psm[:, :, :].rearrange("p e l -> p (e l)")

        impc = sb("impc", [P, NT])
        junk = sb("junk", [P, S])
        cge = sb("cge", [P, NT])
        gtc = sb("gtc", [P, NT])
        eqc = sb("eqc", [P, NT])
        rank = sb("rank", [P, NT])
        kept = sb("kept", [P, NT])
        kep2 = sb("kep2", [P, NT])
        rk = sb("rk", [P, NT])
        onehot = sb("onehot", [P, NT, SLOTS])
        onescol = sb("onescol", [P, 1])
        QT = sb("QT", [P, HC, TOK])
        lgT = QT[0:E, 0, 0:HALF]
        bdK = sb("bdK", [P, HC * B, HPC, SLOTS])
        unused = bdK[:, :, :, :].rearrange("p g h s -> p (g h s)")
        Vbd = sb("Vbd", [SC, B * PAIRS, 2, HD + 1])
        mx = sb("mx", [P, NH])
        mTn = sb("mTn", [NH, P], F32R)
        Pm = sb("Pm", [P, PAIRS, SC])
        s_dtpT = Pm[:, 0:3, :].rearrange("p j s -> p (j s)")[:, 0:H]
        s_ho = Pm[0:NH, :, :].rearrange("p (m j) s -> p m (j s)", m=HC)
        PT = sb("PT", [SC, PAIRS, P])
        s_rows = PT[0:1, 0:4, :].rearrange("p (i j) t -> p i (j t)", i=2)
        rden = sb("rden", [P, NH])
        On = junk
        OT = sb("OT", [P, HC, P])
        x1 = th[:, :, :].rearrange("p e (t h) -> p (e t) h", h=H)
        x2, fin = x1, x1
        st = sb("st", [P, 6])
        st2 = sb("st2", [P, HT, 6])
        mv1, mv2, mv3 = (sb(f"mv{i}", [P, NT, 2]) for i in (1, 2, 3))
        ve1, ve2, ve3 = (sb(f"ve{i}", [P, NT]) for i in (1, 2, 3))
        rs1, rs2, rs3 = (sb(f"rs{i}", [P, NT]) for i in (1, 2, 3))
        mhalf = sb("mhalf", [P, NT])
        nm1 = sb("nm1", [P, NT])

        x2h = [sb(f"x2h{i}", [P, HT, HC, P], F32R) for i in range(2)]
        x2l = [sb(f"x2l{i}", [P, HT, HC, P], F32R) for i in range(2)]
        lg = sb("lg", [P, HT, E])
        cmp1 = imp[:, 0:HT * E * E].rearrange("p (t i j) -> p t i j", t=HT, i=E)
        cmp2 = imp[:, 512:512 + HT * E * E].rearrange("p (t i j) -> p t i j", t=HT, i=E)
        rk8 = sb("rk8", [P, HT, E])
        lm = sb("lm", [P, HT])
        ls = sb("ls", [P, HT, E])
        le = sb("le", [P, HT, E])
        gs = sb("gs", [P, HT])
        gr = sb("gr", [P, HT])
        gates = sb("gates", [P, NT, E])
        cT = OT

        names = ["ctxT", "pkA", "dtpT", "pkC", "xT", "x", "wq", "wk", "wv", "wo", "rows", "ho", "sel", "bo", "ob",
                 "rw", "rb", "ow", "eb"]
        L = {n: sem("ld_" + n) for n in names}
        inproj_mm, xc_ok, th_ok, u_ok, xdbl_mm = sem("inproj_mm"), sem("xc_ok"), sem("th_ok"), sem("u_ok"), sem("xdbl_mm")
        part1_ok, dtl_ok, rest_ok, part2_ok, bc_ok = (sem(n) for n in ("part1_ok", "dtl_ok", "rest_ok", "part2_ok", "bc_ok"))
        dt_mm, spm_ok, spe_ok, spl_ok, delta_ok, du_ok = (sem(n) for n in ("dt_mm", "spm_ok", "spe_ok", "spl_ok", "delta_ok", "du_ok"))
        aexp_ok, aneg_ok, diag_ok, prep_ok = (sem(n) for n in ("aexp_ok", "aneg_ok", "diag_ok", "prep_ok"))
        imp_mm, imp_ok, impc_mm, onehot_ok, qt_mm, qt_ok = (sem(n) for n in ("imp_mm", "imp_ok", "impc_mm", "onehot_ok", "qt_mm", "qt_ok"))
        xsel_mm, xs_ok, kt_mm, v_mm, bdk_ok, vbd_ok, ho_ok = (sem(n) for n in ("xsel_mm", "xs_ok", "kt_mm", "v_mm", "bdk_ok", "vbd_ok", "ho_ok"))
        score_mm, max_ok, mT_mm, mTn_ok, shift_mm, probs_ok, pT_mm, pT_ok, av_mm, on_ok, oT_mm, oT_ok, wo_mm = (
            sem(n) for n in ("score_mm", "max_ok", "mT_mm", "mTn_ok", "shift_mm", "probs_ok", "pT_mm", "pT_ok", "av_mm",
                             "on_ok", "oT_mm", "oT_ok", "wo_mm"))
        xb_ok, y1_ok, mv1_ok, rs1_ok, x1_ok, zt_ok, z_ok = (sem(n) for n in ("xb_ok", "y1_ok", "mv1_ok", "rs1_ok", "x1_ok", "zt_ok", "z_ok"))
        b_mm, bb_ok, c_mm, dA_ok, dBu_ok, scan_ok, prod_ok, sum_mm = (
            sem(n) for n in ("b_mm", "bb_ok", "c_mm", "dA_ok", "dBu_ok", "scan_ok", "prod_ok", "sum_mm"))
        ysum_ok, yg_ok, yT_mm, y2_ok, rs2_ok, x2_ok, x2T_mm, x2h_ok, x2l_ok, x2b_ok = (
            sem(n) for n in ("ysum_ok", "yg_ok", "yT_mm", "y2_ok", "rs2_ok", "x2_ok", "x2T_mm", "x2h_ok", "x2l_ok", "x2b_ok"))
        hi_ok, lo_ok, rt_mm, lg_ok, ls_ok, le_ok = (sem(n) for n in ("hi_ok", "lo_ok", "rt_mm", "lg_ok", "ls_ok", "le_ok"))
        ex_mm, ge_ok, mix_ok, cT_mm, cT_ok, ow_mm, y3_ok, rs3_ok, fin_ok = (
            sem(n) for n in ("ex_mm", "ge_ok", "mix_ok", "cT_mm", "cT_ok", "ow_mm", "y3_ok", "rs3_ok", "fin_ok"))
        mv2_ok, mv3_ok, ewh_ok, ewl_ok, ebh_ok, ebl_ok, top_ok = (
            sem(n) for n in ("mv2_ok", "mv3_ok", "ewh_ok", "ewl_ok", "ebh_ok", "ebl_ok", "top_ok"))
        lgT_ok, lgt_mm, nm_ok, count_ok = (sem(n) for n in ("lgT_ok", "lgt_mm", "nm_ok", "count_ok"))
        stats_ok, stats2_ok = sem("stats_ok"), sem("stats2_ok")
        psm_ok = [sem(f"psm{e}_ok") for e in range(2)]
        ew_ld = [sem(f"ld_ew{q}") for q in range(4)]
        dve_step, pool_step, stored = sem("dve_step"), sem("pool_step"), sem("stored")

        X4 = [psS[:, 2 * e:2 * e + 2, :].rearrange("p n (b l) -> p (n b) l", b=2) for e in range(2)]
        yps = [psS[:, e, :] for e in range(2)]

        def turned(t):
            return (psA if t < HT else psS)[:, (t % HT) // 2, (t % 2) * H:(t % 2 + 1) * H]

        def pair_end(t):
            return t - t % 2 + 2

        def router_bank(hb):
            return psA[:, 2, :] if hb == 0 else psS[:, 2, :]

        def expert_bank(i):
            return psA[:, i % 2, :] if i < UNITS else (psS[:, 3, :], psA[:, 0, :], psA[:, 1, :], psS[:, 2, :])[i % 4]

        cps = psS[:, 2:4, :]
        out_t = out.rearrange("b (t p) h -> (b t) p h", p=P)

        block = ctx.enter_context(nc.Block())

        @block.sync
        def _(sp):
            for dst, src, n in ((a[:], pkA, "pkA"), (s_ctxT[:], ctxT, "ctxT"), (s_xT[:], xT, "xT"),
                                (s_dtpT[32:32 + DR, :], dtpT, "dtpT"), (s_sel[:], sel, "sel")):
                sp.dma_start(dst, src).then_inc(L[n], 16)
            for q in range(4):
                sp.dma_start(ew_in[q], ew[:, q // 2, (q % 2) * TOK:(q % 2 + 1) * TOK]).then_inc(ew_ld[q], 16)
            for dst, src, n in ((s_eb, eb, "eb"), (s_x[:], x, "x"), (s_wk[:], wk, "wk"), (s_wv[:], wv, "wv"),
                                (s_wo[:], wo, "wo")):
                sp.dma_start(dst, src).then_inc(L[n], 16)
            sp.wait_ge(qt_mm, 4)
            sp.dma_start(s_ow[:], ow).then_inc(L["ow"], 16)
            for t in range(NT):
                sp.wait_ge(fin_ok, t + 1)
                sp.dma_start(out_t[t], fin[:, t, :]).then_inc(stored, 16)
            sp.wait_ge(stored, 16 * NT)

        @block.tensor
        def _(pe):
            def in_proj(e):
                for n in range(2):
                    mm = pe.matmul(psS[:, 2 * e + n, :], a[:, A_INP + e * P:A_INP + (e + 1) * P],
                                   s_ctxT[:, n * 512:(n + 1) * 512], start=True, stop=True)
                mm.then_inc(inproj_mm, 1)

            def importance(n):
                dst = psB[:, :] if n == 0 else psA[:, 0, :]
                for k in range(HC):
                    mm = pe.matmul(dst, c[:, C_WI + k * P:C_WI + (k + 1) * P], s_xT[:, k, n * 512:(n + 1) * 512],
                                   start=k == 0, stop=k == HC - 1)
                mm.then_inc(imp_mm, 1)

            def queries(i):
                m, n = i // 2, i % 2
                if i >= 2:
                    pe.wait_ge(qt_ok, i - 1)
                if i == 1:
                    pe.wait_ge(imp_ok, 2)
                for k in range(HC):
                    mm = pe.matmul(psA[:, 2 if n == 0 else 0, :], s_wq[:, k, m * P:(m + 1) * P],
                                   s_xT[:, k, n * 512:(n + 1) * 512], start=k == 0, stop=k == HC - 1)
                mm.then_inc(qt_mm, 1)

            def x_proj(e):
                pe.wait_ge(u_ok, e + 1)
                if e == 0:
                    pe.wait_ge(xc_ok, 1)
                for n in range(2):
                    mm = pe.matmul(psS[:, n, :], a[:, A_XP + e * P:A_XP + (e + 1) * P], u[:, e, n * 512:(n + 1) * 512],
                                   start=e == 0, stop=e == 1)
                    if e == 1:
                        mm.then_inc(xdbl_mm, 1)

            def delta_proj(e):
                for n in range(2):
                    bank = 2 + n if e == 0 else n
                    mm = pe.matmul(psS[:, bank, :], s_dtpT[32:32 + DR, e * P:(e + 1) * P],
                                   dtl[32:32 + DR, n * 512:(n + 1) * 512], start=True, stop=True)
                mm.then_inc(dt_mm, 1)

            def bcast_b(k, j):
                hb, n = k // NPAIR, 2 * (k % NPAIR) + j
                if 2 * k + j >= 1:
                    pe.wait_ge(bb_ok, 2 * k + j)
                pe.matmul(psB[:, :], s_sel[:, n, :], stack[:, hb * 512:(hb + 1) * 512],
                          start=True, stop=True).then_inc(b_mm, 1)

            def bcast_c(k):
                hb, p = k // NPAIR, k % NPAIR
                if k >= 1:
                    pe.wait_ge(prod_ok, 2 * k)
                for j in range(2):
                    mm = pe.matmul(psS[:, 2 + j, :], s_sel[:, NS + 2 * p + j, :], stack[:, hb * 512:(hb + 1) * 512],
                                   start=True, stop=True)
                mm.then_inc(c_mm, 1)

            def skip_sum(hb, e):
                if hb == 1:
                    pe.wait_ge(ysum_ok, e + 1)
                pe.matmul(yps[e], diagD[:, e, :], u[:, e, hb * 512:(hb + 1) * 512], start=True, stop=False)

            def state_sum(k, e):
                if k == NPAIR and e == 1:
                    skip_sum(1, 1)
                pe.wait_ge(psm_ok[e], k + 1)
                pe.matmul(yps[e], ident, psm[:, e, :], start=False, stop=k % NPAIR == NPAIR - 1).then_inc(sum_mm, 1)

            def direct_sum(k):
                pe.wait_ge(prod_ok, 2 * k + 1)
                for j in range(2):
                    mm = pe.matmul(yps[0], ident, hs[:, 0, j * 512:(j + 1) * 512], start=False,
                                   stop=k % NPAIR == NPAIR - 1 and j == 1)
                mm.then_inc(sum_mm, 1)

            def scores(un):
                b, t = un // 2, un
                if un >= 1:
                    pe.wait_ge(pT_ok, un)
                for m in range(HC):
                    mm = pe.matmul(psA[:, m, 0:HPC * SLOTS], QT[:, m, t * P:(t + 1) * P],
                                   bdK[:, m * B + b, :, :], start=True, stop=True)
                mm.then_inc(score_mm, 1)

            def max_turn(un):
                pe.wait_ge(max_ok, un + 1)
                if un >= 2:
                    pe.wait_ge(oT_ok, un - 1)
                pe.transpose(psA[0:NH, 2, 0:P], mx[:, :], ident).then_inc(mT_mm, 1)

            def shift(un):
                pe.wait_ge(mTn_ok, un + 1)
                for m in range(HC):
                    mm = pe.matmul(psA[:, m, 0:HPC * SLOTS], mTn[:, :], ho_r[:, m, :], start=False, stop=True,
                                   skip_group_check=True)
                mm.then_inc(shift_mm, 1)

            def probs_turn(un):
                pe.wait_ge(probs_ok, un + 1)
                for j in range(PAIRS):
                    mm = pe.transpose(psA[0:SC, j // 4, (j % 4) * P:(j % 4 + 1) * P], Pm[:, j, :], ident)
                mm.then_inc(pT_mm, 1)

            def mix_values(un):
                pe.wait_ge(pT_ok, un + 1)
                if un >= 1:
                    pe.wait_ge(oT_ok, un)
                    pe.wait_ge(y1_ok, un)
                for j in range(PAIRS):
                    mm = pe.matmul(psA[:, 2, P + 34 * j:P + 34 * (j + 1)], PT[:, j, :],
                                   Vbd[:, (un // 2) * PAIRS + j, :, :], start=True, stop=True)
                mm.then_inc(av_mm, 1)

            def out_turn(un):
                pe.wait_ge(on_ok, un + 1)
                for m in range(HC):
                    mm = pe.transpose(psA[:, 2, m * P:(m + 1) * P], On[:, m * P:(m + 1) * P], ident)
                mm.then_inc(oT_mm, 1)

            def out_proj(un):
                pe.wait_ge(oT_ok, un + 1)
                for m in range(HC):
                    mm = pe.matmul(psA[:, 2, 256:512], OT[:, m, :], s_wo[:, m, :], start=m == 0, stop=m == HC - 1)
                mm.then_inc(wo_mm, 1)

            pe.wait_ge(L["pkA"], 16)
            pe.wait_ge(L["ctxT"], 16)
            in_proj(0)
            in_proj(1)
            pe.wait_ge(L["pkC"], 16)
            pe.wait_ge(L["xT"], 16)
            importance(0)
            importance(1)
            pe.wait_ge(L["wq"], 16)
            queries(0)
            pe.wait_ge(imp_ok, 2)
            for t in range(NT):
                mm = pe.transpose(psA[:, 1, t:t + 1], imp[0:1, t * P:(t + 1) * P], ident[0:1, 0:1])
            mm.then_inc(impc_mm, 1)
            queries(1)
            queries(2)
            x_proj(0)
            x_proj(1)
            pe.wait_ge(L["dtpT"], 16)
            pe.wait_ge(dtl_ok, 2)
            delta_proj(0)
            pe.wait_ge(rest_ok, 2)
            delta_proj(1)
            pe.wait_ge(bc_ok, 2)
            pe.wait_ge(L["sel"], 16)
            bcast_b(0, 0)
            queries(3)
            bcast_b(0, 1)
            bcast_b(1, 0)
            bcast_b(1, 1)
            pe.wait_ge(onehot_ok, 1)
            pe.wait_ge(prep_ok, 1)
            pe.wait_ge(L["x"], 16)
            pe.wait_ge(qt_ok, 4)
            for k in range(HC):
                if k == 1:
                    pe.wait_ge(delta_ok, 1)
                    bcast_c(0)
                for b in range(B):
                    for q in range(2):
                        t = 2 * b + q
                        pe.matmul(psA[:, 1, (k * B + b) * SLOTS:(k * B + b + 1) * SLOTS], s_x[:, t, k * P:(k + 1) * P],
                                  onehot[:, t, :], start=q == 0, stop=q == 1)
            for b in range(B):
                for q in range(2):
                    mm = pe.matmul(psA[0:1, 0, b * SLOTS:(b + 1) * SLOTS], onescol[:, :], onehot[:, 2 * b + q, :],
                                   start=q == 0, stop=q == 1)
            mm.then_inc(xsel_mm, 1)
            bcast_b(2, 0)
            pe.wait_ge(xs_ok, 2)
            pe.wait_ge(L["wk"], 16)
            pe.wait_ge(L["rows"], 16)
            for m in range(HC):
                dst = psA[:, 2, m * B * SLOTS:(m + 1) * B * SLOTS]
                for k in range(HC):
                    pe.matmul(dst, s_wk[:, k, m * P:(m + 1) * P], xs[:, k, :, 0, :], start=k == 0, stop=False)
                mm = pe.matmul(dst, s_rows[0:1, 0, m * P:(m + 1) * P], occ[:, :, 0, :], start=False, stop=True)
            mm.then_inc(kt_mm, 1)
            bcast_c(1)
            bcast_b(2, 1)
            pe.wait_ge(delta_ok, 2)
            pe.wait_ge(diag_ok, 1)
            skip_sum(0, 0)
            skip_sum(0, 1)
            pe.wait_ge(L["wv"], 16)

            def values(b):
                dst = psA[0:SC, b // 2, (b % 2) * H:(b % 2 + 1) * H]
                for k in range(HC):
                    pe.matmul(dst, xs[:, k, b, :, :], s_wv[:, k, :], start=k == 0, stop=False)
                pe.matmul(dst, occ[:, b, :, :], s_rows[0:1, 1, :], start=False, stop=True).then_inc(v_mm, 1)

            values(0)

            def y_turns(hb):
                pe.wait_ge(yg_ok, 2 * (hb + 1))
                if hb == 0:
                    pe.wait_ge(pT_ok, NT)
                else:
                    pe.wait_ge(ysum_ok, 4)
                for t in range(hb * HT, (hb + 1) * HT):
                    b, q = t // 2, t % 2
                    for e in range(2):
                        mm = pe.transpose(turned(t)[:, e * P:(e + 1) * P],
                                          yg[:, e, (b % 2) * S + q * P:(b % 2) * S + (q + 1) * P], ident)
                    mm.then_inc(yT_mm, 1)

            def x2_turn(t):
                pe.wait_ge(x2_ok, t + 1)
                pe.wait_ge(y2_ok, pair_end(t))
                for m in range(HC):
                    mm = pe.transpose(turned(t)[:, m * P:(m + 1) * P], x2[:, t, m * P:(m + 1) * P], ident)
                mm.then_inc(x2T_mm, 1)

            def router(hb):
                if hb == 0:
                    pe.wait_ge(hi_ok, 1)
                    pe.wait_ge(lo_ok, 1)
                    pe.wait_ge(y1_ok, NT)
                else:
                    pe.wait_ge(prod_ok, 2 * ITER)
                pe.wait_ge(x2l_ok, HT * (hb + 1))
                i = 0
                for m in range(HC):
                    for xx in (x2h[hb], x2l[hb]):
                        for ww in (rw_hi, rw_lo):
                            i += 1
                            mm = pe.matmul(router_bank(hb)[0:E, :], ww[:, m, :], xx[:, :, m, :], start=i == 1, stop=i == 4 * HC)
                mm.then_inc(rt_mm, 1)

            def router_turn(hb):
                pe.wait_ge(lgT_ok, hb + 1)
                for t in range(HT):
                    mm = pe.transpose(router_bank(hb)[:, t * E:(t + 1) * E], lgT[:, t * P:(t + 1) * P], ident[0:E, 0:E])
                mm.then_inc(lgt_mm, 1)

            def expert_pair(i):
                t, q = i // (E // 2), i % (E // 2)
                if i == 0:
                    pe.wait_ge(ebl_ok, 1)
                    pe.wait_ge(x2l_ok, HT)
                elif 2 <= i < UNITS:
                    pe.wait_ge(ge_ok, i - 1)
                elif UNITS <= i < UNITS + 4:
                    pe.wait_ge(ge_ok, UNITS)
                    pe.wait_ge(prod_ok, 2 * ITER)
                    if i == UNITS + 3:
                        pe.wait_ge(lg_ok, 2)
                elif i >= UNITS + 4:
                    pe.wait_ge(ge_ok, i - 3)
                cols = slice(q * 512, (q + 1) * 512)
                dst = expert_bank(i)
                pe.matmul(dst, ones2r[:, :], eb_st[:, cols], start=True, stop=False)
                for m in range(HC):
                    pe.matmul(dst, x2h[t // HT][:, t % HT, m, :], ew_hi[:, m, cols], start=False, stop=False)
                    pe.matmul(dst, x2h[t // HT][:, t % HT, m, :], ew_lo[:, m, cols], start=False, stop=False)
                    mm = pe.matmul(dst, x2l[t // HT][:, t % HT, m, :], ew_hi[:, m, cols], start=False, stop=m == HC - 1)
                mm.then_inc(ex_mm, 1)

            def mixed_turn(t):
                pe.wait_ge(mix_ok, (E // 2) * (t + 1))
                if t == 0:
                    pe.wait_ge(lg_ok, 1)
                if t >= 1:
                    pe.wait_ge(y3_ok, t)
                for m in range(HC):
                    mm = pe.transpose(psA[:, 2, m * P:(m + 1) * P], cmb[:, t % 2, m * P:(m + 1) * P], ident)
                mm.then_inc(cT_mm, 1)

            def mixed_proj(t):
                if t == 0:
                    pe.wait_ge(L["ow"], 16)
                pe.wait_ge(cT_ok, t + 1)
                if t >= 1:
                    pe.wait_ge(y3_ok, t)
                for m in range(HC):
                    mm = pe.matmul(psA[:, 2, H:2 * H], cT[:, m, :], s_ow[:, m, :], start=m == 0, stop=m == HC - 1)
                mm.then_inc(ow_mm, 1)

            for k in range(ITER):
                first, second = k - LAG, k - LAG - 1
                if first >= 2 and first < NT:
                    scores(first)
                if 1 <= k <= DIRECT and not 2 <= first <= NT:
                    state_sum(k - 1, 0)
                if first == 0:
                    pe.wait_ge(bdk_ok, 1)
                    pe.wait_ge(vbd_ok, 1)
                    pe.wait_ge(ho_ok, 1)
                if first in (0, 1):
                    scores(first)
                if 1 <= k < ITER - 2:
                    bcast_b(k + 2, 0)
                if 0 <= second < NT:
                    mix_values(second)
                if 0 <= first < NT:
                    max_turn(first)
                if k == NPAIR + 1:
                    skip_sum(1, 0)
                    shift(first)
                if k == MOE0 - 2:
                    y_turns(0)
                if 2 <= first <= NT:
                    state_sum(k - 1, 0)
                if 2 <= first < NT and k != NPAIR + 1:
                    shift(first)
                if k >= 1 and k != NPAIR + 1:
                    state_sum(k - 1, 1)
                if k == 1:
                    values(1)
                if first in (0, 1):
                    shift(first)
                if k == DIRECT:
                    direct_sum(k)
                if k >= MOE0:
                    expert_pair(PER_ITER * (k - MOE0))
                if k > DIRECT:
                    direct_sum(k)
                if k == MOE0 - 1:
                    for t in range(HT):
                        x2_turn(t)
                if 1 <= k < ITER - 2:
                    bcast_b(k + 2, 1)
                if 0 <= second < NT:
                    out_turn(second)
                if 0 <= first < NT:
                    probs_turn(first)
                if k == NPAIR + 1:
                    state_sum(k - 1, 1)
                if second == 0:
                    pe.wait_ge(L["wo"], 16)
                if 0 <= second < NT:
                    out_proj(second)
                if k == MOE0 + 3:
                    mixed_turn(0)
                if k == ITER - 1:
                    state_sum(k, 1)
                if MOE0 <= k < ITER - 1:
                    bcast_c(k + 1)
                if k >= MOE0:
                    expert_pair(PER_ITER * (k - MOE0) + 1)
                if k == 1:
                    values(2)
                if 1 <= k < MOE0:
                    bcast_c(k + 1)
                if k == 1:
                    values(3)
                if k == MOE0 + 3:
                    mixed_proj(0)
                if k == MOE0 - 1:
                    router(0)
                    router_turn(0)
            expert_pair(LOOPED)
            y_turns(1)
            expert_pair(LOOPED + 1)
            mixed_turn(1)
            expert_pair(LOOPED + 2)
            mixed_proj(1)
            expert_pair(LOOPED + 3)
            for t in range(HT, NT):
                x2_turn(t)
            expert_pair(LOOPED + 4)
            expert_pair(LOOPED + 5)
            router(1)
            expert_pair(LOOPED + 6)
            router_turn(1)
            expert_pair(LOOPED + 7)
            for i in range(UNITS, 2 * UNITS):
                expert_pair(i)
                if i in TURN_AFTER:
                    mixed_turn(TURN_AFTER[i])
                if i in PROJ_AFTER:
                    mixed_proj(PROJ_AFTER[i])
            mixed_turn(NT - 1)
            mixed_proj(NT - 1)

        @block.scalar
        def _(act):
            for dst, src, n in ((c[:], pkC, "pkC"), (s_wq[:], wq, "wq"), (s_rows, rows, "rows"), (s_ho, headones, "ho"),
                                (s_bo[:], bo, "bo"), (s_rw[:], rw, "rw"), (s_rb[:], rb, "rb"), (s_ob[:], ob, "ob")):
                act.dma_start(dst, src).then_inc(L[n], 16)

            def exps(k, e):
                hb, p = k // NPAIR, k % NPAIR
                act.wait_ge(aneg_ok, 1)
                if k >= 1:
                    act.wait_ge(scan_ok, 2 * (k - 1) + e + 1)
                for j in range(2):
                    o = dA[:, e, j, :, 1:]
                    i = delta[:, e, hb * 512:(hb + 1) * 512].rearrange("p (b l) -> p b l", b=2)[:, :, 1:]
                    x_ = act.activation(o, i, ACT.Exp, scale=aneg[:, e * NS + 2 * p + j:e * NS + 2 * p + j + 1])
                x_.then_inc(dA_ok, 1)

            def copy_b(k, j):
                act.wait_ge(b_mm, 2 * k + j + 1)
                if k >= 2:
                    act.wait_ge(dBu_ok, 2 * (k - 1))
                act.copy(Bb[:, k % 2, j * 512:(j + 1) * 512], psB[:, :]).then_inc(bb_ok, 1)

            def weight_high(q):
                act.wait_ge(ew_ld[q], 16)
                act.copy(ew_hi[:, q // 2, (q % 2) * TOK:(q % 2 + 1) * TOK], ew_in[q]).then_inc(ewh_ok, 1)

            def bias_high():
                act.wait_ge(L["eb"], 16)
                act.copy(eb_st[:, :], s_eb).then_inc(ebh_ok, 1)

            def router_high():
                act.wait_ge(L["rw"], 16)
                act.copy(rw_hi[:, :, :], s_rw[:, :, :])
                act.copy(ones2r[:, :], ones2[:, :]).then_inc(hi_ok, 1)

            act.wait_ge(prep_ok, 1)
            act.wait_ge(L["pkA"], 16)
            act.activation(aexp[:, :], a[:, A_AL:A_AL + 2 * NS], ACT.Exp).then_inc(aexp_ok, 1)
            act.wait_ge(L["pkC"], 16)
            for n in range(2):
                act.wait_ge(imp_mm, n + 1)
                act.activation(imp[:, n * 512:(n + 1) * 512], psB[:, :] if n == 0 else psA[:, 0, :], ACT.Identity,
                               bias=c[:, C_BI:C_BI + 1]).then_inc(imp_ok, 1)

            def copy_q(i):
                m, n = i // 2, i % 2
                act.wait_ge(qt_mm, i + 1)
                act.activation(QT[:, m, n * 512:(n + 1) * 512], psA[:, 2 if n == 0 else 0, :], ACT.Identity,
                               bias=c[:, C_BQ + m:C_BQ + m + 1]).then_inc(qt_ok, 1)

            copy_q(0)
            for e in range(2):
                act.wait_ge(xc_ok, e + 1)
                act.activation(th[:, e, :], xc[:, e, :], ACT.Tanh).then_inc(th_ok, 1)
                copy_q(1 + e)
            weight_high(0)
            for n in range(2):
                act.wait_ge(xdbl_mm, n + 1)
                cols = slice(n * 512, (n + 1) * 512)
                act.copy(dtl[32:32 + DR, cols], psS[32:32 + DR, n, :]).then_inc(dtl_ok, 1)
                act.copy(stack[:, cols], psS[:, n, :]).then_inc(part1_ok, 1)
            weight_high(1)
            for n in range(2):
                act.wait_ge(rest_ok, n + 1)
                cols = slice(n * 512, (n + 1) * 512)
                act.copy(stack[64:128, cols], r1[64:128, cols]).then_inc(part2_ok, 1)
            weight_high(2)
            for e in range(2):
                act.wait_ge(spm_ok, e + 1)
                act.activation(spe[:, e, :], spm[:, e, :], ACT.Exp).then_inc(spe_ok, 1)
                if e == 0:
                    weight_high(3)
            bias_high()
            for e in range(2):
                act.wait_ge(spe_ok, e + 1)
                act.activation(spm[:, e, :], spe[:, e, :], ACT.Ln, bias=onescol[:, 0:1]).then_inc(spl_ok, 1)
            copy_b(0, 0)
            copy_q(3)
            copy_b(0, 1)
            copy_b(1, 0)
            act.wait_ge(L["ho"], 16)
            act.wait_ge(dt_mm, 2)
            act.copy(ho_r[:, :, :], s_ho[:, :, :]).then_inc(ho_ok, 1)
            router_high()
            act.wait_ge(delta_ok, 1)
            exps(0, 0)
            act.wait_ge(delta_ok, 2)
            exps(0, 1)
            copy_b(1, 1)
            act.wait_ge(xsel_mm, 1)
            act.wait_ge(spl_ok, 2)
            sel_in = psA[:, 1, 0:HC * B * SLOTS].rearrange("p (k b s) -> p k b s", k=HC, s=SLOTS)
            for d in range(2):
                act.copy(xs[:, :, :, d, :], sel_in)
                act.copy(occ[:, :, d, :], psA[0:1, 0, 0:B * SLOTS].rearrange("p (b s) -> p b s", s=SLOTS)).then_inc(xs_ok, 1)

            def block_keys():
                act.wait_ge(kt_mm, 1)
                for h in range(HPC):
                    i = act.activation(bdK[:, :, h, :], psA[:, 2, 0:HC * B * SLOTS].rearrange("p (g s) -> p g s", s=SLOTS),
                                       ACT.Copy, scale=c[:, C_M8 + h:C_M8 + h + 1])
                i.then_inc(bdk_ok, 1)

            def norm1(t):
                act.wait_ge(nm_ok, t + 1)
                act.activation(x1[:, t, :], x1[:, t, :], ACT.Identity, scale=rs1[:, t:t + 1], bias=nm1[:, t:t + 1]
                               ).then_inc(x1_ok, 1)

            def copy_sums(hb):
                for e in range(2):
                    act.wait_ge(sum_mm, 2 * (NPAIR * (hb + 1) - 1) + e + 1)
                    if hb == 1:
                        act.wait_ge(yg_ok, e + 1)
                    act.copy(ysum[:, e, :], yps[e]).then_inc(ysum_ok, 1)

            def gate_tanh(t):
                act.wait_ge(x1_ok, t + 1)
                act.activation(zt[:, t, :], x1[:, t, :], ACT.Tanh, scale=0.5).then_inc(zt_ok, 1)

            def x2_high(t):
                act.wait_ge(x2T_mm, pair_end(t))
                act.copy(x2h[t // HT][:, t % HT, :, :].rearrange("p m t -> p (m t)"), turned(t)).then_inc(x2h_ok, 1)

            def copy_logits(hb):
                if hb == 0:
                    act.wait_ge(L["rb"], 16)
                else:
                    act.wait_ge(lgt_mm, 1)
                act.wait_ge(rt_mm, hb + 1)
                act.activation(lgT, router_bank(hb)[0:E, :], ACT.Identity, bias=s_rb[:, 0:1]).then_inc(lgT_ok, 1)

            def gate_exp(hb):
                act.wait_ge(ls_ok, hb + 1)
                act.activation(le[:, :, :], ls[:, :, :], ACT.Exp).then_inc(le_ok, 1)

            def gelu(i):
                act.wait_ge(ex_mm, i + 1)
                if i >= 4:
                    act.wait_ge(mix_ok, i - 3)
                act.activation(ge[:, i % 4, :], expert_bank(i), ACT.Gelu_apprx_tanh).then_inc(ge_ok, 1)

            def copy_mixed(t):
                act.wait_ge(cT_mm, t + 1)
                if t >= 1:
                    act.wait_ge(ow_mm, t)
                act.copy(cT[:, :, :].rearrange("p m t -> p (m t)"), psA[:, 2, 0:H]).then_inc(cT_ok, 1)

            for k in range(ITER):
                first, second = k - LAG, k - LAG - 1
                if k + 1 < ITER:
                    exps(k + 1, 0)
                if 1 <= k < ITER - 2:
                    copy_b(k + 2, 0)
                if k + 1 < ITER:
                    exps(k + 1, 1)
                if k == 0:
                    copy_b(2, 0)
                if k == 1:
                    block_keys()
                if 0 <= first < NT:
                    act.wait_ge(mT_mm, first + 1)
                    if first >= 1:
                        act.wait_ge(shift_mm, first)
                    act.mul(mTn[:, :], psA[0:NH, 2, 0:P], -1.0).then_inc(mTn_ok, 1)
                if k == MOE0:
                    gate_exp(0)
                if k == MOE0 - 1:
                    for t in range(HT):
                        x2_high(t)
                if 0 <= first < NT:
                    act.wait_ge(shift_mm, first + 1)
                    if first >= 1:
                        act.wait_ge(pT_mm, first)
                    act.activation(Pm[:, :, :].rearrange("p (m j) s -> p m (j s)", m=HC), psA[:, 0:2, 0:HPC * SLOTS],
                                   ACT.Exp, scale=float(HD) ** -0.5).then_inc(probs_ok, 1)
                if k == NPAIR:
                    copy_sums(0)
                if k + 2 < ITER:
                    copy_b(k + 2, 1)
                if 0 <= second < NT:
                    act.wait_ge(oT_mm, second + 1)
                    if second >= 1:
                        act.wait_ge(wo_mm, second)
                    act.copy(OT[:, :, :].rearrange("p m t -> p (m t)"), psA[:, 2, 0:256]).then_inc(oT_ok, 1)
                if 0 <= first < NT:
                    act.wait_ge(pT_mm, first + 1)
                    if first >= 1:
                        act.wait_ge(av_mm, first)
                    act.copy(PT[:, :, :].rearrange("p (m j) s -> p m (j s)", m=2), psA[0:SC, 0:2, :]).then_inc(pT_ok, 1)
                if 0 <= k - LAG - 2 < NT:
                    norm1(k - LAG - 2)
                    gate_tanh(k - LAG - 2)
                if k == MOE0 - 1:
                    copy_logits(0)
                if k == MOE0:
                    act.wait_ge(qt_mm, 4)
                if k >= MOE0:
                    for j in range(PER_ITER):
                        gelu(PER_ITER * (k - MOE0) + j)
                        if k == MOE0 + 3 and j == 0:
                            copy_mixed(0)
                        if k == ITER - 1 and j == 0:
                            copy_sums(1)
            gelu(LOOPED)
            gelu(LOOPED + 1)
            copy_mixed(1)
            gelu(LOOPED + 2)
            gelu(LOOPED + 3)
            for t in range(HT, NT):
                x2_high(t)
            gelu(LOOPED + 4)
            gelu(LOOPED + 5)
            copy_logits(1)
            gelu(LOOPED + 6)
            gelu(LOOPED + 7)
            gate_exp(1)
            for i in range(UNITS, 2 * UNITS):
                gelu(i)
                if i in TURN_AFTER:
                    copy_mixed(TURN_AFTER[i])
            copy_mixed(NT - 1)

        @block.vector
        def _(dve):
            steps = [0]

            def link(ins):
                steps[0] += 1
                ins.then_inc(dve_step, 1)
                dve.wait_ge(dve_step, steps[0])

            def conv(e):
                dve.wait_ge(inproj_mm, e + 1)
                o = xc[:, e, :].rearrange("p (b l) -> p b l", b=B)
                link(dve.tensor_scalar(o, X4[e], cwh[:, e * TAPS + 3:e * TAPS + 4], cwh[:, 2 * TAPS + e:2 * TAPS + e + 1],
                                       ALU.mult, ALU.add))
                for d in range(1, TAPS):
                    i = dve.scalar_tensor_tensor(o[:, :, d:], X4[e][:, :, :S - d],
                                                 cwh[:, e * TAPS + 3 - d:e * TAPS + 4 - d], o[:, :, d:], ALU.mult, ALU.add)
                    if d < TAPS - 1:
                        link(i)
                i.then_inc(xc_ok, 1)

            def silu(e):
                dve.wait_ge(th_ok, e + 1)
                dve.scalar_tensor_tensor(u[:, e, :], th[:, e, :], 1.0, xc[:, e, :], ALU.add, ALU.mult).then_inc(u_ok, 1)

            def count(t):
                row, col = imp[:, (t // 2) * S:(t // 2 + 1) * S], impc[:, t:t + 1]
                tri = c[:, C_TRI + (t % 2) * S:C_TRI + (t % 2 + 1) * S]
                for i, (op, tot) in enumerate(((ALU.is_ge, cge), (ALU.is_gt, gtc), (ALU.is_equal, eqc))):
                    n = 3 * t + i
                    if n >= UNUSED:
                        dve.wait_ge(count_ok, n - UNUSED + 1)
                    o = unused[:, (n % UNUSED) * S:(n % UNUSED + 1) * S]
                    if op != ALU.is_equal:
                        dve.tensor_scalar(o, row, col, None, op, ALU.add, accum_out=tot[:, t:t + 1]).then_inc(count_ok, 1)
                    else:
                        dve.scalar_tensor_tensor(o, row, col, tri, op, ALU.mult, accum_out=tot[:, t:t + 1]
                                                 ).then_inc(count_ok, 1)

            def delta_in(e):
                return psS[:, 2 if e == 0 else 0:4 if e == 0 else 2, :].rearrange("p n l -> p (n l)")

            dve.wait_ge(L["pkA"], 16)
            link(dve.tensor_scalar(cwh[:, :], a[:, A_CW:A_CB + 2], 0.5, None, ALU.mult))
            conv(0)
            conv(1)
            silu(0)
            silu(1)
            dve.wait_ge(L["pkC"], 16)
            dve.wait_ge(impc_mm, 1)
            dve.wait_ge(imp_ok, 2)
            link(dve.tensor_copy(impc[:, :], psA[:, 1, 0:NT]))
            count(0)
            count(1)
            for n in range(2):
                dve.wait_ge(part1_ok, n + 1)
                cols = slice(n * 512, (n + 1) * 512)
                dve.tensor_tensor(r1[64:128, cols], psS[64:128, n, :], stack[64:128, cols], ALU.subtract).then_inc(rest_ok, 1)

            def clamped(e):
                dve.wait_ge(dt_mm, e + 1)
                dve.tensor_scalar(spm[:, e, :], delta_in(e), a[:, A_DTB + e:A_DTB + e + 1], 40.0, ALU.add,
                                  ALU.min).then_inc(spm_ok, 1)

            clamped(0)
            for n in range(2):
                dve.wait_ge(part2_ok, n + 1)
                cols = slice(n * 512, (n + 1) * 512)
                dve.tensor_tensor(stack[96:128, cols], r1[96:128, cols], stack[96:128, cols], ALU.subtract).then_inc(bc_ok, 1)
            clamped(1)
            for t in range(2, NT):
                count(t)
            dve.wait_ge(count_ok, 3 * NT)
            dve.wait_ge(aexp_ok, 1)
            dve.tensor_scalar(aneg[:, :], aexp[:, :], -1.0, None, ALU.mult).then_inc(aneg_ok, 1)
            for e in range(2):
                i = dve.tensor_scalar(diagD[:, e, :], ident, a[:, A_D + e:A_D + e + 1], None, ALU.mult)
            i.then_inc(diag_ok, 1)
            link(dve.tensor_tensor(rank[:, :], gtc[:, :], eqc[:, :], ALU.add))
            link(dve.tensor_scalar(kept[:, :], cge[:, :], float(TIDX), None, ALU.is_le))
            link(dve.tensor_scalar(kep2[:, :], rank[:, :], float(MINTOK), None, ALU.is_lt))
            link(dve.tensor_tensor(kept[:, :], kept[:, :], kep2[:, :], ALU.max))
            link(dve.tensor_scalar(kept[:, :], kept[:, :], -1000.0, 1000.0, ALU.mult, ALU.add))
            link(dve.tensor_tensor(rk[:, :], rank[:, :], kept[:, :], ALU.add))
            dve.tensor_tensor(onehot[:, :, :], c[:, C_IOTA:C_IOTA + SLOTS].unsqueeze(1).to_broadcast([P, NT, SLOTS]),
                              rk[:, :].unsqueeze(2).to_broadcast([P, NT, SLOTS]), ALU.is_equal).then_inc(onehot_ok, 1)
            for e in range(2):
                dve.wait_ge(spl_ok, e + 1)
                dve.scalar_tensor_tensor(delta[:, e, :], delta_in(e), a[:, A_DTB + e:A_DTB + e + 1], spm[:, e, :],
                                         ALU.add, ALU.max).then_inc(delta_ok, 1)
                dve.wait_ge(delta_ok, e + 1)
                dve.wait_ge(ebl_ok, 1)
                dve.tensor_tensor(du[:, e, :], delta[:, e, :], u[:, e, :], ALU.mult).then_inc(du_ok, 1)

            def block_values():
                dve.wait_ge(v_mm, B)
                for g in range(2):
                    dve.tensor_tensor(Vbd[:, g * 2 * PAIRS:(g + 1) * 2 * PAIRS, :, 0:HD],
                                      psA[0:SC, g, :].rearrange("p (g h d) -> p g h d", h=2, d=HD),
                                      c[0:SC, C_VM:C_VM + 2].unsqueeze(1).unsqueeze(3).to_broadcast([SC, 2 * PAIRS, 2, HD]),
                                      ALU.mult)
                dve.tensor_copy(Vbd[:, :, :, HD:HD + 1],
                                c[0:SC, C_VD:C_VD + 2].unsqueeze(1).unsqueeze(3).to_broadcast([SC, B * PAIRS, 2, 1])
                                ).then_inc(vbd_ok, 1)

            def scan(k, e):
                dve.wait_ge(dA_ok, 2 * k + e + 1)
                dve.wait_ge(dBu_ok, 2 * k + e + 1)
                if k >= 1 and (e == 1 or k <= DIRECT):
                    dve.wait_ge(psm_ok[e], k)
                if k > DIRECT and e == 0:
                    dve.wait_ge(sum_mm, 2 * k - 1)
                dve.tensor_tensor_scan(hs[:, e, :], dA[:, e, :, :, :].rearrange("p j b l -> p (j b l)"), dBu[:, e, :],
                                       0.0, ALU.mult, ALU.add).then_inc(scan_ok, 1)

            def times_c(k, e):
                dve.wait_ge(c_mm, k + 1)
                dve.wait_ge(scan_ok, 2 * k + e + 1)
                dve.tensor_tensor(hs[:, e, :], hs[:, e, :], cps.rearrange("p n l -> p (n l)"), ALU.mult).then_inc(prod_ok, 1)

            def add_pair(k):
                dve.wait_ge(prod_ok, 2 * k + 1)
                if k >= 1:
                    dve.wait_ge(sum_mm, 2 * (k - 1) + 1)
                dve.tensor_tensor(psm[:, 0, :], hs[:, 0, 0:512], hs[:, 0, 512:1024], ALU.add).then_inc(psm_ok[0], 1)

            def score_max(un):
                dve.wait_ge(score_mm, un + 1)
                if un >= 1:
                    dve.wait_ge(mT_mm, un)
                dve.tensor_reduce(mx[:, :].rearrange("p (m h) -> p m h", m=HC),
                                  psA[:, 0:2, 0:HPC * SLOTS].rearrange("p m (h s) -> p m h s", s=SLOTS), AX.X, ALU.max
                                  ).then_inc(max_ok, 1)

            def normalise(un):
                dve.wait_ge(av_mm, un + 1)
                if un >= 1:
                    dve.wait_ge(oT_mm, un)
                if un + 1 < NT:
                    dve.wait_ge(mTn_ok, un + 2)
                o = psA[:, 2, P:P + NH * (HD + 1)].rearrange("p (h d) -> p h d", d=HD + 1)
                link(dve.reciprocal(rden[:, :].unsqueeze(2), o[:, :, HD:HD + 1]))
                dve.tensor_tensor(On[:, :].rearrange("p (h d) -> p h d", d=HD), o[:, :, 0:HD],
                                  rden[:, :].unsqueeze(2).to_broadcast([P, NH, HD]), ALU.mult).then_inc(on_ok, 1)

            def moments(y, mv, done):
                link(dve.bn_stats(st[:, :], y))
                dve.bn_aggr(mv, st[:, :]).then_inc(done, 1)

            def residual1(t):
                dve.wait_ge(wo_mm, t + 1)
                dve.wait_ge(xb_ok, t + 1)
                dve.tensor_tensor(x1[:, t, :], psA[:, 2, 256:512], xb[:, t, :], ALU.add).then_inc(y1_ok, 1)

            def stats1(t):
                dve.wait_ge(y1_ok, t + 1)
                dve.bn_stats(st[:, :], x1[:, t, :]).then_inc(stats_ok, 1)

            def moments1(t):
                dve.wait_ge(stats_ok, t + 1)
                dve.bn_aggr(mv1[:, t, :], st[:, :]).then_inc(mv1_ok, 1)

            def gate_z(t):
                dve.wait_ge(zt_ok, t + 1)
                dve.scalar_tensor_tensor(zt[:, t, :], zt[:, t, :], 1.0, x1[:, t, :], ALU.add, ALU.mult).then_inc(z_ok, 1)

            def gated(hb, e):
                dve.wait_ge(ysum_ok, 2 * hb + e + 1)
                dve.wait_ge(z_ok, 4 * (hb + 1))
                if hb == 1:
                    dve.wait_ge(yT_mm, HT)
                dve.scalar_tensor_tensor(yg[:, e, :].rearrange("p (b l) -> p b l", b=2),
                                         ysum[:, e, :].rearrange("p (b l) -> p b l", b=2), 0.5,
                                         zt[:, :, :].rearrange("p (b e) l -> p b e l", e=2)[:, 2 * hb:2 * hb + 2, e, :],
                                         ALU.mult, ALU.mult).then_inc(yg_ok, 1)

            def residuals2(hb):
                tiles = range(hb * HT, (hb + 1) * HT)
                for t in tiles:
                    dve.wait_ge(yT_mm, pair_end(t))
                    dve.tensor_tensor(x2[:, t, :], turned(t), x1[:, t, :], ALU.add).then_inc(y2_ok, 1)
                for t in tiles:
                    dve.wait_ge(y2_ok, t + 1)
                    dve.bn_stats(st2[:, t % HT, :], x2[:, t, :]).then_inc(stats2_ok, 1)
                for t in tiles:
                    dve.wait_ge(stats2_ok, t + 1)
                    dve.bn_aggr(mv2[:, t, :], st2[:, t % HT, :]).then_inc(mv2_ok, 1)

            def norm2(t):
                dve.wait_ge(rs2_ok, t + 1)
                dve.tensor_scalar(x2[:, t, :], x2[:, t, :], mv2[:, t, 0:1], rs2[:, t:t + 1], ALU.subtract,
                                  ALU.mult).then_inc(x2_ok, 1)

            def x2_low(t):
                dve.wait_ge(x2h_ok, pair_end(t))
                dve.tensor_tensor(x2l[t // HT][:, t % HT, :, :].rearrange("p m t -> p (m t)"), turned(t),
                                  x2h[t // HT][:, t % HT, :, :].rearrange("p m t -> p (m t)").bitcast(F32), ALU.subtract
                                  ).then_inc(x2l_ok, 1)

            def gate_ranks(hb):
                dve.wait_ge(lgt_mm, hb + 1)
                dve.tensor_copy(lg[:, :, :].rearrange("p t e -> p (t e)"), router_bank(hb)[:, 0:HT * E]).then_inc(lg_ok, 1)
                dve.wait_ge(lg_ok, hb + 1)
                over = lg[:, :, :].unsqueeze(2).to_broadcast([P, HT, E, E])
                own = lg[:, :, :].unsqueeze(3).to_broadcast([P, HT, E, E])
                tri8 = c[:, C_TR8:C_TR8 + E * E].rearrange("p (i j) -> p i j", i=E).unsqueeze(1).to_broadcast([P, HT, E, E])
                link(dve.tensor_reduce(lm[:, :], lg[:, :, :], AX.X, ALU.max))
                dve.tensor_tensor(ls[:, :, :], lg[:, :, :], lm[:, :].unsqueeze(2).to_broadcast([P, HT, E]),
                                  ALU.subtract).then_inc(ls_ok, 1)
                dve.tensor_tensor(cmp1, over, own, ALU.is_gt)
                link(dve.tensor_tensor(cmp2, over, own, ALU.is_equal))
                link(dve.tensor_tensor(cmp2, cmp2, tri8, ALU.mult))
                link(dve.tensor_tensor(cmp1, cmp1, cmp2, ALU.add))
                link(dve.tensor_reduce(rk8[:, :, :], cmp1, AX.X, ALU.add))
                dve.tensor_scalar(rk8[:, :, :], rk8[:, :, :], 2.0, None, ALU.is_lt).then_inc(top_ok, 1)

            def gate_weights(hb):
                dve.wait_ge(le_ok, hb + 1)
                dve.wait_ge(top_ok, hb + 1)
                link(dve.tensor_tensor(le[:, :, :], le[:, :, :], rk8[:, :, :], ALU.mult))
                link(dve.tensor_reduce(gs[:, :], le[:, :, :], AX.X, ALU.add))
                link(dve.reciprocal(gr[:, :], gs[:, :]))
                link(dve.tensor_tensor(gates[:, hb * HT:(hb + 1) * HT, :], le[:, :, :],
                                       gr[:, :].unsqueeze(2).to_broadcast([P, HT, E]), ALU.mult))

            def mix(i):
                t, q = i // (E // 2), i % (E // 2)
                o = cmb[:, t % 2, :]
                if q == 0 and t >= 2:
                    dve.wait_ge(cT_mm, t - 1)
                dve.wait_ge(ge_ok, i + 1)
                for h in range(2):
                    x_ = 2 * q + h
                    g, src = gates[:, t, x_:x_ + 1], ge[:, i % 4, h * H:(h + 1) * H]
                    if x_ == 0:
                        link(dve.tensor_scalar(o, src, g, None, ALU.mult))
                    else:
                        ins = dve.scalar_tensor_tensor(o, src, g, o, ALU.mult, ALU.add)
                        if h == 0:
                            link(ins)
                ins.then_inc(mix_ok, 1)
                dve.wait_ge(mix_ok, i + 1)

            def residual3(t):
                dve.wait_ge(ow_mm, t + 1)
                dve.wait_ge(x2b_ok, t // HT + 1)
                dve.tensor_tensor(y3[:, t % 2, :], psA[:, 2, H:2 * H], x2b[:, t, :], ALU.add).then_inc(y3_ok, 1)
                dve.wait_ge(y3_ok, t + 1)
                moments(y3[:, t % 2, :], mv3[:, t, :], mv3_ok)

            def norm3(t):
                dve.wait_ge(rs3_ok, t + 1)
                dve.tensor_scalar(fin[:, t, :], y3[:, t % 2, :], mv3[:, t, 0:1], rs3[:, t:t + 1], ALU.subtract,
                                  ALU.mult).then_inc(fin_ok, 1)

            for k in range(ITER):
                first, second = k - LAG, k - LAG - 1
                scan(k, 0)
                if 0 <= k - LAG - 2 < NT:
                    residual1(k - LAG - 2)
                scan(k, 1)
                if 0 <= k - LAG - 2 < NT:
                    stats1(k - LAG - 2)
                if first == 0:
                    block_values()
                if 2 <= first < NT:
                    score_max(first)
                if 0 <= k - LAG - 2 < NT:
                    moments1(k - LAG - 2)
                if k == MOE0 - 1:
                    for t in range(HT):
                        norm2(t)
                times_c(k, 0)
                if 0 <= k - LAG - 3 < NT:
                    gate_z(k - LAG - 3)
                if 1 <= second < NT:
                    normalise(second)
                times_c(k, 1)
                if first in (0, 1):
                    score_max(first)
                if k == MOE0:
                    gate_ranks(0)
                if k > MOE0:
                    for j in range(PER_ITER):
                        mix(PER_ITER * (k - MOE0 - 1) + j)
                if k < DIRECT:
                    add_pair(k)
                if second == 0:
                    normalise(0)
                if k == NPAIR:
                    gated(0, 0)
                    gated(0, 1)
                if k == MOE0 - 2:
                    residuals2(0)
                if k == MOE0 - 1:
                    for t in range(HT):
                        x2_low(t)
                if k == MOE0:
                    gate_weights(0)
            mix(LOOPED - 2)
            gated(1, 0)
            gated(1, 1)
            mix(LOOPED - 1)
            residual3(0)
            residuals2(1)
            mix(LOOPED)
            mix(LOOPED + 1)
            for t in range(HT, NT):
                norm2(t)
            norm3(0)
            mix(LOOPED + 2)
            for t in range(HT, NT):
                x2_low(t)
            residual3(1)
            mix(LOOPED + 3)
            mix(LOOPED + 4)
            norm3(1)
            mix(LOOPED + 5)
            gate_ranks(1)
            mix(LOOPED + 6)
            mix(LOOPED + 7)
            gate_weights(1)
            for i in range(UNITS, 2 * UNITS):
                mix(i)
                if i in RESIDUAL_AFTER:
                    residual3(RESIDUAL_AFTER[i])
                if i in NORM_AFTER:
                    norm3(NORM_AFTER[i])
            residual3(NT - 1)
            norm3(NT - 1)

        @block.gpsimd
        def _(pool):
            steps = [0]

            def link(ins):
                steps[0] += 1
                ins.then_inc(pool_step, 1)
                pool.wait_ge(pool_step, steps[0])

            def rstd(mv, ve, rs, t, done, ready, n=1):
                pool.wait_ge(ready, t + n)
                link(pool.tensor_scalar(ve[:, t:t + n], mv[:, t:t + n, 1], EPS, 1.0, ALU.add, ALU.mult))
                pool.tensor_tensor(rs[:, t:t + n], ve[:, t:t + n], mhalf[:, t:t + n], ALU.pow).then_inc(done, n)

            def add_bias(hb):
                pool.wait_ge(x2_ok, HT * (hb + 1))
                pool.wait_ge(L["ob"], 16)
                pool.tensor_tensor(x2b[:, hb * HT:(hb + 1) * HT, :], x2[:, hb * HT:(hb + 1) * HT, :],
                                   s_ob[:, :].unsqueeze(1).to_broadcast([P, HT, H]), ALU.add).then_inc(x2b_ok, 1)

            def add_pair(k):
                pool.wait_ge(prod_ok, 2 * k + 2)
                if k >= 1:
                    pool.wait_ge(sum_mm, 2 * k)
                pool.tensor_tensor(psm[:, 1, :], hs[:, 1, 0:512], hs[:, 1, 512:1024], ALU.add).then_inc(psm_ok[1], 1)

            for e in range(2):
                pool.memset(dA[:, e, :, :, 0:1], 0.0)
            pool.memset(mhalf[:, :], -0.5)
            pool.memset(onescol[:, :], 1.0).then_inc(prep_ok, 1)
            pool.wait_ge(prep_ok, 1)
            for q in range(4):
                pool.wait_ge(ewh_ok, q + 1)
                part = slice((q % 2) * TOK, (q % 2 + 1) * TOK)
                pool.tensor_tensor(ew_lo[:, q // 2, part], ew_in[q], ew_hi[:, q // 2, part].bitcast(F32),
                                   ALU.subtract).then_inc(ewl_ok, 1)
            pool.wait_ge(ebh_ok, 1)
            pool.wait_ge(ewl_ok, 4)
            pool.tensor_tensor(eb_st[32:33, :], s_eb[32:33, :], eb_st[32:33, :].bitcast(F32), ALU.subtract).then_inc(ebl_ok, 1)
            pool.wait_ge(ebl_ok, 1)
            pool.wait_ge(hi_ok, 1)
            pool.tensor_tensor(rw_lo[:, :, :], s_rw[:, :, :], rw_hi[:, :, :].bitcast(F32), ALU.subtract).then_inc(lo_ok, 1)
            pool.wait_ge(L["bo"], 16)
            for k in range(ITER):
                hb = k // NPAIR
                for e in range(2):
                    pool.wait_ge(du_ok, e + 1)
                    pool.wait_ge(bb_ok, 2 * k + 2)
                    if k >= 1:
                        pool.wait_ge(scan_ok, 2 * (k - 1) + e + 1)
                    pool.tensor_tensor(dBu[:, e, :].rearrange("p (j l) -> p j l", j=2),
                                       Bb[:, k % 2, :].rearrange("p (j l) -> p j l", j=2),
                                       du[:, e, hb * 512:(hb + 1) * 512].unsqueeze(1).to_broadcast([P, 2, 512]),
                                       ALU.mult).then_inc(dBu_ok, 1)
                    if e == 0 and 0 <= k - LAG - 3 < NT:
                        t = k - LAG - 3
                        rstd(mv1, ve1, rs1, t, rs1_ok, mv1_ok)
                        pool.wait_ge(rs1_ok, t + 1)
                        pool.tensor_scalar(nm1[:, t:t + 1], mv1[:, t, 0:1], rs1[:, t:t + 1], -1.0, ALU.mult, ALU.mult
                                           ).then_inc(nm_ok, 1)
                if k >= 1:
                    add_pair(k - 1)
                if 1 <= k <= NT:
                    pool.wait_ge(xsel_mm, 1)
                    pool.tensor_tensor(xb[:, k - 1, :], s_x[:, k - 1, :], s_bo[:, :], ALU.add).then_inc(xb_ok, 1)
                if k == MOE0 - 1:
                    rstd(mv2, ve2, rs2, 0, rs2_ok, mv2_ok, HT)
                if k == MOE0 + 1:
                    add_bias(0)
            add_pair(ITER - 1)
            rstd(mv3, ve3, rs3, 0, rs3_ok, mv3_ok)
            rstd(mv2, ve2, rs2, HT, rs2_ok, mv2_ok, HT)
            add_bias(1)
            for t in range(1, NT):
                rstd(mv3, ve3, rs3, t, rs3_ok, mv3_ok)


def constants():
    p = np.arange(P)
    j = np.arange(S)
    tri = np.concatenate([(j[None, :] < (q * P + p)[:, None]) for q in range(2)], 1).astype(np.float32)
    mask8 = (p[:, None] // HD == np.arange(HPC)[None, :]).astype(np.float32)
    iota = np.broadcast_to(np.arange(SLOTS, dtype=np.float32), (P, SLOTS))
    own = (p[:, None] // SLOTS == np.arange(2)[None, :]).astype(np.float32)
    weight = np.where(p % SLOTS == SLOTS - 1, S - SLOTS + 1, 1).astype(np.float32)
    i8 = np.arange(E)
    tri8 = np.broadcast_to((i8[None, :] < i8[:, None]).astype(np.float32).reshape(1, -1), (P, E * E))
    ones2 = np.zeros((P, P), np.float32)
    ones2[[BIAS, BIAS + 32]] = 1
    headones = np.zeros((NH, HC, HPC, SLOTS), np.float32)
    for h in range(NH):
        headones[h, h // HPC, h % HPC] = 1
    sel = np.zeros((P, 2 * NS, P), np.float32)
    for r in range(2 * NS):
        for first in (0, 64, 96):
            sel[first + r, r] = 1
    return np.eye(P, dtype=np.float32), mask8, iota, tri, own, own * weight[:, None], tri8, ones2, headones.reshape(NH, HC, -1), sel


def chunked(w):
    return np.ascontiguousarray(w.reshape(2, P, -1).transpose(1, 0, 2))


def kernel(**inputs):
    import concourse.bacc as bacc
    from concourse.bass_utils import run_bass_kernel_spmd
    import ml_dtypes

    g = {k: np.asarray(v) for k, v in inputs.items()}
    at, xa, ff = ({k[len(p):]: v for k, v in g.items() if k.startswith(p)} for p in ("L0_attn_", "L0_xattn_", "L0_ffn_"))
    ident, mask8, iota, tri, own, weight, tri8, ones2, headones, sel = constants()
    x = g["x"].reshape(TOK, H)

    def flat(v):
        return chunked(v).reshape(P, -1)

    rows_of = list(range(DR, DR + 2 * NS))
    xp = np.zeros((P, H), np.float32)
    xp[0:32] = xa["x_proj_w"][rows_of]
    xp[32:32 + DR] = xa["x_proj_w"][0:DR]
    xp[64:96] = xa["x_proj_w"][rows_of]
    xp[96:128] = xa["x_proj_w"][rows_of]
    pkA = np.concatenate([xa["in_proj_w"].T, flat(xa["conv_w"]), flat(xa["conv_b"]), flat(xp.T), flat(xa["dt_proj_b"]),
                          flat(xa["A_log"]), flat(xa["D"])], 1)
    pkC = np.concatenate([ident, np.repeat(chunked(at["Wi"]), P, 2).reshape(P, -1), flat(at["bq"]),
                          np.broadcast_to(at["bi"].reshape(1, 1), (P, 1)), mask8, iota, tri, own, weight, tri8, ones2], 1)
    eb = np.zeros((64, E * H), np.float32)
    eb[0] = eb[32] = ff["expert_b"].reshape(-1)
    arrays = dict(
        ctxT=g["ctx_1024"].reshape(TOK, DC).T, pkA=pkA, dtpT=xa["dt_proj_w"].T, pkC=pkC,
        xT=chunked(x.T), x=x.reshape(NT, P, H).transpose(1, 0, 2), wq=chunked(at["Wq"]), wk=chunked(at["Wk"]),
        wv=chunked(at["Wv"]), wo=chunked(at["Wo"]), rows=np.stack([at["bk"], at["bv"]])[None], headones=headones,
        sel=sel.astype(ml_dtypes.bfloat16), bo=np.broadcast_to(at["bo"], (P, H)), ob=np.broadcast_to(ff["out_b"], (P, H)),
        ew=ff["expert_w"].reshape(E, HC, P, H).transpose(2, 1, 0, 3).reshape(P, HC, E * H), rw=chunked(ff["router_w"]),
        ow=chunked(ff["out_w"]), eb=eb, rb=ff["router_b"].reshape(E, 1))
    nc = bacc.Bacc("TRN2", target_bir_lowering=False, num_devices=1, dynamic_dma_scratch_size=1024)
    feed, args = {}, []
    for name, v in arrays.items():
        v = np.ascontiguousarray(v)
        feed["in_" + name] = v
        args.append(nc.dram_tensor("in_" + name, v.shape, mybir.dt.from_np(v.dtype), kind="ExternalInput").ap())
    out = nc.dram_tensor("out", (B, S, H), F32, kind="ExternalOutput").ap()
    decoder_layer(nc, *args, out)
    r = run_bass_kernel_spmd(nc, [feed], core_ids=[0])
    return r.results[0]["out"]
```
